# Optimizing a Trainium2 kernel written in Bass

```python
import numpy as np
import jax
import jax.numpy as jnp

def _softmax(x, axis=-1):
    return jax.nn.softmax(x, axis=axis)

def _gelu(x):
    return jax.nn.gelu(x, approximate=True)

def _silu(x):
    return jax.nn.silu(x)

def _sigmoid(x):
    return jax.nn.sigmoid(x)

def _layernorm(x, axis=-1, eps=1e-05):
    m = jnp.mean(x, axis=axis, keepdims=True)
    v = jnp.var(x, axis=axis, keepdims=True)
    return (x - m) / jnp.sqrt(v + eps)

def _scatter_add(tgt, idx, src, axis=0):
    return tgt.at[idx].add(src)

def _segment_sum(src, seg, n):
    return jax.ops.segment_sum(src, seg, n)
kernel_name = 'mk_gnn_ffn_d2_gnn_r32_edb052'

def setup_inputs(seed: int=0):
    np.random.seed(seed)
    _w = jnp.asarray

    def _rec_inputs():
        import jax
        import jax.numpy as jnp
        _gk = jax.random.key(seed)
        x = -6.415e-05 + 1 * jax.random.normal(jax.random.fold_in(_gk, 1), (625, 512), jnp.float32)
        src = jax.random.randint(jax.random.fold_in(_gk, 2), (20000,), 0, 625, jnp.int32)
        dst = jnp.minimum((625 * jax.random.uniform(jax.random.fold_in(_gk, 3), (20000,)) ** 2.0).astype(jnp.int32), 19999)
        _o = jnp.argsort(dst, stable=True)
        src = src[_o]
        dst = dst[_o]
        edge_type_3 = jax.random.randint(jax.random.fold_in(_gk, 13), (20000,), 0, 3, jnp.int32)
        node_type_3 = jax.random.randint(jax.random.fold_in(_gk, 14), (625,), 0, 3, jnp.int32)
        return (x, src, dst, edge_type_3, node_type_3)
    x, src, dst, edge_type_3, node_type_3 = _rec_inputs()

    def _L0_gnn_setup():
        import jax, jax.numpy as jnp
        import numpy as np
        N_NODES = 625
        N_EDGES = 150000
        D_IN = 512
        D_OUT = 512
        N_REL = 3
        N_NT = 3
        key = jax.random.key(seed)
        ks = jax.random.split(key, 8)
        x = jax.random.normal(ks[0], (N_NODES, D_IN), dtype=jnp.float32)
        W_rel = jax.random.normal(ks[1], (N_REL, D_IN, D_OUT), dtype=jnp.float32) * 0.02
        b_rel = jnp.zeros((N_REL, D_OUT), dtype=jnp.float32)
        W_self = jax.random.normal(ks[2], (N_NT, D_IN, D_OUT), dtype=jnp.float32) * 0.02
        b_self = jnp.zeros((N_NT, D_OUT), dtype=jnp.float32)
        edge_src = jax.random.randint(ks[3], (N_EDGES,), 0, N_NODES, dtype=jnp.int32)
        edge_dst = jax.random.randint(ks[4], (N_EDGES,), 0, N_NODES, dtype=jnp.int32)
        edge_type = jax.random.randint(ks[5], (N_EDGES,), 0, N_REL, dtype=jnp.int32)
        node_type = jax.random.randint(ks[6], (N_NODES,), 0, N_NT, dtype=jnp.int32)
        return {'x': x, 'W_rel': W_rel, 'b_rel': b_rel, 'W_self': W_self, 'b_self': b_self, 'edge_src': edge_src, 'edge_dst': edge_dst, 'edge_type': edge_type, 'node_type': node_type}
    _L0_gnn_all = _L0_gnn_setup()
    _L0_gnn_in = {k: v for k, v in _L0_gnn_all.items() if k in ('W_rel', 'b_rel', 'W_self', 'b_self')}
    del _L0_gnn_all

    def _L0_ffn_setup():
        import jax, jax.numpy as jnp
        import numpy as np
        B, T, D, H = (2, 1024, 512, 64)
        G, E = (4, 8)
        GK, EK = (2, 2)
        EPS = 1e-05
        SCALE = 0.02

        def _layernorm(x, g, b):
            m = jnp.mean(x, axis=-1, keepdims=True)
            xc = x - m
            v = jnp.mean(xc * xc, axis=-1, keepdims=True)
            return xc * jax.lax.rsqrt(v + EPS) * g + b

        def _topk_gate(logits, k, n):
            v, i = jax.lax.top_k(logits, k)
            sc = jax.nn.softmax(v, axis=-1)
            return jnp.sum(jax.nn.one_hot(i, n, dtype=logits.dtype) * sc[..., None], axis=-2)
        key = jax.random.key(seed)
        ks = jax.random.split(key, 6)
        return {'inp': jax.random.normal(ks[0], (B, T, D), jnp.float32), 'ln_g': jnp.ones((D,), jnp.float32), 'ln_b': jnp.zeros((D,), jnp.float32), 'wg_group': jax.random.normal(ks[1], (D, G), jnp.float32) * SCALE, 'wg_inner': jax.random.normal(ks[2], (G, D, E), jnp.float32) * SCALE, 'W1': jax.random.normal(ks[3], (G, E, D, H), jnp.float32) * SCALE, 'b1': jnp.zeros((G, E, H), jnp.float32), 'W2': jax.random.normal(ks[4], (G, E, H, D), jnp.float32) * SCALE, 'b2': jnp.zeros((G, E, D), jnp.float32), 'gln_g': jnp.ones((G, D), jnp.float32), 'gln_b': jnp.zeros((G, D), jnp.float32)}
    _L0_ffn_all = _L0_ffn_setup()
    _L0_ffn_in = {k: v for k, v in _L0_ffn_all.items() if k in ('ln_g', 'ln_b', 'wg_group', 'wg_inner', 'W1', 'b1', 'W2', 'b2', 'gln_g', 'gln_b')}
    del _L0_ffn_all

    def _L1_gnn_setup():
        import jax, jax.numpy as jnp
        import numpy as np
        N, E, D = (50000, 12500, 512)

        def _sage_conv(x, src, dst, Wl, bl, Wr, n_nodes):
            agg = jax.ops.segment_sum(x[src], dst, num_segments=n_nodes)
            deg = jax.ops.segment_sum(jnp.ones((src.shape[0],), x.dtype), dst, num_segments=n_nodes)
            agg = agg / jnp.maximum(deg, 1.0)[:, None]
            return agg @ Wl.T + bl + x @ Wr.T

        def _layer_norm(h, w, b, eps=1e-05):
            mu = jnp.mean(h, axis=-1, keepdims=True)
            var = jnp.mean(jnp.square(h - mu), axis=-1, keepdims=True)
            return (h - mu) * jax.lax.rsqrt(var + eps) * w + b
        key = jax.random.key(seed)
        ks = jax.random.split(key, 8)
        s = 1.0 / np.sqrt(D)
        x = jax.random.normal(ks[0], (N, D), dtype=jnp.float32)
        edge_index = jax.random.randint(ks[1], (2, E), 0, N, dtype=jnp.int64)
        return {'x': x, 'edge_index': edge_index, 'W1l': jax.random.uniform(ks[2], (D, D), jnp.float32, -s, s), 'b1l': jnp.zeros((D,), jnp.float32), 'W1r': jax.random.uniform(ks[3], (D, D), jnp.float32, -s, s), 'W2l': jax.random.uniform(ks[4], (D, D), jnp.float32, -s, s), 'b2l': jnp.zeros((D,), jnp.float32), 'W2r': jax.random.uniform(ks[5], (D, D), jnp.float32, -s, s), 'ln1_w': jnp.ones((D,), jnp.float32), 'ln1_b': jnp.zeros((D,), jnp.float32), 'ln2_w': jnp.ones((D,), jnp.float32), 'ln2_b': jnp.zeros((D,), jnp.float32)}
    _L1_gnn_all = _L1_gnn_setup()
    _L1_gnn_in = {k: v for k, v in _L1_gnn_all.items() if k in ('W1l', 'b1l', 'W1r', 'W2l', 'b2l', 'W2r', 'ln1_w', 'ln1_b', 'ln2_w', 'ln2_b')}
    del _L1_gnn_all

    def _L1_ffn_setup():
        import jax, jax.numpy as jnp
        import numpy as np
        D = 512
        E = 8
        K = 2
        EXP = 4
        LN_EPS = 1e-05
        key = jax.random.key(seed)
        ks = jax.random.split(key, 8)
        B, T = (8, 64)
        Dh = D * EXP
        x = jax.random.normal(ks[0], (B, T, D), dtype=jnp.float32)
        ln_g = jnp.ones((D,), dtype=jnp.float32)
        ln_b = jnp.zeros((D,), dtype=jnp.float32)
        lim_r = np.sqrt(6.0 / (D + E)).astype(np.float32)
        w_r = jax.random.uniform(ks[1], (E, D), dtype=jnp.float32, minval=-lim_r, maxval=lim_r)
        b_r = jnp.zeros((E,), dtype=jnp.float32)
        lim1 = np.sqrt(6.0 / (D + Dh)).astype(np.float32)
        W1 = jax.random.uniform(ks[2], (E, D, Dh), dtype=jnp.float32, minval=-lim1, maxval=lim1)
        b1 = jnp.zeros((E, Dh), dtype=jnp.float32)
        W2 = jax.random.uniform(ks[3], (E, Dh, D), dtype=jnp.float32, minval=-lim1, maxval=lim1)
        b2 = jnp.zeros((E, D), dtype=jnp.float32)
        return {'x': x, 'ln_g': ln_g, 'ln_b': ln_b, 'w_r': w_r, 'b_r': b_r, 'W1': W1, 'b1': b1, 'W2': W2, 'b2': b2}
    _L1_ffn_all = _L1_ffn_setup()
    _L1_ffn_in = {k: v for k, v in _L1_ffn_all.items() if k in ('ln_g', 'ln_b', 'w_r', 'b_r', 'W1', 'b1', 'W2', 'b2')}
    del _L1_ffn_all
    return {'x': x, 'src': src, 'dst': dst, 'edge_type_3': edge_type_3, 'node_type_3': node_type_3, 'L0_gnn_W_rel': _L0_gnn_in['W_rel'], 'L0_gnn_b_rel': _L0_gnn_in['b_rel'], 'L0_gnn_W_self': _L0_gnn_in['W_self'], 'L0_gnn_b_self': _L0_gnn_in['b_self'], 'L0_ffn_ln_g': _L0_ffn_in['ln_g'], 'L0_ffn_ln_b': _L0_ffn_in['ln_b'], 'L0_ffn_wg_group': _L0_ffn_in['wg_group'], 'L0_ffn_wg_inner': _L0_ffn_in['wg_inner'], 'L0_ffn_W1': _L0_ffn_in['W1'], 'L0_ffn_b1': _L0_ffn_in['b1'], 'L0_ffn_W2': _L0_ffn_in['W2'], 'L0_ffn_b2': _L0_ffn_in['b2'], 'L0_ffn_gln_g': _L0_ffn_in['gln_g'], 'L0_ffn_gln_b': _L0_ffn_in['gln_b'], 'L1_gnn_W1l': _L1_gnn_in['W1l'], 'L1_gnn_b1l': _L1_gnn_in['b1l'], 'L1_gnn_W1r': _L1_gnn_in['W1r'], 'L1_gnn_W2l': _L1_gnn_in['W2l'], 'L1_gnn_b2l': _L1_gnn_in['b2l'], 'L1_gnn_W2r': _L1_gnn_in['W2r'], 'L1_gnn_ln1_w': _L1_gnn_in['ln1_w'], 'L1_gnn_ln1_b': _L1_gnn_in['ln1_b'], 'L1_gnn_ln2_w': _L1_gnn_in['ln2_w'], 'L1_gnn_ln2_b': _L1_gnn_in['ln2_b'], 'L1_ffn_ln_g': _L1_ffn_in['ln_g'], 'L1_ffn_ln_b': _L1_ffn_in['ln_b'], 'L1_ffn_w_r': _L1_ffn_in['w_r'], 'L1_ffn_b_r': _L1_ffn_in['b_r'], 'L1_ffn_W1': _L1_ffn_in['W1'], 'L1_ffn_b1': _L1_ffn_in['b1'], 'L1_ffn_W2': _L1_ffn_in['W2'], 'L1_ffn_b2': _L1_ffn_in['b2']}

def reference(x, src, dst, edge_type_3, node_type_3, L0_gnn_W_rel, L0_gnn_b_rel, L0_gnn_W_self, L0_gnn_b_self, L0_ffn_ln_g, L0_ffn_ln_b, L0_ffn_wg_group, L0_ffn_wg_inner, L0_ffn_W1, L0_ffn_b1, L0_ffn_W2, L0_ffn_b2, L0_ffn_gln_g, L0_ffn_gln_b, L1_gnn_W1l, L1_gnn_b1l, L1_gnn_W1r, L1_gnn_W2l, L1_gnn_b2l, L1_gnn_W2r, L1_gnn_ln1_w, L1_gnn_ln1_b, L1_gnn_ln2_w, L1_gnn_ln2_b, L1_ffn_ln_g, L1_ffn_ln_b, L1_ffn_w_r, L1_ffn_b_r, L1_ffn_W1, L1_ffn_b1, L1_ffn_W2, L1_ffn_b2):
    import jax
    import jax.numpy as jnp

    def _L0_gnn_ref(x, W_rel, b_rel, W_self, b_self, edge_src, edge_dst, edge_type, node_type):
        import jax, jax.numpy as jnp
        import numpy as np
        N_NODES = 625
        N_EDGES = 150000
        D_IN = 512
        D_OUT = 512
        N_REL = 3
        N_NT = 3
        xr = jnp.einsum('nd,rde->rne', x, W_rel)
        msg = xr[edge_type, edge_src] + b_rel[edge_type]
        agg = jax.ops.segment_sum(msg, edge_dst, num_segments=N_NODES)
        xs = jnp.einsum('nd,tde->tne', x, W_self)
        h_self = xs[node_type, jnp.arange(N_NODES)] + b_self[node_type]
        return jax.nn.relu(h_self + agg)

    def _L0_ffn_ref(inp, ln_g, ln_b, wg_group, wg_inner, W1, b1, W2, b2, gln_g, gln_b):
        import jax, jax.numpy as jnp
        import numpy as np
        B, T, D, H = (2, 1024, 512, 64)
        G, E = (4, 8)
        GK, EK = (2, 2)
        EPS = 1e-05
        SCALE = 0.02

        def _layernorm(x, g, b):
            m = jnp.mean(x, axis=-1, keepdims=True)
            xc = x - m
            v = jnp.mean(xc * xc, axis=-1, keepdims=True)
            return xc * jax.lax.rsqrt(v + EPS) * g + b

        def _topk_gate(logits, k, n):
            v, i = jax.lax.top_k(logits, k)
            sc = jax.nn.softmax(v, axis=-1)
            return jnp.sum(jax.nn.one_hot(i, n, dtype=logits.dtype) * sc[..., None], axis=-2)
        b, t, d = inp.shape
        x = inp.reshape(-1, d)
        gw = _topk_gate(x @ wg_group, GK, G)
        z = _layernorm(x, ln_g, ln_b)
        out = jnp.zeros_like(x)
        for g in range(G):
            iw = _topk_gate(z @ wg_inner[g], EK, E)
            moe = jnp.zeros_like(z)
            for e in range(E):
                h = jax.nn.relu(z @ W1[g, e] + b1[g, e])
                moe = moe + iw[:, e:e + 1] * (h @ W2[g, e] + b2[g, e])
            y = _layernorm(z + moe, gln_g[g], gln_b[g])
            out = out + gw[:, g:g + 1] * y
        return out.reshape(b, t, d) + inp

    def _L1_gnn_ref(x, edge_index, W1l, b1l, W1r, W2l, b2l, W2r, ln1_w, ln1_b, ln2_w, ln2_b):
        import jax, jax.numpy as jnp
        import numpy as np
        N, E, D = (50000, 12500, 512)

        def _sage_conv(x, src, dst, Wl, bl, Wr, n_nodes):
            agg = jax.ops.segment_sum(x[src], dst, num_segments=n_nodes)
            deg = jax.ops.segment_sum(jnp.ones((src.shape[0],), x.dtype), dst, num_segments=n_nodes)
            agg = agg / jnp.maximum(deg, 1.0)[:, None]
            return agg @ Wl.T + bl + x @ Wr.T

        def _layer_norm(h, w, b, eps=1e-05):
            mu = jnp.mean(h, axis=-1, keepdims=True)
            var = jnp.mean(jnp.square(h - mu), axis=-1, keepdims=True)
            return (h - mu) * jax.lax.rsqrt(var + eps) * w + b
        src, dst = (edge_index[0], edge_index[1])
        n_nodes = x.shape[0]
        h = _sage_conv(x, src, dst, W1l, b1l, W1r, n_nodes)
        h = jax.nn.relu(_layer_norm(h, ln1_w, ln1_b)) + x
        h2 = _sage_conv(h, src, dst, W2l, b2l, W2r, n_nodes)
        h2 = _layer_norm(h2, ln2_w, ln2_b)
        return h2 + h

    def _L1_ffn_ref(x, ln_g, ln_b, w_r, b_r, W1, b1, W2, b2):
        import jax, jax.numpy as jnp
        import numpy as np
        D = 512
        E = 8
        K = 2
        EXP = 4
        LN_EPS = 1e-05
        B, T, d = x.shape
        mu = jnp.mean(x, axis=-1, keepdims=True)
        var = jnp.mean(jnp.square(x - mu), axis=-1, keepdims=True)
        h = (x - mu) * jax.lax.rsqrt(var + LN_EPS) * ln_g + ln_b
        logits = jnp.einsum('btd,ed->bte', h, w_r) + b_r
        topk_vals, topk_idx = jax.lax.top_k(logits, K)
        gates = jax.nn.softmax(topk_vals, axis=-1)
        hf = h.reshape(B * T, d)
        hid = jax.nn.gelu(jnp.einsum('nd,edf->nef', hf, W1) + b1, approximate=False)
        expert_stack = jnp.einsum('nef,efd->ned', hid, W2) + b2
        idx_flat = topk_idx.reshape(B * T, K)
        gates_flat = gates.reshape(B * T, K)
        gathered = jnp.take_along_axis(expert_stack, idx_flat[:, :, None], axis=1)
        mixed = jnp.sum(gathered * gates_flat[:, :, None], axis=1).reshape(B, T, d)
        return x + mixed
    edge_index = jnp.stack([src, dst])
    x = x + _L0_gnn_ref(_layernorm(x, axis=-1), L0_gnn_W_rel, L0_gnn_b_rel, L0_gnn_W_self, L0_gnn_b_self, src, dst, edge_type_3, node_type_3)
    x = x + _L0_ffn_ref(_layernorm(x, axis=-1)[None], L0_ffn_ln_g, L0_ffn_ln_b, L0_ffn_wg_group, L0_ffn_wg_inner, L0_ffn_W1, L0_ffn_b1, L0_ffn_W2, L0_ffn_b2, L0_ffn_gln_g, L0_ffn_gln_b)[0]
    x = x + _L1_gnn_ref(_layernorm(x, axis=-1), edge_index, L1_gnn_W1l, L1_gnn_b1l, L1_gnn_W1r, L1_gnn_W2l, L1_gnn_b2l, L1_gnn_W2r, L1_gnn_ln1_w, L1_gnn_ln1_b, L1_gnn_ln2_w, L1_gnn_ln2_b)
    x = x + _L1_ffn_ref(_layernorm(x, axis=-1)[None], L1_ffn_ln_g, L1_ffn_ln_b, L1_ffn_w_r, L1_ffn_b_r, L1_ffn_W1, L1_ffn_b1, L1_ffn_W2, L1_ffn_b2)[0]
    return x

_drawn_inputs = setup_inputs


def setup_inputs(seed=0):
    import zlib

    import numpy as np

    out = dict(_drawn_inputs(seed))
    spreads = {'L0_gnn_b_rel': (0.0, 0.1),
     'L0_gnn_b_self': (0.0, 0.1),
     'L0_ffn_ln_g': (1.0, 0.2),
     'L0_ffn_ln_b': (0.0, 0.314),
     'L0_ffn_b1': (0.0, 0.8),
     'L0_ffn_b2': (0.0, 0.608),
     'L0_ffn_gln_g': (1.0, 0.2),
     'L0_ffn_gln_b': (0.0, 0.454),
     'L1_gnn_b1l': (0.0, 0.1),
     'L1_gnn_b2l': (0.0, 0.358),
     'L1_gnn_ln1_w': (1.0, 0.2),
     'L1_gnn_ln1_b': (0.0, 0.44),
     'L1_gnn_ln2_w': (1.0, 0.2),
     'L1_gnn_ln2_b': (0.0, 0.422),
     'L1_ffn_ln_g': (1.0, 0.6),
     'L1_ffn_ln_b': (0.0, 0.525),
     'L1_ffn_b_r': (0.0, 0.8),
     'L1_ffn_b1': (0.0, 0.8),
     'L1_ffn_b2': (0.0, 0.693)}
    factors = {'L0_ffn_wg_inner': 4.456, 'L0_ffn_W1': 8.0, 'L0_ffn_W2': 7.707}
    for name, (base, spread) in spreads.items():
        noise = np.random.default_rng([zlib.crc32(name.encode()), seed]).standard_normal(out[name].shape)
        drawn = base * np.exp(spread * noise) if base else spread * noise
        out[name] = jnp.asarray(drawn.astype(out[name].dtype))
    for name, factor in factors.items():
        out[name] = (out[name] * factor).astype(out[name].dtype)
    return out
```

```python
from contextlib import ExitStack

import numpy as np

import concourse.bass as bass
from concourse import mybir

F32 = mybir.dt.float32
F32R = mybir.dt.float32r
F16 = mybir.dt.float16
I32 = mybir.dt.int32
U32 = mybir.dt.uint32
U16 = mybir.dt.uint16
ALU = mybir.AluOpType
ACT = mybir.ActivationFunctionType
AX = mybir.AxisListType

N = 625
D = 512
NT, TP = 5, 125
NP2 = N + 1
HALF = [(0, 314), (314, 312)]
KD = D // 128
E = 20000
ET = E // TP
UNR = 4
NR = 3
CW = NR * TP
G0, E0 = 4, 8
NX = 8
DH = 2048
SLOTS = 256
NI = 12
assert NI >= (2 * N + NX * (SLOTS - 1)) // SLOTS
EPS = 1e-5
NEG = -3.0e38
HU = 1024
STATIC = 36
PER_ITEM = 16
RING = 4
PARTS = [(0, 3), (3, 5)]

WORK, ACC = {}, {}
_n = 0
for _name, _uses in [("T0", 8), ("Y", 15), ("SELF", 15), ("AGG", 5), ("T1", 8), ("LG", 1), ("T2", 8),
                     ("LI", 1), ("GT", 4), ("FF", 64), ("GB", 5), ("T3", 8), ("DEG", 1), ("AG1", 8),
                     ("C1", 5), ("T4", 8), ("AG2", 8), ("C2", 5), ("T5", 8), ("LR", 1), ("POS", 1),
                     ("GX", 2), ("FB", 5), ("DG", 5), ("END", 0)]:
    WORK[_name] = _n
    _n += _uses
_n = 0
for _name, _uses in [("CNT", 25), ("MOE", 20), ("C1", 5), ("C2", 5), ("END", 0)]:
    ACC[_name] = _n
    _n += _uses
LN = {n: i for i, n in enumerate(["x0", "x1", "z", "g0", "g1", "g2", "g3", "x2", "c1", "c2", "x3", "w0"])}

LN_OUT = {n: i for i, n in enumerate([n for n in LN if n[0] != "g"])}


def unit_end(k):
    if k < 3:
        return "work", WORK["Y"] + 5 * (k + 1)
    if k < 6:
        return "work", WORK["SELF"] + 5 * (k - 2)
    if k < 14:
        kind, g = [("h", 0), ("h", 1), ("o", 0), ("h", 2), ("o", 1), ("h", 3), ("o", 2), ("o", 3)][k - 6]
        return ("work", WORK["FF"] + 16 * (g + 1)) if kind == "h" else ("acc", ACC["MOE"] + 5 * (g + 1))
    return [("acc", ACC["C1"] + 5), ("work", WORK["C1"] + 5),
            ("acc", ACC["C2"] + 5), ("work", WORK["C2"] + 5)][k - 14]


def gnn_moe(nc, x_in, ids_in, ntype_in, rows_in, wstat, wmoe, gate_in, b1_0, b2_0, glnb_in,
            rb_in, b1_1, b2_1, out):
    with ExitStack() as ctx:
        def sb(name, shape, dt=F32):
            return ctx.enter_context(nc.sbuf_tensor(name, shape, dt))

        sems = {}

        def sem(name):
            if name not in sems:
                sems[name] = ctx.enter_context(nc.semaphore(name))
            return sems[name]

        X = sb("X", [TP, NT, D])
        U = sb("U", [128, NT, D])
        Z = sb("Z", [128, NT, D])
        HB = sb("HB", [128, NT, D])
        rows = sb("rows", [TP, 6, D])
        raw = sb("raw", [128, RING, HU])
        wsp = sb("wsp", [128, RING, 2, HU], F32R)
        XT = sb("XT", [128, 2, KD, NP2], F32R)
        BIGW = 2 * NR * NT * D + 2 * NT * CW
        BIG = sb("BIG", [128, BIGW], F32R)
        tot = sb("tot", [TP, NT, NP2], U16)
        iota = sb("iota", [TP, 16])
        mk = sb("mk", [128, 128])
        mk64 = sb("mk64", [32, 128])
        kg = sb("kg", [32, 2, G0])
        ident = sb("ident", [128, 128])
        ones = sb("ones", [TP, 128])
        ones_r = sb("ones_r", [TP, 2], F32R)
        epst = sb("epst", [TP, 1])
        nti = sb("nti", [TP, NT], I32)
        ntf = sb("ntf", [TP, NT])
        mask = sb("mask", [TP, NR, NT])
        stats = sb("stats", [TP, NT, 6])
        mv = sb("mv", [TP, NT, 2])
        std = sb("std", [TP, NT])
        rs = sb("rs", [TP, NT])
        ga = sb("ga", [TP, NT])
        gc = sb("gc", [TP, NT])
        gw = sb("gw", [128, 2, KD, 44], F32R)
        LGT = sb("LGT", [TP, NT, 5, 8])
        v8 = sb("v8", [TP, NT, 5, 8])
        idxf = sb("idxf", [TP, NT, 5, 2])
        p12 = sb("p12", [TP, NT, 5, 2])
        ex = sb("ex", [TP, NT, 5])
        gat = v8
        eqt = LGT
        b1c = sb("b1c", [128, 16])
        b1e = sb("b1e", [128, NX * 16])
        rbt = sb("rbt", [TP, NX])
        rdeg = sb("rdeg", [TP, NT])
        cum = sb("cum", [128, 3, NX])
        one8 = sb("one8", [128, NX])
        i12 = sb("i12", [1, NI])
        itf = sb("itf", [1, NI])
        items = sb("items", [1, NI], I32)
        gsl = sb("gsl", [TP, NT, 4])
        gcur = sb("gcur", [TP, NT, 2])
        sid = sb("sid", [128, 2])
        gs = sb("gs", [128, 2, 2])
        gsum = sb("gsum", [128, 2])

        def flat(t):
            return t[:, :, :].rearrange("p a b -> p (a b)")

        def big(p, off, *shape):
            n = int(np.prod(shape))
            names = list("abcde"[:len(shape)])
            pat = f"p ({' '.join(names)}) -> p {' '.join(names)}"
            return BIG[0:p, off:off + n].rearrange(pat, **dict(zip(names, shape)))

        Y = big(TP, 0, 2, NR * NT, D)
        AC = big(TP, 2 * NR * NT * D, 2, NT, CW)
        HT = big(128, 0, 2, 2, KD, NP2)
        o = 4 * KD * NP2
        IW = big(32, o, 2, NP2)
        o += 2 * NP2
        SEL = big(32, o, 16, 128)
        o += 16 * 128
        B2 = big(32, o, 2, G0, D)
        assert o + 2 * G0 * D <= BIGW
        XS = big(TP, 0, 2, NT, D)
        AT = big(TP, 2 * NT * D, 2, NT, NP2)
        AG = big(128, 2 * NT * D + 2 * NT * NP2, 2, KD, NP2)
        o = 2 * NT * D
        XC = big(128, o, 2, KD, SLOTS)
        o += 2 * KD * SLOTS
        S = big(TP, o, NT, SLOTS)
        o += NT * SLOTS
        HD = big(128, o, 2, 2, 2, SLOTS)
        o += 8 * SLOTS
        ST = big(128, o, 2, N)
        o += 2 * N
        YS = big(128, o, 2, 2, D)
        assert o + 4 * D <= BIGW

        zf, uf, hf = flat(Z), flat(U), flat(HB)
        es, ek = zf[0:TP, 0:ET], zf[0:TP, ET:2 * ET]
        iok = zf[0:TP, 320:1260].bitcast(F16)
        ohs = zf[0:TP, 1260:2516].bitcast(F16)[:, 0:UNR * 628].rearrange("p (u n) -> p u n", u=UNR)
        ohk = uf[0:TP, 0:752].bitcast(F16).rearrange("p (u n) -> p u n", u=UNR)
        zero = uf[0:TP, 752:752 + 188].bitcast(F16)
        ytmp = [uf[0:TP, 1024 + D * i:1536 + D * i] for i in range(3)]
        ids = hf[0:TP, 0:3 * ET].bitcast(I32).rearrange("p (a n) -> p a n", a=3)
        gwraw = hf[:, 3 * ET:3 * ET + KD * 44].rearrange("p (a n) -> p a n", a=KD)
        f1 = [uf[:, 314 * i:314 * i + 314] for i in range(2)]
        f2 = [uf[:, 314 * (i + 2):314 * (i + 2) + 314] for i in range(2)]
        gT = uf[0:8, 1256:1256 + NP2]
        bT = uf[0:8, 1882:1882 + D]
        i8 = hf[0:TP, 2000:2200].bitcast(U32).rearrange("p (a b n) -> p a b n", a=NT, b=5)
        b2f = hf[0:32, 0:D]
        b2m = hf[0:32, D:2 * D]
        R4 = uf[:, 0:4 * N].rearrange("p (a n) -> p a n", a=4)
        dg = [hf[0:TP, 500 * i:500 * i + 500].rearrange("p (a n) -> p a n", a=4) for i in range(2)]
        selt = hf[0:TP, 1000:1040].rearrange("p (a n) -> p a n", a=NT)
        gsb = hf[0:TP, 1040:1080].rearrange("p (a n) -> p a n", a=NT)
        eq1 = hf[0:TP, 1080:1120].rearrange("p (a n) -> p a n", a=NT)
        cbase = hf[0:128, 1120:1128]
        ele = hf[0:1, 1400:1400 + NI * NX].rearrange("p (a n) -> p a n", a=NI)
        tri = hf[0:TP, 1200:1325]
        stmp, junk = hf[:, 0:N], hf[:, N:2 * N]
        s1 = hf[0:TP, 1250:1250 + NT * SLOTS].rearrange("p (a n) -> p a n", a=NT)
        hid = zf[:, 0:1024].rearrange("p (b c s) -> p b c s", b=2, c=2)
        ysf = zf[:, 1024:2048].rearrange("p (a n) -> p a n", a=2)
        siota = rows[:, 5, 0:SLOTS]

        ps = [ctx.enter_context(nc.psum_tensor(f"bank{i}", [128, 512], F32)) for i in range(8)]

        x_in_s, ids_in_s, small_in = sem("x_landed"), sem("ids_landed"), sem("small_landed")
        rows_in_s = [sem(f"rows_landed{i}") for i in range(4)]
        bt_in = [sem(f"bias_rows_landed{i}") for i in range(2)]
        b2_in = sem("b2_landed")
        raw_in = [sem(f"raw_landed{i}") for i in range(RING)]
        weight_hi, weight_lo = sem("weight_hi"), sem("weight_lo")
        work_full, work_drained = sem("work_full"), sem("work_drained")
        acc_full, acc_drained = sem("acc_full"), sem("acc_drained")
        iotas, step = sem("iotas_made"), sem("vector_step")
        ln_std, ln_mom, ln_out = sem("ln_std"), sem("ln_moments"), sem("ln_out")
        xt_hi, y_hi, y_lo = sem("xt_hi"), sem("y_hi"), sem("y_lo")
        oh_ready, oh_used = sem("onehot_ready"), sem("onehot_used")
        ac_hi, ag_hi = sem("ac_hi"), sem("ag_hi")
        ex_in, ex_out = sem("exp_in"), sem("exp_out")
        gates_ready, gt_hi = sem("gates_ready"), sem("gates_t_hi")
        relu_done, f2_done, ht_hi, ht_lo = sem("relu_done"), sem("gated"), sem("ht_hi"), sem("ht_lo")
        xs_src, xs_hi, xs_lo = sem("xs_source"), sem("xs_hi"), sem("xs_lo")
        at_hi, at_lo = sem("at_hi"), sem("at_lo")
        consts_ready, x1_done, z_done = sem("constants_ready"), sem("x1_done"), sem("z_done")
        rows_free = sem("rows_free")
        sel_ready, diag_ready, items_ready = sem("sel_ready"), sem("diag_ready"), sem("items_ready")
        route_ready, s_ready, st_ready = sem("route_ready"), sem("s_ready"), sem("st_ready")
        xc_full, xc_hi, xc_lo = sem("xc_full"), sem("xc_hi"), sem("xc_lo")
        h_full, hid_done, hd_hi, hd_lo = sem("h_full"), sem("hid_done"), sem("hd_hi"), sem("hd_lo")
        w2_used, o_full, ys_done, ys_hi, ys_lo = (sem("w2_used"), sem("o_full"), sem("ys_done"),
                                                  sem("ys_hi"), sem("ys_lo"))
        sc_full, sc_added = sem("scattered"), sem("scatter_added")
        out_done = sem("out_landed")

        block = ctx.enter_context(nc.Block())

        def bank_w(k):
            return ps[5 + k % 3]

        @block.sync
        def _(sp):
            sp.dma_start(X[:, :, :], x_in).then_inc(x_in_s, 16)
            sp.dma_start(ids, ids_in).then_inc(ids_in_s, 16)
            for n in range(STATIC):
                if n >= RING:
                    sp.wait_ge(weight_lo, n - RING + 1)
                sp.dma_start(raw[:, n % RING, :], wstat[n]).then_inc(raw_in[n % RING], 16)
            sp.wait_ge(items_ready, 1)
            with sp.Fori(0, NI) as i:
                e = sp.value_load(items[0:1, bass.ds(i, 1)], min_val=0, max_val=NX - 1)
                for k in range(PER_ITEM):
                    sp.wait_ge(weight_lo, i * PER_ITEM + (STATIC + k - RING + 1))
                    sp.dma_start(raw[:, k % RING, :],
                                 wmoe[bass.ds(e, 1), k].rearrange("a p n -> (a p) n")
                                 ).then_inc(raw_in[k % RING], 16)
            sp.wait_ge(sc_added, NT * NI + NT)
            sp.dma_start(out, X[:, :, :]).then_inc(out_done, 16)
            sp.wait_ge(out_done, 16)

        @block.gpsimd
        def _(pool):
            def io(o_, pattern, mul):
                pool.iota(o_, pattern, base=0, channel_multiplier=mul,
                          allow_small_or_imprecise_dtypes=True).then_inc(iotas, 1)

            io(mk[:, :], [[1, 128]], -1)
            io(iota[:, :], [[1, 16]], 0)
            io(mk64[:, :], [[1, 2], [0, 64]], -1)
            io(kg[:, 0, :], [[-8, G0]], 1)
            io(iok, [[1, 1880]], 0)
            io(i12[:, :], [[1, NI]], 0)
            io(sid[:, :], [[128, 2]], 1)

            def lo(slot):
                pool.tensor_tensor(wsp[:, slot, 1, :], raw[:, slot, :],
                                   wsp[:, slot, 0, :].bitcast(F32), ALU.subtract).then_inc(weight_lo, 1)

            for n in range(STATIC):
                pool.wait_ge(weight_hi, n + 1)
                lo(n % RING)
            pool.wait_ge(rows_free, 4)
            io(siota, [[1, SLOTS]], 0)
            with pool.Fori(0, NI) as i:
                for k in range(PER_ITEM):
                    pool.wait_ge(weight_hi, i * PER_ITEM + (STATIC + k + 1))
                    lo(k % RING)

        @block.scalar
        def _(act):
            def rows_load(dst0, src0, n, sem_):
                for r in range(n):
                    act.dma_start(rows[:, dst0 + r, :],
                                  rows_in[src0 + r:src0 + r + 1, :].partition_broadcast(TP)
                                  .rearrange("p a n -> p (a n)")).then_inc(sem_, 16)

            act.dma_start(gwraw, gate_in).then_inc(small_in, 16)
            act.dma_start(nti[:, :], ntype_in).then_inc(small_in, 16)
            act.dma_start(b1c[:, :], b1_0).then_inc(small_in, 16)
            act.dma_start(b1e[:, :], b1_1).then_inc(small_in, 16)
            act.dma_start(rbt[:, :], rb_in.partition_broadcast(TP).rearrange("p a n -> p (a n)")
                          ).then_inc(small_in, 16)
            rows_load(0, 0, 6, rows_in_s[0])

            def copy(dst, src, sem_):
                act.activation(dst, src, ACT.Copy).then_inc(sem_, 1)

            def hi_unit(k):
                if k >= STATIC // 2:
                    return
                for n in (2 * k, 2 * k + 1):
                    act.wait_ge(raw_in[n % RING], 16 * (n // RING + 1))
                    if k >= 2:
                        kind, v = unit_end(k - 2)
                        act.wait_ge(work_full if kind == "work" else acc_full, v)
                    copy(wsp[:, n % RING, 0, :], raw[:, n % RING, :], weight_hi)

            def norm(name):
                act.wait_ge(ln_mom, LN[name] + 1)
                act.activation(std[:, :], mv[:, :, 1], ACT.Sqrt, bias=epst[:, 0:1]).then_inc(ln_std, 1)

            def transposed(name):
                k = WORK[name]
                for dk in range(KD):
                    for a, b in PARTS:
                        act.wait_ge(work_full, k + 1)
                        copy(XT[:, 0, dk, TP * a:TP * b], bank_w(k)[:, 0:TP * (b - a)], xt_hi)
                        k += 1

            def split_rows(s):
                for j in range(NT):
                    act.wait_ge(xs_src, NT * s + j + 1)
                    copy(XS[:, 0, j, :], (U, U, Z)[s][0:TP, j, :], xs_hi)

            def aggregated(name, s):
                k = WORK[name]
                for dk in range(KD):
                    for c0, w in HALF:
                        act.wait_ge(work_full, k + 1)
                        copy(AG[:, 0, dk, c0:c0 + w], bank_w(k)[:, 0:w], ag_hi)
                        k += 1

            def gate_exp(s):
                act.wait_ge(ex_in, s + 1)
                act.activation(ex[:, :, :], ex[:, :, :], ACT.Exp).then_inc(ex_out, 1)

            hi_unit(0)
            hi_unit(1)
            act.wait_ge(consts_ready, 1)
            norm("x0")
            transposed("T0")
            for r in range(NR):
                for j in range(NT):
                    act.wait_ge(work_drained, WORK["Y"] + NT * r + j + 1)
                    copy(Y[:, 0, NT * r + j, :], ytmp[(NT * r + j) % 3], y_hi)
                hi_unit(r + 2)
            for t in range(NR):
                hi_unit(t + 5)
            for c in range(NT):
                for j in range(NT):
                    act.wait_ge(acc_full, NT * c + j + 1)
                    copy(AC[:, 0, j, :], ps[j][0:TP, 0:CW], ac_hi)
            act.wait_ge(rows_free, 1)
            rows_load(0, 6, 6, rows_in_s[1])
            act.dma_start(b2f, b2_0).then_inc(b2_in, 16)
            norm("x1")
            transposed("T1")
            norm("z")
            transposed("T2")
            act.wait_ge(z_done, 1)
            act.dma_start(bT[0:G0, :], glnb_in).then_inc(bt_in[0], 16)
            gate_exp(0)
            for k in range(2):
                act.wait_ge(work_full, WORK["GT"] + k + 1)
                a, b = PARTS[k]
                copy(IW[:, 0, TP * a:TP * b], bank_w(WORK["GT"] + k)[0:32, 0:TP * (b - a)], gt_hi)

            def hidden(g):
                for s in range(8):
                    cc, (c0, w) = s // 2, HALF[s % 2]
                    k = WORK["FF"] + 16 * g + 2 * s
                    q = 8 * g + s
                    act.wait_ge(work_full, k + 1)
                    if q >= 2:
                        act.wait_ge(f2_done, q - 1)
                    act.activation(f1[q % 2][:, 0:w], bank_w(k)[:, 0:w], ACT.Relu,
                                   bias=b1c[:, 4 * g + cc:4 * g + cc + 1]).then_inc(relu_done, 1)
                    act.wait_ge(f2_done, q + 1)
                    copy(HT[:, g % 2, 0, cc, c0:c0 + w], f2[q % 2][:, 0:w], ht_hi)

            hidden(0)
            hi_unit(8)
            hidden(1)
            hi_unit(9)
            norm("g0")
            hi_unit(10)
            hidden(2)
            hi_unit(11)
            norm("g1")
            hi_unit(12)
            hidden(3)
            hi_unit(13)
            norm("g2")
            hi_unit(14)
            norm("g3")
            hi_unit(15)
            act.wait_ge(rows_free, 2)
            rows_load(0, 12, 6, rows_in_s[2])
            norm("x2")
            for j in range(NT):
                act.wait_ge(work_full, WORK["GB"] + 5)
                act.wait_ge(xs_src, j + 1)
                copy(XS[:, 0, j, :], U[0:TP, j, :], xs_hi)
                copy(AT[:, 0, j, :], tot[:, j, :], at_hi)
            transposed("T3")
            aggregated("AG1", 0)
            hi_unit(16)
            hi_unit(17)
            norm("c1")
            split_rows(1)
            transposed("T4")
            aggregated("AG2", 1)
            norm("c2")
            act.wait_ge(rows_free, 3)
            rows_load(0, 18, 2, rows_in_s[3])
            norm("x3")
            norm("w0")
            split_rows(2)
            transposed("T5")
            act.wait_ge(z_done, 2)
            act.dma_start(bT, b2_1).then_inc(bt_in[1], 16)
            gate_exp(1)
            act.wait_ge(items_ready, 1)
            act.wait_ge(work_drained, WORK["END"])
            def hi_item(i, k):
                act.wait_ge(raw_in[k % RING], i * (16 * PER_ITEM // RING)
                            + 16 * ((STATIC + k) // RING + 1))
                used(i, k - RING)
                copy(wsp[:, k % RING, 0, :], raw[:, k % RING, :], weight_hi)

            def used(i, k):
                kind, q = ORDER[k % PER_ITEM]
                d = k // PER_ITEM
                if kind == "h":
                    act.wait_ge(h_full, i * 16 + (16 * d + 2 * q + 2))
                elif q < 7:
                    act.wait_ge(w2_used, i * 7 + (7 * d + q + 1))
                else:
                    act.wait_ge(o_full, i * 2 + (2 * d + 2))

            for n in range(RING):
                act.wait_ge(raw_in[n], 16 * ((STATIC + n) // RING + 1))
                copy(wsp[:, n, 0, :], raw[:, n, :], weight_hi)
            with act.Fori(0, NI) as i:
                e = act.value_load(items[0:1, bass.ds(i, 1)], min_val=0, max_val=NX - 1)
                for dk in range(KD):
                    act.wait_ge(xc_full, i * KD + (dk + 1))
                    copy(XC[:, 0, dk, :], ps[6 + dk % 2][:, 0:SLOTS], xc_hi)
                for m, (kind, q) in enumerate(ORDER):
                    if kind == "h":
                        for f in range(2):
                            n = 2 * q + f
                            act.wait_ge(h_full, i * 16 + (n + 1))
                            if n >= 4:
                                act.wait_ge(hd_lo, i * 16 + (n - 3))
                            act.activation(hid[:, q % 2, f, :], ps[2 + n % 4][:, 0:SLOTS], ACT.Gelu,
                                           bias=b1e[:, bass.ds(e * 16 + n, 1)]).then_inc(hid_done, 1)
                            act.wait_ge(hid_done, i * 16 + (n + 1))
                            copy(HD[:, q % 2, 0, f, :], hid[:, q % 2, f, :], hd_hi)
                    if m >= 1 and m - 1 + RING < PER_ITEM:
                        hi_item(i, m - 1 + RING)
                for h in range(2):
                    act.wait_ge(ys_done, i * 2 + (h + 1))
                    copy(YS[:, 0, h, :], ysf[:, h, :], ys_hi)
                with act.If(i < NI - 1):
                    for k in range(PER_ITEM, PER_ITEM + RING):
                        hi_item(i, k)

        @block.tensor
        def _(pe):
            w = [0]
            a = [0]

            def work():
                k = w[0]
                if k >= 3:
                    pe.wait_ge(work_drained, k - 2)
                w[0] += 1
                return bank_w(k)

            def acc(j):
                if a[0] >= NT:
                    pe.wait_ge(acc_drained, a[0] - NT + 1)
                a[0] += 1
                return ps[j]

            def three(o_, terms, start, stop):
                last = None
                for n, (lh, ll, rh, rl) in enumerate(terms):
                    for m, (l, r) in enumerate([(lh, rh), (lh, rl), (ll, rh)]):
                        last = pe.matmul(o_, l, r, start=start and n == 0 and m == 0,
                                         stop=stop and n == len(terms) - 1 and m == 2)
                return last

            def weights(k):
                pe.wait_ge(weight_lo, 2 * k + 2)

            def wpart(k, kc, part, c0=0, cw=D):
                return wsp[:, (2 * k) % RING + kc // 2, part, (kc % 2) * D + c0:(kc % 2) * D + c0 + cw]

            def transpose(name, src):
                assert w[0] == WORK[name]
                for dk in range(KD):
                    for t0, t1 in PARTS:
                        b = work()
                        for j in range(t0, t1):
                            last = pe.transpose(b[:, TP * (j - t0):TP * (j - t0 + 1)],
                                                src[0:TP, j, 128 * dk:128 * dk + 128], ident[0:TP, 0:TP])
                        last.then_inc(work_full, 1)

            def rows_by(o_, src, j, k):
                return three(o_, [(src[:, 0, kc, TP * j:TP * j + TP], src[:, 1, kc, TP * j:TP * j + TP],
                                   wpart(k, kc, 0), wpart(k, kc, 1)) for kc in range(KD)], True, True)

            def small(name, c0, n, stride):
                assert w[0] == WORK[name]
                b = work()
                for j in range(NT):
                    last = three(b[0:TP, stride * j:stride * j + n],
                                 [(XT[:, 0, kc, TP * j:TP * j + TP], XT[:, 1, kc, TP * j:TP * j + TP],
                                   gw[:, 0, kc, c0:c0 + n], gw[:, 1, kc, c0:c0 + n])
                                  for kc in range(KD)], True, True)
                last.then_inc(work_full, 1)

            pe.nop().then_inc(oh_used, UNR)
            pe.wait_ge(consts_ready, 1)
            pe.wait_ge(ln_out, NT)
            transpose("T0", U)
            pe.wait_ge(work_drained, WORK["Y"])
            for r in range(NR):
                weights(r)
                for j in range(NT):
                    rows_by(work()[0:TP, :], XT, j, r).then_inc(work_full, 1)
            for t in range(NR):
                weights(NR + t)
                for j in range(NT):
                    rows_by(work()[0:TP, :], XT, j, NR + t).then_inc(work_full, 1)
            for c in range(NT):
                pe.wait_ge(oh_ready, ET * c + 1)
                for j in range(NT):
                    acc(j)
                    pe.matmul(ps[j][0:TP, 0:CW], zero[:, 0:TP], zero[:, 0:CW], start=True, stop=False)
                with pe.Fori(0, ET // UNR) as it:
                    for u in range(UNR):
                        pe.wait_ge(oh_ready, it * UNR + (ET * c + u + 1))
                        for j in range(NT):
                            last = pe.matmul(ps[j][0:TP, 0:CW], ohs[:, u, TP * j:TP * j + TP],
                                             ohk[:, u, 0:CW], start=False, stop=False)
                        last.then_inc(oh_used, 1)
                for j in range(NT):
                    pe.matmul(ps[j][0:TP, 0:CW], zero[:, 0:TP], zero[:, 0:CW],
                              start=False, stop=True).then_inc(acc_full, 1)
                if c == 0:
                    pe.wait_ge(y_lo, NR * NT)
                pe.wait_ge(acc_drained, NT * (c + 1))
                three(work()[0:TP, :],
                      [(AC[:, 0, j, TP * r:TP * r + TP], AC[:, 1, j, TP * r:TP * r + TP],
                        Y[:, 0, NT * r + j, :], Y[:, 1, NT * r + j, :])
                       for r in range(NR) for j in range(NT)], True, True).then_inc(work_full, 1)
            pe.wait_ge(ln_out, NT * (LN_OUT["x1"] + 1))
            transpose("T1", U)
            pe.wait_ge(work_drained, WORK["LG"])
            small("LG", 0, 4, 8)
            pe.wait_ge(z_done, 1)
            transpose("T2", Z)
            pe.wait_ge(work_drained, WORK["LI"])
            small("LI", 4, 32, 32)
            pe.wait_ge(gates_ready, 1)
            for width, sl in ((32, None), (G0, 4)):
                for t0, t1 in PARTS:
                    b = work()
                    for j in range(t0, t1):
                        src = (gat[:, j, 0:4, :].rearrange("p a b -> p (a b)") if sl is None
                               else gat[:, j, 4, 0:G0])
                        last = pe.transpose(b[0:width, TP * (j - t0):TP * (j - t0 + 1)], src,
                                            ident[0:TP, 0:TP])
                    last.then_inc(work_full, 1)
            pe.wait_ge(work_drained, WORK["FF"])

            def hidden(g, k):
                weights(k)
                for cc in range(KD):
                    for c0, cw in HALF:
                        b = work()
                        three(b[:, 0:cw], [(wpart(k, kc, 0, 128 * cc, 128), wpart(k, kc, 1, 128 * cc, 128),
                                            XT[:, 0, kc, c0:c0 + cw], XT[:, 1, kc, c0:c0 + cw])
                                           for kc in range(KD)], True, True).then_inc(work_full, 1)
                        b = work()
                        pe.matmul(b[:, 0:cw], SEL[:, 4 * g + cc, :], IW[:, 0, c0:c0 + cw],
                                  start=True, stop=False)
                        pe.matmul(b[:, 0:cw], SEL[:, 4 * g + cc, :], IW[:, 1, c0:c0 + cw],
                                  start=False, stop=True).then_inc(work_full, 1)

            def second(g, k):
                weights(k)
                pe.wait_ge(ht_lo, 8 * (g + 1))
                for j in range(NT):
                    sl = slice(TP * j, TP * j + TP)
                    b = acc(j)[0:TP, :]
                    three(b, [(HT[:, g % 2, 0, cc, sl], HT[:, g % 2, 1, cc, sl], wpart(k, cc, 0),
                               wpart(k, cc, 1)) for cc in range(KD)], True, False)
                    three(b, [(IW[:, 0, sl], IW[:, 1, sl], B2[:, 0, g, :], B2[:, 1, g, :])],
                          False, True).then_inc(acc_full, 1)

            hidden(0, 6)
            hidden(1, 7)
            second(0, 8)
            hidden(2, 9)
            second(1, 10)
            hidden(3, 11)
            second(2, 12)
            second(3, 13)
            pe.wait_ge(bt_in[0], 16)
            for j in range(NT):
                pe.matmul(work()[0:TP, :], gT[0:G0, TP * j:TP * j + TP], bT[0:G0, :], start=True,
                          stop=True).then_inc(work_full, 1)
            pe.wait_ge(ln_out, NT * (LN_OUT["x2"] + 1))
            transpose("T3", U)
            pe.wait_ge(at_lo, NT)
            b = work()
            for i in range(NT):
                terms = [(part, j) for part in range(2) for j in range(NT)]
                for n, (part, j) in enumerate(terms):
                    last = pe.matmul(b[0:TP, 2 * i:2 * i + 2], AT[:, part, j, TP * i:TP * i + TP],
                                     ones_r[:, :], start=n == 0, stop=n == len(terms) - 1)
            last.then_inc(work_full, 1)

            def conv(s, k):
                pe.wait_ge(xs_lo, NT * (s + 1))
                for dk in range(KD):
                    for c0, cw in HALF:
                        three(work()[:, 0:cw],
                              [(XS[:, 0, j, 128 * dk:128 * dk + 128], XS[:, 1, j, 128 * dk:128 * dk + 128],
                                AT[:, 0, j, c0:c0 + cw], AT[:, 1, j, c0:c0 + cw])
                               for j in range(NT)], True, True).then_inc(work_full, 1)
                pe.wait_ge(work_drained, WORK[("AG1", "AG2")[s]] + 8)
                weights(k)
                for j in range(NT):
                    rows_by(acc(j)[0:TP, :], AG, j, k).then_inc(acc_full, 1)
                weights(k + 1)
                for j in range(NT):
                    rows_by(work()[0:TP, :], XT, j, k + 1).then_inc(work_full, 1)

            conv(0, 14)
            pe.wait_ge(xs_src, 2 * NT)
            transpose("T4", U)
            conv(1, 16)
            pe.wait_ge(xs_src, 3 * NT)
            transpose("T5", Z)
            pe.wait_ge(work_drained, WORK["LR"])
            small("LR", 36, NX, 8)
            pe.wait_ge(sel_ready, 1)
            b = work()
            for i in range(NT):
                for j in range(i + 1):
                    pe.matmul(b[0:TP, 8 * i:8 * i + 8], tri if j == i else ones[:, 0:TP], selt[:, j, :],
                              start=j == 0, stop=j == i)
            for j in range(NT):
                last = pe.matmul(b[:, 64:72], ones[:, :], selt[:, j, :], start=j == 0, stop=j == NT - 1)
            last.then_inc(work_full, 1)
            for t0, t1 in PARTS:
                b = work()
                for j in range(t0, t1):
                    last = pe.transpose(b[0:NX, TP * (j - t0):TP * (j - t0 + 1)], gat[:, j, 0, :],
                                        ident[0:TP, 0:TP])
                last.then_inc(work_full, 1)
            pe.wait_ge(bt_in[1], 16)
            pe.wait_ge(work_drained, WORK["FB"])
            for j in range(NT):
                pe.matmul(work()[0:TP, :], gT[:, TP * j:TP * j + TP], bT, start=True,
                          stop=True).then_inc(work_full, 1)
            for j in range(NT):
                pe.wait_ge(diag_ready, j + 1)
                pe.matmul(work()[:, 0:4 * TP], ones[:, :], dg[j % 2].rearrange("p a n -> p (a n)"),
                          start=True, stop=True).then_inc(work_full, 1)
            assert w[0] == WORK["END"] and a[0] == ACC["END"]
            pe.wait_ge(work_drained, WORK["END"])
            pe.wait_ge(acc_drained, ACC["END"])
            with pe.Fori(0, NI) as i:
                pe.wait_ge(s_ready, i + 1)
                for dk in range(KD):
                    if dk < 2:
                        pe.wait_ge(sc_added, i * NT + NT)
                    else:
                        pe.wait_ge(xc_lo, i * KD + (dk - 1))
                    for j in range(NT):
                        for part in range(2):
                            last = pe.matmul(ps[6 + dk % 2][:, 0:SLOTS],
                                             XS[:, part, j, 128 * dk:128 * dk + 128], S[:, j, :],
                                             start=j == 0 and part == 0, stop=j == NT - 1 and part == 1)
                    last.then_inc(xc_full, 1)
                pe.wait_ge(xc_lo, i * KD + KD)
                for m, (kind, q) in enumerate(ORDER):
                    pe.wait_ge(weight_lo, i * PER_ITEM + (STATIC + m + 1))
                    wh = wsp[:, m % RING, 0, :].rearrange("p (a n) -> p a n", a=KD if kind == "h" else 2)
                    wl = wsp[:, m % RING, 1, :].rearrange("p (a n) -> p a n", a=KD if kind == "h" else 2)
                    if kind == "h":
                        for f in range(2):
                            n = 2 * q + f
                            if n >= 4:
                                pe.wait_ge(hid_done, i * 16 + (n - 3))
                            three(ps[2 + n % 4][:, 0:SLOTS],
                                  [(wh[:, kc, 128 * f:128 * f + 128], wl[:, kc, 128 * f:128 * f + 128],
                                    XC[:, 0, kc, :], XC[:, 1, kc, :]) for kc in range(KD)],
                                  True, True).then_inc(h_full, 1)
                    else:
                        pe.wait_ge(hd_lo, i * 16 + (2 * q + 2))
                        for h in range(2):
                            hs = slice(128 * h, 128 * h + 128)
                            last = three(ps[h][:, :],
                                         [(HD[:, q % 2, 0, f, hs], HD[:, q % 2, 1, f, hs],
                                           wh[:, f, :], wl[:, f, :]) for f in range(2)], q == 0, q == 7)
                            if q == 7:
                                last.then_inc(o_full, 1)
                        if q < 7:
                            last.then_inc(w2_used, 1)
                pe.wait_ge(st_ready, i + 1)
                pe.wait_ge(ys_lo, i * 2 + 2)
                for j in range(NT):
                    if j >= 2:
                        pe.wait_ge(sc_added, i * NT + (NT + j - 1))
                    for h in range(2):
                        for part in range(2):
                            last = pe.matmul(ps[6 + j % 2][0:TP, :], ST[:, h, TP * j:TP * j + TP],
                                             YS[:, part, h, :], start=h == 0 and part == 0,
                                             stop=h == 1 and part == 1)
                    last.then_inc(sc_full, 1)

        @block.vector
        def _(dve):
            steps = [0]

            def did(ins):
                ins.then_inc(step, 1)
                steps[0] += 1

            def settle():
                dve.wait_ge(step, steps[0])

            def minus(dst, src, hi, sem_=None):
                ins = dve.tensor_tensor(dst, src, hi.bitcast(F32), ALU.subtract)
                if sem_ is None:
                    did(ins)
                else:
                    ins.then_inc(sem_, 1)

            def moments(name, src):
                for j in range(NT):
                    did(dve.bn_stats(stats[:, j, :], src[0:TP, j, :]))
                settle()
                for j in range(NT):
                    ins = dve.bn_aggr(mv[:, j, :], stats[:, j, :])
                    if j < NT - 1:
                        did(ins)
                ins.then_inc(ln_mom, 1)
                dve.wait_ge(ln_std, LN[name] + 1)
                did(dve.reciprocal(rs[:, :], std[:, :]))
                settle()

            def norm(name, src, dst):
                moments(name, src)
                for j in range(NT):
                    dve.tensor_scalar(dst[0:TP, j, :], src[0:TP, j, :], mv[:, j, 0:1], rs[:, j:j + 1],
                                      ALU.subtract, ALU.mult).then_inc(ln_out, 1)
                dve.wait_ge(ln_out, NT * (LN_OUT[name] + 1))

            xt_n = [0]

            def transposed(name):
                k = WORK[name]
                for dk in range(KD):
                    for t0, t1 in PARTS:
                        xt_n[0] += 1
                        dve.wait_ge(work_full, k + 1)
                        dve.wait_ge(xt_hi, xt_n[0])
                        sl = slice(TP * t0, TP * t1)
                        minus(XT[:, 1, dk, sl], bank_w(k)[:, 0:TP * (t1 - t0)], XT[:, 0, dk, sl],
                              work_drained)
                        k += 1

            def gates(n, s):
                settle()
                for j in range(NT):
                    for p in range(n):
                        did(dve.max(v8[:, j, p, :], LGT[:, j, p, :]))
                settle()
                for j in range(NT):
                    for p in range(n):
                        did(dve.max_index(i8[:, j, p, :], v8[:, j, p, :], LGT[:, j, p, :]))
                if n < 5:
                    did(dve.memset(ex[:, :, :], 0.0))
                    settle()
                dve.tensor_tensor(ex[:, :, 0:n], v8[:, :, 0:n, 1], v8[:, :, 0:n, 0],
                                  ALU.subtract).then_inc(ex_in, 1)
                settle()
                did(dve.tensor_copy(idxf[:, :, 0:n, :], i8[:, :, 0:n, 0:2]))
                dve.wait_ge(ex_out, s + 1)
                did(dve.tensor_scalar(p12[:, :, 0:n, 1], ex[:, :, 0:n], 1.0, None, ALU.add))
                settle()
                did(dve.reciprocal(p12[:, :, 0:n, 0], p12[:, :, 0:n, 1]))
                settle()
                did(dve.tensor_tensor(p12[:, :, 0:n, 1], ex[:, :, 0:n], p12[:, :, 0:n, 0], ALU.mult))
                for c, (o_, last) in enumerate(((gat, False), (eqt, True))):
                    shape = [TP, NT, n, 8]
                    it = iota[:, 0:8].unsqueeze(1).unsqueeze(1).to_broadcast(shape)
                    settle()
                    did(dve.tensor_tensor(o_[:, :, 0:n, :], it,
                                          idxf[:, :, 0:n, c:c + 1].to_broadcast(shape), ALU.is_equal))
                    settle()
                    did(dve.tensor_tensor(o_[:, :, 0:n, :], o_[:, :, 0:n, :],
                                          p12[:, :, 0:n, c:c + 1].to_broadcast(shape), ALU.mult))
                settle()
                did(dve.tensor_tensor(gat[:, :, 0:n, :], gat[:, :, 0:n, :], eqt[:, :, 0:n, :], ALU.add))
                settle()

            dve.nop().then_inc(sc_added, NT)
            dve.wait_ge(iotas, 7)
            did(dve.tensor_scalar(ident[:, :], mk[:, :], 0.0, None, ALU.is_equal))
            did(dve.memset(ones[:, :], 1.0))
            did(dve.memset(one8[:, :], 1.0))
            did(dve.memset(ones_r[:, :].bitcast(F32), 1.0))
            did(dve.memset(epst[:, :], EPS))
            did(dve.memset(XT[:, :, :, N:NP2].bitcast(F32), 0.0))
            did(dve.memset(tot[:, :, N:NP2], 0))
            did(dve.memset(LGT[:, :, 4, 4:8], NEG))
            dve.wait_ge(ids_in_s, 16)
            did(dve.tensor_copy(es, ids[:, 0, :]))
            did(dve.tensor_copy(ek, ids[:, 1, :]))
            did(dve.tensor_copy(zf[0:TP, 1260:1260 + ET], ids[:, 2, :]))
            settle()
            did(dve.scalar_tensor_tensor(ek, zf[0:TP, 1260:1260 + ET], float(N), ek, ALU.mult, ALU.add))
            dve.wait_ge(small_in, 80)
            did(dve.tensor_copy(gw[:, 0, :, :], gwraw))
            settle()
            minus(gw[:, 1, :, :], gwraw, gw[:, 0, :, :])
            did(dve.tensor_copy(ntf[:, :], nti[:, :]))
            settle()
            for t in range(NR):
                did(dve.tensor_scalar(mask[:, t, :], ntf[:, :], float(t), None, ALU.is_equal))
            settle()
            dve.nop().then_inc(consts_ready, 1)
            dve.wait_ge(x_in_s, 16)
            norm("x0", X, U)
            dve.wait_ge(rows_in_s[0], 96)
            for j in range(NT):
                did(dve.tensor_scalar(HB[0:TP, j, :], rows[:, 3, :], mask[:, 0, j:j + 1], None, ALU.mult))
            for t in range(1, NR):
                settle()
                for j in range(NT):
                    did(dve.scalar_tensor_tensor(HB[0:TP, j, :], rows[:, 3 + t, :], mask[:, t, j:j + 1],
                                                 HB[0:TP, j, :], ALU.mult, ALU.add))
            transposed("T0")

            def y_low(n):
                dve.wait_ge(y_hi, n + 1)
                minus(Y[:, 1, n, :], ytmp[n % 3], Y[:, 0, n, :], y_lo)

            for n in range(NR * NT):
                k = WORK["Y"] + n
                dve.wait_ge(work_full, k + 1)
                if n >= 3:
                    dve.wait_ge(y_lo, n - 2)
                dve.tensor_tensor(ytmp[n % 3], bank_w(k)[0:TP, :], rows[:, n // NT, :],
                                  ALU.add).then_inc(work_drained, 1)
                if n >= 1:
                    y_low(n - 1)
            y_low(NR * NT - 1)
            settle()
            for n in range(NR * NT):
                t, j = divmod(n, NT)
                k = WORK["SELF"] + n
                dve.wait_ge(work_full, k + 1)
                if t >= 1:
                    dve.wait_ge(work_drained, k - NT + 1)
                dve.scalar_tensor_tensor(HB[0:TP, j, :], bank_w(k)[0:TP, :], mask[:, t, j:j + 1],
                                         HB[0:TP, j, :], ALU.mult, ALU.add).then_inc(work_drained, 1)
            did(dve.memset(zero, 0.0))
            iokr = iok[:, 0:NR * N].rearrange("p (r n) -> p r n", r=NR)
            settle()
            for c in range(NT):
                with dve.Fori(0, ET // UNR) as it:
                    for u in range(UNR):
                        t = it * UNR + u
                        dve.wait_ge(oh_used, it * UNR + (ET * c + u + 1))
                        dve.tensor_scalar(ohs[:, u, 0:N], iok[:, 0:N], es[:, bass.ds(t, 1)], None,
                                          ALU.is_equal)
                        dve.tensor_scalar(
                            ohk[:, u, 0:CW].rearrange("p (r n) -> p r n", r=NR),
                            iokr[:, :, TP * c:TP * c + TP], ek[:, bass.ds(t, 1)], None,
                            ALU.is_equal).then_inc(oh_ready, 1)
                if c >= 1:
                    dve.wait_ge(work_full, WORK["AGG"] + c)
                for j in range(NT):
                    dve.wait_ge(acc_full, NT * c + j + 1)
                    dve.wait_ge(ac_hi, NT * c + j + 1)
                    minus(AC[:, 1, j, :], ps[j][0:TP, 0:CW], AC[:, 0, j, :])
                    with nc.allow_low_precision(reason="counts up to 20000 are exact in uint16"):
                        dve.tensor_reduce(tot[:, j, TP * c:TP * c + TP],
                                          ps[j][0:TP, 0:CW].rearrange("p (r n) -> p n r", r=NR), AX.X,
                                          ALU.add).then_inc(acc_drained, 1)
                k = WORK["AGG"] + c
                dve.wait_ge(work_full, k + 1)
                dve.wait_ge(work_drained, k)
                dve.tensor_tensor(HB[0:TP, c, :], bank_w(k)[0:TP, :], HB[0:TP, c, :],
                                  ALU.add).then_inc(work_drained, 1)
                dve.wait_ge(work_drained, k + 1)
                did(dve.scalar_tensor_tensor(X[:, c, :], HB[0:TP, c, :], 0.0, X[:, c, :],
                                             ALU.max, ALU.add))
            settle()
            dve.nop().then_inc(rows_free, 1)
            norm("x1", X, U)
            for j in range(NT):
                did(dve.tensor_tensor(X[:, j, :], X[:, j, :], U[0:TP, j, :], ALU.add))
            transposed("T1")
            k = WORK["LG"]
            dve.wait_ge(work_full, k + 1)
            dve.tensor_copy(LGT[:, :, 4, 0:4],
                            bank_w(k)[0:TP, 0:40].rearrange("p (a b) -> p a b", a=NT)[:, :, 0:4]
                            ).then_inc(work_drained, 1)
            norm("z", U, Z)
            dve.wait_ge(rows_in_s[1], 96)
            for j in range(NT):
                did(dve.tensor_tensor(Z[0:TP, j, :], Z[0:TP, j, :], rows[:, 0, :], ALU.mult))
            settle()
            for j in range(NT):
                did(dve.tensor_tensor(Z[0:TP, j, :], Z[0:TP, j, :], rows[:, 1, :], ALU.add))
            settle()
            dve.nop().then_inc(z_done, 1)
            for c in range(16):
                did(dve.tensor_scalar(SEL[:, c, :], mk64[:, :], -2.0 * c, None, ALU.is_equal))
            did(dve.memset(IW[:, :, N:NP2].bitcast(F32), 0.0))
            did(dve.tensor_scalar(kg[:, 1, :], kg[:, 0, :], 7.5, None, ALU.is_lt))
            settle()
            did(dve.scalar_tensor_tensor(kg[:, 1, :], kg[:, 0, :], -0.5, kg[:, 1, :], ALU.is_gt, ALU.mult))
            dve.wait_ge(b2_in, 16)
            settle()
            for g in range(G0):
                settle()
                did(dve.tensor_scalar(b2m, b2f, kg[:, 1, g:g + 1], None, ALU.mult))
                settle()
                did(dve.tensor_copy(B2[:, 0, g, :], b2m))
                settle()
                minus(B2[:, 1, g, :], b2m, B2[:, 0, g, :])
            transposed("T2")
            k = WORK["LI"]
            dve.wait_ge(work_full, k + 1)
            dve.tensor_copy(LGT[:, :, 0:4, :],
                            bank_w(k)[0:TP, 0:160].rearrange("p (a b n) -> p a b n", a=NT, b=4)
                            ).then_inc(work_drained, 1)
            dve.wait_ge(work_drained, k + 1)
            gates(5, 0)
            dve.nop().then_inc(gates_ready, 1)
            for n in range(4):
                k = WORK["GT"] + n
                t0, t1 = PARTS[n % 2]
                sl = slice(TP * t0, TP * t1)
                dve.wait_ge(work_full, k + 1)
                if n < 2:
                    dve.wait_ge(gt_hi, n + 1)
                    minus(IW[:, 1, sl], bank_w(k)[0:32, 0:TP * (t1 - t0)], IW[:, 0, sl], work_drained)
                else:
                    dve.tensor_copy(gT[0:G0, sl], bank_w(k)[0:G0, 0:TP * (t1 - t0)]).then_inc(work_drained, 1)

            def hidden(g):
                for s in range(8):
                    cc, (c0, w) = s // 2, HALF[s % 2]
                    k = WORK["FF"] + 16 * g + 2 * s
                    q = 8 * g + s
                    dve.wait_ge(work_full, k + 2)
                    dve.wait_ge(relu_done, q + 1)
                    if q >= 2:
                        dve.wait_ge(ht_lo, q - 1)
                    dve.tensor_tensor(f2[q % 2][:, 0:w], f1[q % 2][:, 0:w], bank_w(k + 1)[:, 0:w],
                                      ALU.mult).then_inc(f2_done, 1)
                    dve.wait_ge(f2_done, q + 1)
                    dve.sem_inc(work_drained, 2)
                    dve.wait_ge(ht_hi, q + 1)
                    minus(HT[:, g % 2, 1, cc, c0:c0 + w], f2[q % 2][:, 0:w],
                          HT[:, g % 2, 0, cc, c0:c0 + w], ht_lo)

            def group(g):
                for j in range(NT):
                    n = ACC["MOE"] + NT * g + j
                    dve.wait_ge(acc_full, n + 1)
                    dve.tensor_tensor(HB[0:TP, j, :], ps[j][0:TP, :], Z[0:TP, j, :],
                                      ALU.add).then_inc(acc_drained, 1)
                dve.wait_ge(acc_drained, ACC["MOE"] + NT * (g + 1))
                moments(f"g{g}", HB)
                did(dve.tensor_tensor(ga[:, :], gat[:, :, 4, g], rs[:, :], ALU.mult))
                settle()
                did(dve.scalar_tensor_tensor(gc[:, :], mv[:, :, 0], -1.0, ga[:, :], ALU.mult, ALU.mult))
                for j in range(NT):
                    did(dve.scalar_tensor_tensor(HB[0:TP, j, :], HB[0:TP, j, :], ga[:, j:j + 1],
                                                 rows[:, 2 + g, :], ALU.mult, ALU.mult))
                settle()
                for j in range(NT):
                    did(dve.tensor_tensor(X[:, j, :], X[:, j, :], HB[0:TP, j, :], ALU.add))
                settle()
                for j in range(NT):
                    did(dve.scalar_tensor_tensor(X[:, j, :], rows[:, 2 + g, :], gc[:, j:j + 1],
                                                 X[:, j, :], ALU.mult, ALU.add))
                settle()

            hidden(0)
            hidden(1)
            group(0)
            hidden(2)
            group(1)
            hidden(3)
            group(2)
            group(3)
            dve.nop().then_inc(rows_free, 1)
            for j in range(NT):
                k = WORK["GB"] + j
                dve.wait_ge(work_full, k + 1)
                dve.tensor_tensor(X[:, j, :], bank_w(k)[0:TP, :], X[:, j, :], ALU.add).then_inc(work_drained, 1)
            dve.wait_ge(work_drained, WORK["GB"] + NT)
            norm("x2", X, U)
            for j in range(NT):
                dve.nop().then_inc(xs_src, 1)
            for j in range(NT):
                dve.wait_ge(xs_hi, j + 1)
                minus(XS[:, 1, j, :], U[0:TP, j, :], XS[:, 0, j, :], xs_lo)
                dve.wait_ge(at_hi, j + 1)
                minus(AT[:, 1, j, :], tot[:, j, :], AT[:, 0, j, :], at_lo)
            transposed("T3")
            k = WORK["DEG"]
            dve.wait_ge(work_full, k + 1)
            dve.tensor_scalar(rdeg[:, :], bank_w(k)[0:TP, 0:2 * NT].rearrange("p (a b) -> p a b", b=2)[:, :, 0],
                              1.0, None, ALU.max).then_inc(work_drained, 1)
            dve.wait_ge(work_drained, k + 1)
            did(dve.reciprocal(rdeg[:, :], rdeg[:, :]))
            settle()
            ag_n = [0]

            def conv(s):
                k = WORK[("AG1", "AG2")[s]]
                for dk in range(KD):
                    for c0, w in HALF:
                        ag_n[0] += 1
                        dve.wait_ge(work_full, k + 1)
                        dve.wait_ge(ag_hi, ag_n[0])
                        minus(AG[:, 1, dk, c0:c0 + w], bank_w(k)[:, 0:w], AG[:, 0, dk, c0:c0 + w],
                              work_drained)
                        k += 1
                if s == 0:
                    dve.wait_ge(rows_in_s[2], 96)
                name = ("C1", "C2")[s]
                for j in range(NT):
                    n = ACC[name] + j
                    dve.wait_ge(acc_full, n + 1)
                    dve.scalar_tensor_tensor(Z[0:TP, j, :], ps[j][0:TP, :], rdeg[:, j:j + 1],
                                             rows[:, 3 * s, :], ALU.mult, ALU.add).then_inc(acc_drained, 1)
                dve.wait_ge(acc_drained, ACC[name] + NT)
                for j in range(NT):
                    k = WORK[name] + j
                    dve.wait_ge(work_full, k + 1)
                    dve.tensor_tensor(Z[0:TP, j, :], bank_w(k)[0:TP, :], Z[0:TP, j, :],
                                      ALU.add).then_inc(work_drained, 1)
                dve.wait_ge(work_drained, WORK[name] + NT)
                norm(("c1", "c2")[s], Z, Z)
                for j in range(NT):
                    did(dve.tensor_tensor(Z[0:TP, j, :], Z[0:TP, j, :], rows[:, 3 * s + 1, :], ALU.mult))
                settle()
                for j in range(NT):
                    did(dve.tensor_tensor(Z[0:TP, j, :], Z[0:TP, j, :], rows[:, 3 * s + 2, :], ALU.add))
                settle()

            conv(0)
            for j in range(NT):
                dve.scalar_tensor_tensor(U[0:TP, j, :], Z[0:TP, j, :], 0.0, U[0:TP, j, :],
                                         ALU.max, ALU.add).then_inc(xs_src, 1)
            dve.wait_ge(xs_src, 2 * NT)
            for j in range(NT):
                dve.wait_ge(xs_hi, NT + j + 1)
                minus(XS[:, 1, j, :], U[0:TP, j, :], XS[:, 0, j, :], xs_lo)
            transposed("T4")
            conv(1)
            dve.nop().then_inc(rows_free, 1)
            for src in (Z, U):
                for j in range(NT):
                    did(dve.tensor_tensor(X[:, j, :], X[:, j, :], src[0:TP, j, :], ALU.add))
                settle()
            norm("x3", X, U)
            norm("w0", U, Z)
            dve.wait_ge(rows_in_s[3], 32)
            for j in range(NT):
                did(dve.tensor_tensor(Z[0:TP, j, :], Z[0:TP, j, :], rows[:, 0, :], ALU.mult))
                did(dve.tensor_tensor(X[:, j, :], X[:, j, :], U[0:TP, j, :], ALU.add))
            settle()
            for j in range(NT):
                dve.tensor_tensor(Z[0:TP, j, :], Z[0:TP, j, :], rows[:, 1, :], ALU.add).then_inc(xs_src, 1)
            dve.wait_ge(xs_src, 3 * NT)
            dve.nop().then_inc(z_done, 1)
            dve.nop().then_inc(rows_free, 1)
            for j in range(NT):
                dve.wait_ge(xs_hi, 2 * NT + j + 1)
                minus(XS[:, 1, j, :], Z[0:TP, j, :], XS[:, 0, j, :], xs_lo)
            transposed("T5")
            k = WORK["LR"]
            dve.wait_ge(work_full, k + 1)
            dve.tensor_tensor(LGT[:, :, 0, :], bank_w(k)[0:TP, 0:40].rearrange("p (a b) -> p a b", a=NT),
                              rbt[:, :].unsqueeze(1).to_broadcast([TP, NT, NX]), ALU.add
                              ).then_inc(work_drained, 1)
            dve.wait_ge(work_drained, k + 1)
            gates(1, 1)
            shape = [TP, NT, NX]
            it = iota[:, 0:8].unsqueeze(1).to_broadcast(shape)
            did(dve.tensor_tensor(eq1, it, idxf[:, :, 0, 0:1].to_broadcast(shape), ALU.is_equal))
            did(dve.tensor_tensor(gsb, it, idxf[:, :, 0, 1:2].to_broadcast(shape), ALU.is_equal))
            did(dve.tensor_scalar(tri, mk[0:TP, 0:TP], 0.0, None, ALU.is_gt))
            settle()
            did(dve.tensor_tensor(selt, eq1, gsb, ALU.add))
            settle()
            dve.nop().then_inc(sel_ready, 1)
            k = WORK["POS"]
            dve.wait_ge(work_full, k + 1)
            b = bank_w(k)
            did(dve.tensor_scalar(cum[:, 1, :], b[:, 64:72], 0.5, None, ALU.is_gt))
            for lim in (SLOTS + 0.5, 2 * SLOTS + 0.5):
                settle()
                did(dve.scalar_tensor_tensor(cum[:, 1, :], b[:, 64:72], lim, cum[:, 1, :],
                                             ALU.is_gt, ALU.add))
            settle()
            did(dve.tensor_tensor_scan(cum[:, 2, :], one8[:, :], cum[:, 1, :], 0.0, ALU.mult, ALU.add))
            settle()
            did(dve.tensor_tensor(cbase, cum[:, 2, :], cum[:, 1, :], ALU.subtract))
            si = [1, NI, NX]
            did(dve.tensor_tensor(ele[:, :, :], cum[0:1, 2, :].unsqueeze(1).to_broadcast(si),
                                  i12[:, :].unsqueeze(2).to_broadcast(si), ALU.is_le))
            settle()
            did(dve.tensor_reduce(itf[:, :], ele[:, :, :], AX.X, ALU.add))
            settle()
            did(dve.tensor_scalar(itf[:, :], itf[:, :], float(NX - 1), None, ALU.min))
            settle()
            dve.tensor_copy(items[:, :], itf[:, :]).then_inc(items_ready, 1)
            gsv = selt
            did(dve.tensor_scalar(cbase, cbase, float(SLOTS), None, ALU.mult))
            settle()
            dve.tensor_tensor(gsv, b[0:TP, 0:40].rearrange("p (a b) -> p a b", a=NT),
                              cbase[0:TP, :].unsqueeze(1).to_broadcast(shape), ALU.add
                              ).then_inc(work_drained, 1)
            dve.wait_ge(work_drained, k + 1)
            did(dve.tensor_tensor(eq1, eq1, gsv, ALU.mult))
            did(dve.tensor_tensor(gsb, gsb, gsv, ALU.mult))
            settle()
            did(dve.tensor_reduce(gsl[:, :, 0], eq1, AX.X, ALU.add))
            did(dve.tensor_reduce(gsl[:, :, 1], gsb, AX.X, ALU.add))
            did(dve.tensor_copy(gsl[:, :, 2:4], p12[:, :, 0, :]))
            settle()
            did(dve.tensor_copy(gcur[:, :, :], gsl[:, :, 0:2]))
            for n in range(2):
                k = WORK["GX"] + n
                t0, t1 = PARTS[n]
                dve.wait_ge(work_full, k + 1)
                dve.tensor_copy(gT[:, TP * t0:TP * t1], bank_w(k)[0:NX, 0:TP * (t1 - t0)]
                                ).then_inc(work_drained, 1)
            for j in range(NT):
                k = WORK["FB"] + j
                dve.wait_ge(work_full, k + 1)
                dve.tensor_tensor(X[:, j, :], bank_w(k)[0:TP, :], X[:, j, :], ALU.add
                                  ).then_inc(work_drained, 1)
            for j in range(NT):
                k = WORK["DG"] + j
                if j >= 2:
                    dve.wait_ge(work_full, k - 1)
                for v in range(4):
                    ins = dve.tensor_scalar(dg[j % 2][:, v, :], ident[0:TP, 0:TP], gsl[:, j, v:v + 1],
                                            None, ALU.mult)
                ins.then_inc(diag_ready, 1)
                dve.wait_ge(work_full, k + 1)
                dve.tensor_copy(R4[:, :, TP * j:TP * j + TP],
                                bank_w(k)[:, 0:4 * TP].rearrange("p (a n) -> p a n", a=4)
                                ).then_inc(work_drained, 1)
            dve.wait_ge(work_drained, WORK["END"])
            settle()

            loop = sem("item_step")

            def s_first(j):
                return dve.tensor_scalar(s1[:, j, :], siota, gcur[:, j, 0:1], None, ALU.is_equal)

            def s_second(j):
                return dve.scalar_tensor_tensor(S[:, j, :], siota, gcur[:, j, 1:2], s1[:, j, :],
                                                ALU.is_equal, ALU.add)

            dve.wait_ge(iotas, 8)
            for j in range(NT):
                did(s_first(j))
            settle()
            for j in range(NT):
                ins = s_second(j)
            ins.then_inc(s_ready, 1)
            with dve.Fori(0, NI) as i:
                for dk in range(KD):
                    dve.wait_ge(xc_full, i * KD + (dk + 1))
                    dve.wait_ge(xc_hi, i * KD + (dk + 1))
                    minus(XC[:, 1, dk, :], ps[6 + dk % 2][:, 0:SLOTS], XC[:, 0, dk, :], xc_lo)

                def loop_did(ins):
                    ins.then_inc(loop, 1)

                def hidden_low(q):
                    for f in range(2):
                        n = 2 * q + f
                        dve.wait_ge(hd_hi, i * 16 + (n + 1))
                        minus(HD[:, q % 2, 1, f, :], hid[:, q % 2, f, :], HD[:, q % 2, 0, f, :], hd_lo)

                def at(n):
                    dve.wait_ge(loop, i * CHAIN + n)

                hidden_low(0)
                n = 0
                for h in range(2):
                    loop_did(dve.tensor_scalar(stmp, R4[:, 0, :], sid[:, h:h + 1], None, ALU.is_equal))
                    n += 1
                    at(n)
                    loop_did(dve.scalar_tensor_tensor(ST[:, h, :], R4[:, 1, :], sid[:, h:h + 1], stmp,
                                                      ALU.is_equal, ALU.add))
                    n += 1
                    for c in range(2):
                        loop_did(dve.scalar_tensor_tensor(junk, R4[:, c, :], sid[:, h:h + 1],
                                                          R4[:, 2 + c, :], ALU.is_equal, ALU.mult,
                                                          accum_out=gs[:, h, c:c + 1]))
                        n += 1
                        at(n)
                    hidden_low(1 + h)
                dve.tensor_tensor(gsum[:, :], gs[:, :, 0], gs[:, :, 1], ALU.add).then_inc(st_ready, 1)
                loop_did(dve.tensor_scalar(sid[:, :], sid[:, :], float(SLOTS), None, ALU.add))
                n += 1
                hidden_low(3)
                loop_did(dve.tensor_scalar(gcur[:, :, :], gcur[:, :, :], -float(SLOTS), None, ALU.add))
                n += 1
                at(n)
                for j in range(NT):
                    loop_did(s_first(j))
                    n += 1
                hidden_low(4)
                at(n)
                for j in range(NT):
                    ins = s_second(j)
                ins.then_inc(s_ready, 1)
                for q in range(5, 8):
                    hidden_low(q)
                dve.wait_ge(st_ready, i + 1)
                for h in range(2):
                    dve.wait_ge(o_full, i * 2 + (h + 1))
                    dve.tensor_scalar(ysf[:, h, :], ps[h][:, :], gsum[:, h:h + 1], None,
                                      ALU.mult).then_inc(ys_done, 1)
                for h in range(2):
                    dve.wait_ge(ys_hi, i * 2 + (h + 1))
                    minus(YS[:, 1, h, :], ysf[:, h, :], YS[:, 0, h, :], ys_lo)
                for j in range(NT):
                    dve.wait_ge(sc_full, i * NT + (j + 1))
                    dve.tensor_tensor(X[:, j, :], ps[6 + j % 2][0:TP, :], X[:, j, :],
                                      ALU.add).then_inc(sc_added, 1)
                assert n == CHAIN


CHAIN = 15
ORDER = [("h", 0)] + [u for q in range(1, 8) for u in (("h", q), ("o", q - 1))] + [("o", 7)]


def kernel(**inputs):
    import numpy as _np
    import concourse.bacc as _bacc
    from concourse import mybir as _mybir
    from concourse.bass_utils import run_bass_kernel_spmd as _run

    a = {k: _np.asarray(v) for k, v in inputs.items()}

    def unit(m):
        return m.reshape(2, 2, 128, 512).transpose(0, 2, 1, 3).reshape(2, 128, HU)

    def w1_0(g):
        return unit(a["L0_ffn_W1"][g].transpose(1, 0, 2).reshape(D, D))

    def w2_0(g):
        return unit(a["L0_ffn_W2"][g].reshape(D, D))

    units = [unit(a["L0_gnn_W_rel"][r]) for r in range(3)] + [unit(a["L0_gnn_W_self"][t]) for t in range(3)]
    units += [w1_0(0), w1_0(1), w2_0(0), w1_0(2), w2_0(1), w1_0(3), w2_0(2), w2_0(3)]
    units += [unit(a[n].T) for n in ("L1_gnn_W1l", "L1_gnn_W1r", "L1_gnn_W2l", "L1_gnn_W2r")]
    w1 = a["L1_ffn_W1"].reshape(NX, KD, 128, 8, 256).transpose(0, 3, 2, 1, 4).reshape(NX, 8, 128, HU)
    w2 = a["L1_ffn_W2"].reshape(NX, 8, 2, 128, D).transpose(0, 1, 3, 2, 4).reshape(NX, 8, 128, HU)
    wmoe = _np.stack([(w1 if kind == "h" else w2)[:, q] for kind, q in ORDER], 1)
    gate = _np.concatenate([a["L0_ffn_wg_group"], a["L0_ffn_wg_inner"].transpose(1, 0, 2).reshape(D, 32),
                            a["L1_ffn_w_r"].T], 1).reshape(KD, 128, 44).transpose(1, 0, 2)
    rows = [a["L0_gnn_b_rel"], a["L0_gnn_b_self"], a["L0_ffn_ln_g"][None], a["L0_ffn_ln_b"][None],
            a["L0_ffn_gln_g"]]
    rows += [a[n][None] for n in ("L1_gnn_b1l", "L1_gnn_ln1_w", "L1_gnn_ln1_b", "L1_gnn_b2l",
                                  "L1_gnn_ln2_w", "L1_gnn_ln2_b", "L1_ffn_ln_g", "L1_ffn_ln_b")]
    ids = _np.stack([a["src"], a["dst"], a["edge_type_3"]]).reshape(3, ET, TP).transpose(2, 0, 1)
    arrays = {
        "x": a["x"].reshape(NT, TP, D).transpose(1, 0, 2), "ids": ids,
        "ntype": a["node_type_3"].reshape(NT, TP).T, "rows": _np.concatenate(rows),
        "wstat": _np.concatenate(units), "wmoe": wmoe, "gate": gate,
        "b1_0": a["L0_ffn_b1"].reshape(16, 128).T, "b2_0": a["L0_ffn_b2"].reshape(32, D),
        "glnb": a["L0_ffn_gln_b"], "rb": a["L1_ffn_b_r"][None],
        "b1_1": a["L1_ffn_b1"].reshape(NX * 16, 128).T, "b2_1": a["L1_ffn_b2"],
    }
    arrays = {f"in_{k}": _np.ascontiguousarray(v) for k, v in arrays.items()}
    nc = _bacc.Bacc("TRN2", target_bir_lowering=False, num_devices=1)
    args = [nc.dram_tensor(k, v.shape, _mybir.dt.from_np(v.dtype), kind="ExternalInput").ap()
            for k, v in arrays.items()]
    args.append(nc.dram_tensor("out_x", (TP, NT, D), _mybir.dt.float32, kind="ExternalOutput").ap())
    gnn_moe(nc, *args)
    r = _run(nc, [arrays], core_ids=[0])
    return _np.ascontiguousarray(r.results[0]["out_x"].transpose(1, 0, 2).reshape(N, D))
```

```python
from contextlib import ExitStack

import numpy as np

import concourse.bass as bass
from concourse import mybir

F32 = mybir.dt.float32
F32R = mybir.dt.float32r
F16 = mybir.dt.float16
I32 = mybir.dt.int32
U32 = mybir.dt.uint32
U16 = mybir.dt.uint16
ALU = mybir.AluOpType
ACT = mybir.ActivationFunctionType
AX = mybir.AxisListType

N = 625
D = 512
NT, TP = 5, 125
NP2 = N + 1
HALF = [(0, 314), (314, 312)]
KD = D // 128
E = 20000
ET = E // TP
UNR = 4
EG = ET // UNR
NR = 3
CW = NR * TP
SUB = [(0, 63), (63, 62)]
NS = NT * len(SUB)
FLAGS = [(0, 3), (3, 6), (6, 9), (9, 10)]
G0, E0 = 4, 8
NX = 8
DH = 2048
SLOTS = 256
NI = 12
assert NI >= (2 * N + NX * (SLOTS - 1)) // SLOTS
EPS = 1e-5
NEG = -3.0e38
HU = 1024
STATIC = 36
PER_ITEM = 16
RING = 4
PARTS = [(0, 3), (3, 5)]

WORK, ACC = {}, {}
_n = 0
for _name, _uses in [("T0", 8), ("Y", 15), ("FLAG", 4), ("SELF", 15), ("AGG", 5), ("T1", 8), ("LG", 1), ("T2", 8),
                     ("LI", 1), ("GT", 4), ("FF", 64), ("GB", 5), ("T3", 8), ("DEG", 1), ("AG1", 8),
                     ("C1", 5), ("T4", 8), ("AG2", 8), ("C2", 5), ("T5", 8), ("LR", 1), ("POS", 1),
                     ("GX", 2), ("FB", 5), ("DG", 5), ("END", 0)]:
    WORK[_name] = _n
    _n += _uses
_n = 0
for _name, _uses in [("CNT", 25), ("MOE", 20), ("C1", 5), ("C2", 5), ("END", 0)]:
    ACC[_name] = _n
    _n += _uses
LN = {n: i for i, n in enumerate(["x0", "x1", "z", "g0", "g1", "g2", "g3", "x2", "c1", "c2", "x3", "w0"])}

LN_OUT = {n: i for i, n in enumerate([n for n in LN if n[0] != "g"])}


def unit_end(k):
    if k < 3:
        return "work", WORK["Y"] + 5 * (k + 1)
    if k < 6:
        return "work", WORK["SELF"] + 5 * (k - 2)
    if k < 14:
        kind, g = [("h", 0), ("h", 1), ("o", 0), ("h", 2), ("o", 1), ("h", 3), ("o", 2), ("o", 3)][k - 6]
        return ("work", WORK["FF"] + 16 * (g + 1)) if kind == "h" else ("acc", ACC["MOE"] + 5 * (g + 1))
    return [("acc", ACC["C1"] + 5), ("work", WORK["C1"] + 5),
            ("acc", ACC["C2"] + 5), ("work", WORK["C2"] + 5)][k - 14]


def gnn_moe(nc, x_in, ids_in, ntype_in, rows_in, wstat, wmoe, gate_in, b1_0, b2_0, glnb_in,
            rb_in, b1_1, b2_1, out):
    with ExitStack() as ctx:
        def sb(name, shape, dt=F32):
            return ctx.enter_context(nc.sbuf_tensor(name, shape, dt))

        sems = {}

        def sem(name):
            if name not in sems:
                sems[name] = ctx.enter_context(nc.semaphore(name))
            return sems[name]

        X = sb("X", [TP, NT, D])
        U = sb("U", [128, NT, D])
        Z = sb("Z", [128, NT, D])
        HB = sb("HB", [128, NT, D])
        rows = sb("rows", [TP, 6, D])
        raw = sb("raw", [128, RING, HU])
        wsp = sb("wsp", [128, RING, 2, HU], F32R)
        XT = sb("XT", [128, 2, KD, NP2], F32R)
        BIGW = 2 * NR * NT * D + 2 * NT * CW
        BIG = sb("BIG", [128, BIGW], F32R)
        tot = sb("tot", [TP, NT, NP2], U16)
        iota = sb("iota", [TP, 16])
        mk = sb("mk", [128, 128])
        mk64 = sb("mk64", [32, 128])
        kg = sb("kg", [32, 2, G0])
        ident = sb("ident", [128, 128])
        ones = sb("ones", [TP, 128])
        ones_h = sb("ones_h", [TP, 128], F16)
        epst = sb("epst", [TP, 1])
        nti = sb("nti", [TP, NT], I32)
        ntf = sb("ntf", [TP, NT])
        mask = sb("mask", [TP, NR, NT])
        stats = sb("stats", [TP, NT, 6])
        mv = sb("mv", [TP, NT, 2])
        std = sb("std", [TP, NT])
        rs = sb("rs", [TP, NT])
        ga = sb("ga", [TP, NT])
        gc = sb("gc", [TP, NT])
        gw = sb("gw", [128, KD, 44])
        LGT = sb("LGT", [TP, NT, 5, 8])
        v8 = sb("v8", [TP, NT, 5, 8])
        idxf = sb("idxf", [TP, NT, 5, 2])
        p12 = sb("p12", [TP, NT, 5, 2])
        ex = sb("ex", [TP, NT, 5])
        gat = v8
        eqt = LGT
        b1c = sb("b1c", [128, 16])
        b1e = sb("b1e", [128, NX * 16])
        rbt = sb("rbt", [TP, NX])
        rdeg = sb("rdeg", [TP, NT])
        cum = sb("cum", [128, 3, NX])
        one8 = sb("one8", [128, 10])
        i12 = sb("i12", [1, NI])
        itf = sb("itf", [1, NI])
        items = sb("items", [1, 2 * NI + 1], I32)
        spanf = sb("spanf", [1, 4, NS])
        spans = sb("spans", [1, 3, NS], I32)
        stepno = sb("stepno", [1, EG])
        gsl = sb("gsl", [TP, NT, 4])
        gcur = sb("gcur", [TP, NT, 2])
        sid = sb("sid", [128, 2])
        gs = sb("gs", [128, 2, 2])
        gsum = sb("gsum", [128, 2])

        def flat(t):
            return t[:, :, :].rearrange("p a b -> p (a b)")

        def big(p, off, *shape):
            n = int(np.prod(shape))
            names = list("abcde"[:len(shape)])
            pat = f"p ({' '.join(names)}) -> p {' '.join(names)}"
            return BIG[0:p, off:off + n].rearrange(pat, **dict(zip(names, shape)))

        Y = big(TP, 0, 2, NR * NT, D)
        AC = [big(TP, 2 * NR * NT * D, 2, NT, CW),
              XT[0:TP, :, :, :].rearrange("p a b n -> p (a b n)")[:, 0:2 * NT * CW]
              .rearrange("p (a b n) -> p a b n", a=2, b=NT)]
        HT = big(128, 0, 2, 2, KD, NP2)
        o = 4 * KD * NP2
        IW = big(32, o, 2, NP2)
        o += 2 * NP2
        SEL = big(32, o, 16, 128)
        o += 16 * 128
        B2 = big(32, o, 2, G0, D)
        assert o + 2 * G0 * D <= BIGW
        XS = big(TP, 0, 2, NT, D)
        AT = big(TP, 2 * NT * D, 2, NT, NP2)
        AG = big(128, 2 * NT * D + 2 * NT * NP2, 2, KD, NP2)
        o = 2 * NT * D
        XC = big(128, o, 2, KD, SLOTS)
        o += 2 * KD * SLOTS
        S = big(TP, o, NT, SLOTS)
        o += NT * SLOTS
        HD = big(128, o, 2, 2, 2, SLOTS)
        o += 8 * SLOTS
        ST = big(128, o, 2, N)
        o += 2 * N
        YS = big(128, o, 2, 2, D)
        assert o + 4 * D <= BIGW

        zf, uf, hf = flat(Z), flat(U), flat(HB)
        es, ek = zf[0:TP, 0:ET], zf[0:TP, ET:2 * ET]
        iok = zf[0:TP, 320:1260].bitcast(F16)
        ohs = zf[0:TP, 1260:2516].bitcast(F16)[:, 0:UNR * 628].rearrange("p (u n) -> p u n", u=UNR)
        ohk = uf[0:TP, 0:752].bitcast(F16).rearrange("p (u n) -> p u n", u=UNR)
        zero = uf[0:TP, 752:752 + 188].bitcast(F16)
        etype = zf[0:TP, 1260:1260 + ET]
        in_half = zf[0:TP, 1420:1420 + NS * ET // 2].bitcast(F16).rearrange("p (c n) -> p c n", c=NS)
        above = [zf[0:TP, 2220 + ET * i:2220 + ET * i + ET] for i in range(2)]
        ytmp = [uf[0:TP, 1024 + D * i:1536 + D * i] for i in range(3)]
        ids = hf[0:TP, 0:3 * ET].bitcast(I32).rearrange("p (a n) -> p a n", a=3)
        f1 = [uf[:, 314 * i:314 * i + 314] for i in range(2)]
        f2 = [uf[:, 314 * (i + 2):314 * (i + 2) + 314] for i in range(2)]
        gT = uf[0:8, 1256:1256 + NP2]
        bT = uf[0:8, 1882:1882 + D]
        i8 = hf[0:TP, 2000:2200].bitcast(U32).rearrange("p (a b n) -> p a b n", a=NT, b=5)
        b2f = hf[0:32, 0:D]
        b2m = hf[0:32, D:2 * D]
        R4 = uf[:, 0:4 * N].rearrange("p (a n) -> p a n", a=4)
        dg = [hf[0:TP, 500 * i:500 * i + 500].rearrange("p (a n) -> p a n", a=4) for i in range(2)]
        gsb = hf[0:TP, 1040:1080].rearrange("p (a n) -> p a n", a=NT)
        eq1 = hf[0:TP, 1080:1120].rearrange("p (a n) -> p a n", a=NT)
        cbase = hf[0:128, 1120:1128]
        marked = uf[0:1, 0:800].rearrange("p (a c n) -> p a c n", a=2, c=NS)
        present = uf[0:1, 1024:1424].rearrange("p (c n) -> p c n", c=NS)
        ele, ele2 = [hf[0:1, 1400 + NI * NX * i:1400 + NI * NX * (i + 1)].rearrange("p (a n) -> p a n", a=NI)
                     for i in range(2)]
        ends2 = hf[0:1, 1630:1630 + NI]
        ends, lims = hf[0:1, 1600:1600 + NX], hf[0:1, 1610:1610 + NI]
        gsv = hf[0:TP, 1130:1170].rearrange("p (a n) -> p a n", a=NT)
        tri = hf[0:TP, 1200:1263].bitcast(F16)[:, 0:TP]
        sel16 = hf[0:TP, 1270:1290].bitcast(F16).rearrange("p (a n) -> p a n", a=NT)
        stmp, junk = hf[:, 0:N], hf[:, N:2 * N]
        s1 = hf[0:TP, 1250:1250 + NT * SLOTS].rearrange("p (a n) -> p a n", a=NT)
        hid = zf[:, 0:1024].rearrange("p (b c s) -> p b c s", b=2, c=2)
        ysf = zf[:, 1024:2048].rearrange("p (a n) -> p a n", a=2)
        siota = rows[:, 5, 0:SLOTS]

        ps = [ctx.enter_context(nc.psum_tensor(f"bank{i}", [128, 512], F32)) for i in range(8)]

        x_in_s, ids_in_s, small_in = sem("x_landed"), sem("ids_landed"), sem("small_landed")
        rows_in_s = [sem(f"rows_landed{i}") for i in range(4)]
        bt_in = [sem(f"bias_rows_landed{i}") for i in range(2)]
        b2_in = sem("b2_landed")
        raw_in = [sem(f"raw_landed{i}") for i in range(RING)]
        weight_hi, weight_lo = sem("weight_hi"), sem("weight_lo")
        work_full, work_drained = sem("work_full"), sem("work_drained")
        acc_full, acc_drained = sem("acc_full"), sem("acc_drained")
        iotas, step = sem("iotas_made"), sem("vector_step")
        ln_std, ln_mom, ln_out = sem("ln_std"), sem("ln_moments"), sem("ln_out")
        xt_hi, y_hi, y_lo = sem("xt_hi"), sem("y_hi"), sem("y_lo")
        oh_ready, oh_used = sem("onehot_ready"), sem("onehot_used")
        ac_hi, ag_hi = sem("ac_hi"), sem("ag_hi")
        ex_in, ex_out = sem("exp_in"), sem("exp_out")
        gates_ready, gt_hi = sem("gates_ready"), sem("gates_t_hi")
        relu_done, f2_done, ht_hi, ht_lo = sem("relu_done"), sem("gated"), sem("ht_hi"), sem("ht_lo")
        xs_src, xs_hi, xs_lo = sem("xs_source"), sem("xs_hi"), sem("xs_lo")
        at_hi, at_lo = sem("at_hi"), sem("at_lo")
        flags_ready, spans_ready = sem("chunk_flags_ready"), sem("spans_ready")
        zeros_ready = sem("zeros_ready")
        consts_ready, x1_done, z_done = sem("constants_ready"), sem("x1_done"), sem("z_done")
        rows_free = sem("rows_free")
        sel_ready, diag_ready, items_ready = sem("sel_ready"), sem("diag_ready"), sem("items_ready")
        route_ready, s_ready, st_ready = sem("route_ready"), sem("s_ready"), sem("st_ready")
        xc_full, xc_hi, xc_lo = sem("xc_full"), sem("xc_hi"), sem("xc_lo")
        h_full, hid_done, hd_hi, hd_lo = sem("h_full"), sem("hid_done"), sem("hd_hi"), sem("hd_lo")
        w2_used, o_full, ys_done, ys_hi, ys_lo = (sem("w2_used"), sem("o_full"), sem("ys_done"),
                                                  sem("ys_hi"), sem("ys_lo"))
        sc_full, sc_added = sem("scattered"), sem("scatter_added")
        out_done = sem("out_landed")

        block = ctx.enter_context(nc.Block())

        def bank_w(k):
            return ps[5 + k % 3]

        @block.sync
        def _(sp):
            sp.dma_start(X[:, :, :], x_in).then_inc(x_in_s, 16)
            sp.dma_start(ids, ids_in).then_inc(ids_in_s, 16)
            for n in range(STATIC):
                if n >= RING:
                    sp.wait_ge(weight_lo, n - RING + 1)
                sp.dma_start(raw[:, n % RING, :], wstat[n]).then_inc(raw_in[n % RING], 16)
            sp.wait_ge(items_ready, 1)
            n_items = sp.value_load(items[0:1, NI:NI + 1], min_val=1, max_val=NI)
            with sp.Fori(0, n_items) as i:
                e = sp.value_load(items[0:1, bass.ds(i, 1)], min_val=0, max_val=NX - 1)
                for k in range(PER_ITEM):
                    sp.wait_ge(weight_lo, i * PER_ITEM + (STATIC + k - RING + 1))
                    sp.dma_start(raw[:, k % RING, :],
                                 wmoe[bass.ds(e, 1), k].rearrange("a p n -> (a p) n")
                                 ).then_inc(raw_in[k % RING], 16)
            for k in range(RING):
                sp.wait_ge(weight_lo, n_items * PER_ITEM + (STATIC + k - RING + 1))
                sp.dma_start(raw[:, k, :], wmoe[0, k]).then_inc(raw_in[k], 16)
            sp.wait_ge(sc_added, n_items * NT + NT)
            sp.dma_start(out, X[:, :, :]).then_inc(out_done, 16)
            sp.wait_ge(out_done, 16)

        @block.gpsimd
        def _(pool):
            def io(o_, pattern, mul):
                pool.iota(o_, pattern, base=0, channel_multiplier=mul,
                          allow_small_or_imprecise_dtypes=True).then_inc(iotas, 1)

            io(mk[:, :], [[1, 128]], -1)
            io(iota[:, :], [[1, 16]], 0)
            io(mk64[:, :], [[1, 2], [0, 64]], -1)
            io(kg[:, 0, :], [[-8, G0]], 1)
            io(iok, [[1, 1880]], 0)
            io(i12[:, :], [[1, NI]], 0)
            io(sid[:, :], [[128, 2]], 1)
            pool.iota(stepno[:, :], [[1, EG]], base=1, channel_multiplier=0,
                      allow_small_or_imprecise_dtypes=True).then_inc(iotas, 1)

            def lo(slot):
                pool.tensor_tensor(wsp[:, slot, 1, :], raw[:, slot, :],
                                   wsp[:, slot, 0, :].bitcast(F32), ALU.subtract).then_inc(weight_lo, 1)

            for n in range(STATIC):
                pool.wait_ge(weight_hi, n + 1)
                lo(n % RING)
            pool.wait_ge(rows_free, 4)
            io(siota, [[1, SLOTS]], 0)
            pool.wait_ge(items_ready, 1)
            n_items = pool.value_load(items[0:1, NI:NI + 1], min_val=1, max_val=NI)
            with pool.Fori(0, n_items) as i:
                for k in range(PER_ITEM):
                    pool.wait_ge(weight_hi, i * PER_ITEM + (STATIC + k + 1))
                    lo(k % RING)

        @block.scalar
        def _(act):
            def rows_load(dst0, src0, n, sem_):
                for r in range(n):
                    act.dma_start(rows[:, dst0 + r, :],
                                  rows_in[src0 + r:src0 + r + 1, :].partition_broadcast(TP)
                                  .rearrange("p a n -> p (a n)")).then_inc(sem_, 16)

            act.dma_start(gw[:, :, :], gate_in).then_inc(small_in, 16)
            act.dma_start(nti[:, :], ntype_in).then_inc(small_in, 16)
            act.dma_start(b1c[:, :], b1_0).then_inc(small_in, 16)
            act.dma_start(b1e[:, :], b1_1).then_inc(small_in, 16)
            act.dma_start(rbt[:, :], rb_in.partition_broadcast(TP).rearrange("p a n -> p (a n)")
                          ).then_inc(small_in, 16)
            rows_load(0, 0, 6, rows_in_s[0])

            def copy(dst, src, sem_):
                act.activation(dst, src, ACT.Copy).then_inc(sem_, 1)

            def hi_unit(k):
                if k >= STATIC // 2:
                    return
                for n in (2 * k, 2 * k + 1):
                    act.wait_ge(raw_in[n % RING], 16 * (n // RING + 1))
                    if k >= 2:
                        kind, v = unit_end(k - 2)
                        act.wait_ge(work_full if kind == "work" else acc_full, v)
                    copy(wsp[:, n % RING, 0, :], raw[:, n % RING, :], weight_hi)

            def norm(name):
                act.wait_ge(ln_mom, LN[name] + 1)
                act.activation(std[:, :], mv[:, :, 1], ACT.Sqrt, bias=epst[:, 0:1]).then_inc(ln_std, 1)

            def transposed(name):
                k = WORK[name]
                for dk in range(KD):
                    for a, b in PARTS:
                        act.wait_ge(work_full, k + 1)
                        copy(XT[:, 0, dk, TP * a:TP * b], bank_w(k)[:, 0:TP * (b - a)], xt_hi)
                        k += 1

            def split_rows(s):
                for j in range(NT):
                    act.wait_ge(xs_src, NT * s + j + 1)
                    copy(XS[:, 0, j, :], (U, U, Z)[s][0:TP, j, :], xs_hi)

            def aggregated(name, s):
                k = WORK[name]
                for dk in range(KD):
                    for c0, w in HALF:
                        act.wait_ge(work_full, k + 1)
                        copy(AG[:, 0, dk, c0:c0 + w], bank_w(k)[:, 0:w], ag_hi)
                        k += 1

            def gate_exp(s):
                act.wait_ge(ex_in, s + 1)
                act.activation(ex[:, :, :], ex[:, :, :], ACT.Exp).then_inc(ex_out, 1)

            hi_unit(0)
            hi_unit(1)
            act.wait_ge(consts_ready, 1)
            norm("x0")
            transposed("T0")
            for r in range(NR):
                for j in range(NT):
                    act.wait_ge(work_drained, WORK["Y"] + NT * r + j + 1)
                    copy(Y[:, 0, NT * r + j, :], ytmp[(NT * r + j) % 3], y_hi)
                hi_unit(r + 2)
            for t in range(NR):
                hi_unit(t + 5)
            for c in range(NT):
                for j in range(NT):
                    act.wait_ge(acc_full, NT * c + j + 1)
                    copy(AC[c % 2][:, 0, j, :], ps[j][0:TP, 0:CW], ac_hi)
            act.wait_ge(rows_free, 1)
            rows_load(0, 6, 6, rows_in_s[1])
            act.dma_start(b2f, b2_0).then_inc(b2_in, 16)
            norm("x1")
            transposed("T1")
            norm("z")
            transposed("T2")
            act.wait_ge(z_done, 1)
            act.dma_start(bT[0:G0, :], glnb_in).then_inc(bt_in[0], 16)
            gate_exp(0)
            for k in range(2):
                act.wait_ge(work_full, WORK["GT"] + k + 1)
                a, b = PARTS[k]
                copy(IW[:, 0, TP * a:TP * b], bank_w(WORK["GT"] + k)[0:32, 0:TP * (b - a)], gt_hi)

            def hidden(g):
                for s in range(8):
                    cc, (c0, w) = s // 2, HALF[s % 2]
                    k = WORK["FF"] + 16 * g + 2 * s
                    q = 8 * g + s
                    act.wait_ge(work_full, k + 1)
                    if q >= 2:
                        act.wait_ge(f2_done, q - 1)
                    act.activation(f1[q % 2][:, 0:w], bank_w(k)[:, 0:w], ACT.Relu,
                                   bias=b1c[:, 4 * g + cc:4 * g + cc + 1]).then_inc(relu_done, 1)
                    act.wait_ge(f2_done, q + 1)
                    copy(HT[:, g % 2, 0, cc, c0:c0 + w], f2[q % 2][:, 0:w], ht_hi)

            hidden(0)
            hi_unit(8)
            hidden(1)
            hi_unit(9)
            norm("g0")
            hi_unit(10)
            hidden(2)
            hi_unit(11)
            norm("g1")
            hi_unit(12)
            hidden(3)
            hi_unit(13)
            norm("g2")
            hi_unit(14)
            norm("g3")
            hi_unit(15)
            act.wait_ge(rows_free, 2)
            rows_load(0, 12, 6, rows_in_s[2])
            norm("x2")
            for j in range(NT):
                act.wait_ge(work_full, WORK["GB"] + 5)
                act.wait_ge(xs_src, j + 1)
                copy(XS[:, 0, j, :], U[0:TP, j, :], xs_hi)
                copy(AT[:, 0, j, :], tot[:, j, :], at_hi)
            transposed("T3")
            aggregated("AG1", 0)
            hi_unit(16)
            hi_unit(17)
            norm("c1")
            split_rows(1)
            transposed("T4")
            aggregated("AG2", 1)
            norm("c2")
            act.wait_ge(rows_free, 3)
            rows_load(0, 18, 2, rows_in_s[3])
            norm("x3")
            norm("w0")
            split_rows(2)
            transposed("T5")
            act.wait_ge(z_done, 2)
            act.dma_start(bT, b2_1).then_inc(bt_in[1], 16)
            gate_exp(1)
            act.wait_ge(items_ready, 1)
            act.wait_ge(work_drained, WORK["END"])
            def hi_item(i, k):
                act.wait_ge(raw_in[k % RING], i * (16 * PER_ITEM // RING)
                            + 16 * ((STATIC + k) // RING + 1))
                used(i, k - RING)
                copy(wsp[:, k % RING, 0, :], raw[:, k % RING, :], weight_hi)

            def used(i, k):
                kind, q = ORDER[k % PER_ITEM]
                d = k // PER_ITEM
                if kind == "h":
                    act.wait_ge(h_full, i * 16 + (16 * d + 2 * q + 2))
                elif q < 7:
                    act.wait_ge(w2_used, i * 7 + (7 * d + q + 1))
                else:
                    act.wait_ge(o_full, i * 2 + (2 * d + 2))

            def gathered(done):
                for dk in range(KD):
                    act.wait_ge(xc_full, done + (dk + 1))
                    copy(XC[:, 0, dk, :], ps[6 + dk % 2][:, 0:SLOTS], xc_hi)

            gathered(0)
            for n in range(RING):
                act.wait_ge(raw_in[n], 16 * ((STATIC + n) // RING + 1))
                copy(wsp[:, n, 0, :], raw[:, n, :], weight_hi)
            n_items = act.value_load(items[0:1, NI:NI + 1], min_val=1, max_val=NI)
            with act.Fori(0, n_items) as i:
                e = act.value_load(items[0:1, bass.ds(i, 1)], min_val=0, max_val=NX - 1)
                for m, (kind, q) in enumerate(ORDER):
                    if kind == "h":
                        for f in range(2):
                            n = 2 * q + f
                            act.wait_ge(h_full, i * 16 + (n + 1))
                            if n >= 4:
                                act.wait_ge(hd_lo, i * 16 + (n - 3))
                            act.activation(hid[:, q % 2, f, :], ps[2 + n % 4][:, 0:SLOTS], ACT.Gelu,
                                           bias=b1e[:, bass.ds(e * 16 + n, 1)]).then_inc(hid_done, 1)
                            act.wait_ge(hid_done, i * 16 + (n + 1))
                            copy(HD[:, q % 2, 0, f, :], hid[:, q % 2, f, :], hd_hi)
                    if (kind, q) == ("h", 7):
                        gathered(i * KD + KD)
                    if m >= 1:
                        hi_item(i, m - 1 + RING)
                for h in range(2):
                    act.wait_ge(ys_done, i * 2 + (h + 1))
                    copy(YS[:, 0, h, :], ysf[:, h, :], ys_hi)
                hi_item(i, PER_ITEM + RING - 1)

        @block.tensor
        def _(pe):
            w = [0]
            a = [0]

            def work():
                k = w[0]
                if k >= 3:
                    pe.wait_ge(work_drained, k - 2)
                w[0] += 1
                return bank_w(k)

            def acc(j):
                if a[0] >= NT:
                    pe.wait_ge(acc_drained, a[0] - NT + 1)
                a[0] += 1
                return ps[j]

            def three(o_, terms, start, stop):
                last = None
                for n, (lh, ll, rh, rl) in enumerate(terms):
                    for m, (l, r) in enumerate([(lh, rh), (lh, rl), (ll, rh)]):
                        last = pe.matmul(o_, l, r, start=start and n == 0 and m == 0,
                                         stop=stop and n == len(terms) - 1 and m == 2)
                return last

            def weights(k):
                pe.wait_ge(weight_lo, 2 * k + 2)

            def wpart(k, kc, part, c0=0, cw=D):
                return wsp[:, (2 * k) % RING + kc // 2, part, (kc % 2) * D + c0:(kc % 2) * D + c0 + cw]

            def transpose(name, src):
                assert w[0] == WORK[name]
                for dk in range(KD):
                    for t0, t1 in PARTS:
                        b = work()
                        for j in range(t0, t1):
                            last = pe.transpose(b[:, TP * (j - t0):TP * (j - t0 + 1)],
                                                src[0:TP, j, 128 * dk:128 * dk + 128], ident[0:TP, 0:TP])
                        last.then_inc(work_full, 1)

            def rows_by(o_, src, j, k):
                return three(o_, [(src[:, 0, kc, TP * j:TP * j + TP], src[:, 1, kc, TP * j:TP * j + TP],
                                   wpart(k, kc, 0), wpart(k, kc, 1)) for kc in range(KD)], True, True)

            def small(name, c0, n, stride):
                assert w[0] == WORK[name]
                b = work()
                for j in range(NT):
                    for kc in range(KD):
                        for part in range(2):
                            last = pe.matmul(b[0:TP, stride * j:stride * j + n],
                                             XT[:, part, kc, TP * j:TP * j + TP].bitcast(F32),
                                             gw[:, kc, c0:c0 + n], start=kc == 0 and part == 0,
                                             stop=kc == KD - 1 and part == 1)
                last.then_inc(work_full, 1)

            pe.nop().then_inc(oh_used, UNR + ET)
            pe.wait_ge(consts_ready, 1)
            pe.wait_ge(ln_out, NT)
            transpose("T0", U)
            pe.wait_ge(work_drained, WORK["Y"])
            for r in range(NR):
                weights(r)
                for j in range(NT):
                    rows_by(work()[0:TP, :], XT, j, r).then_inc(work_full, 1)
            pe.wait_ge(flags_ready, 1)
            for c0, c1 in FLAGS:
                pe.matmul(work()[:, 0:(c1 - c0) * ET], ones_h[:, :],
                          in_half[:, c0:c1, :].rearrange("p c n -> p (c n)"),
                          start=True, stop=True).then_inc(work_full, 1)
            for t in range(NR):
                weights(NR + t)
                for j in range(NT):
                    rows_by(work()[0:TP, :], XT, j, NR + t).then_inc(work_full, 1)
            pe.wait_ge(spans_ready, 1)
            pe.wait_ge(zeros_ready, 1)

            def messages(c):
                if c == 0:
                    pe.wait_ge(y_lo, NR * NT)
                pe.wait_ge(acc_drained, NT * (c + 1))
                three(work()[0:TP, :],
                      [(AC[c % 2][:, 0, j, TP * r:TP * r + TP], AC[c % 2][:, 1, j, TP * r:TP * r + TP],
                        Y[:, 0, NT * r + j, :], Y[:, 1, NT * r + j, :])
                       for r in range(NR) for j in range(NT)], True, True).then_inc(work_full, 1)

            for c in range(NT):
                for j in range(NT):
                    acc(j)
                    pe.matmul(ps[j][0:TP, 0:CW], zero[:, 0:TP], zero[:, 0:CW], start=True, stop=False)
                for h, (d0, dw) in enumerate(SUB):
                    n = 2 * c + h
                    first = pe.value_load(spans[0:1, 0, n:n + 1], min_val=0, max_val=EG - 1)
                    end = pe.value_load(spans[0:1, 1, n:n + 1], min_val=1, max_val=EG)
                    before = pe.value_load(spans[0:1, 2, n:n + 1], min_val=UNR, max_val=NS * ET)
                    with pe.Fori(first, end) as it:
                        for u in range(UNR):
                            pe.wait_ge(oh_ready, before + it * UNR + (u + 1))
                            for j in range(NT):
                                last = pe.matmul(
                                    ps[j][0:TP, 0:CW].rearrange("p (r n) -> p r n", r=NR)[:, :, d0:d0 + dw],
                                    ohs[:, u, TP * j:TP * j + TP],
                                    ohk[:, u, 0:NR * dw].rearrange("p (r n) -> p r n", r=NR),
                                    start=False, stop=False)
                            last.then_inc(oh_used, 1)
                for j in range(NT):
                    pe.matmul(ps[j][0:TP, 0:CW], zero[:, 0:TP], zero[:, 0:CW],
                              start=False, stop=True).then_inc(acc_full, 1)
                if c >= 1:
                    messages(c - 1)
            messages(NT - 1)
            pe.wait_ge(ln_out, NT * (LN_OUT["x1"] + 1))
            transpose("T1", U)
            pe.wait_ge(work_drained, WORK["LG"])
            small("LG", 0, 4, 8)
            pe.wait_ge(z_done, 1)
            transpose("T2", Z)
            pe.wait_ge(work_drained, WORK["LI"])
            small("LI", 4, 32, 32)
            pe.wait_ge(gates_ready, 1)
            for width, sl in ((32, None), (G0, 4)):
                for t0, t1 in PARTS:
                    b = work()
                    for j in range(t0, t1):
                        src = (gat[:, j, 0:4, :].rearrange("p a b -> p (a b)") if sl is None
                               else gat[:, j, 4, 0:G0])
                        last = pe.transpose(b[0:width, TP * (j - t0):TP * (j - t0 + 1)], src,
                                            ident[0:TP, 0:TP])
                    last.then_inc(work_full, 1)
            pe.wait_ge(work_drained, WORK["FF"])

            def hidden(g, k):
                weights(k)
                for cc in range(KD):
                    for c0, cw in HALF:
                        b = work()
                        three(b[:, 0:cw], [(wpart(k, kc, 0, 128 * cc, 128), wpart(k, kc, 1, 128 * cc, 128),
                                            XT[:, 0, kc, c0:c0 + cw], XT[:, 1, kc, c0:c0 + cw])
                                           for kc in range(KD)], True, True).then_inc(work_full, 1)
                        b = work()
                        pe.matmul(b[:, 0:cw], SEL[:, 4 * g + cc, :], IW[:, 0, c0:c0 + cw],
                                  start=True, stop=False)
                        pe.matmul(b[:, 0:cw], SEL[:, 4 * g + cc, :], IW[:, 1, c0:c0 + cw],
                                  start=False, stop=True).then_inc(work_full, 1)

            def second(g, k):
                weights(k)
                pe.wait_ge(ht_lo, 8 * (g + 1))
                for j in range(NT):
                    sl = slice(TP * j, TP * j + TP)
                    b = acc(j)[0:TP, :]
                    three(b, [(HT[:, g % 2, 0, cc, sl], HT[:, g % 2, 1, cc, sl], wpart(k, cc, 0),
                               wpart(k, cc, 1)) for cc in range(KD)], True, False)
                    three(b, [(IW[:, 0, sl], IW[:, 1, sl], B2[:, 0, g, :], B2[:, 1, g, :])],
                          False, True).then_inc(acc_full, 1)

            hidden(0, 6)
            hidden(1, 7)
            second(0, 8)
            hidden(2, 9)
            second(1, 10)
            hidden(3, 11)
            second(2, 12)
            second(3, 13)
            pe.wait_ge(bt_in[0], 16)
            for j in range(NT):
                pe.matmul(work()[0:TP, :], gT[0:G0, TP * j:TP * j + TP], bT[0:G0, :], start=True,
                          stop=True).then_inc(work_full, 1)
            pe.wait_ge(ln_out, NT * (LN_OUT["x2"] + 1))
            transpose("T3", U)
            pe.wait_ge(at_lo, NT)
            b = work()
            for i in range(NT):
                terms = [(part, j) for part in range(2) for j in range(NT)]
                for n, (part, j) in enumerate(terms):
                    last = pe.matmul(b[0:TP, i:i + 1], AT[:, part, j, TP * i:TP * i + TP].bitcast(F32),
                                     ones[:, 0:1], start=n == 0, stop=n == len(terms) - 1)
            last.then_inc(work_full, 1)

            def conv(s, k):
                pe.wait_ge(xs_lo, NT * (s + 1))
                for dk in range(KD):
                    for c0, cw in HALF:
                        three(work()[:, 0:cw],
                              [(XS[:, 0, j, 128 * dk:128 * dk + 128], XS[:, 1, j, 128 * dk:128 * dk + 128],
                                AT[:, 0, j, c0:c0 + cw], AT[:, 1, j, c0:c0 + cw])
                               for j in range(NT)], True, True).then_inc(work_full, 1)
                pe.wait_ge(work_drained, WORK[("AG1", "AG2")[s]] + 8)
                weights(k)
                for j in range(NT):
                    rows_by(acc(j)[0:TP, :], AG, j, k).then_inc(acc_full, 1)
                weights(k + 1)
                for j in range(NT):
                    rows_by(work()[0:TP, :], XT, j, k + 1).then_inc(work_full, 1)

            conv(0, 14)
            pe.wait_ge(xs_src, 2 * NT)
            transpose("T4", U)
            conv(1, 16)
            pe.wait_ge(xs_src, 3 * NT)
            transpose("T5", Z)
            pe.wait_ge(work_drained, WORK["LR"])
            small("LR", 36, NX, 8)
            pe.wait_ge(sel_ready, 1)
            b = work()
            for i in range(NT):
                for j in range(i + 1):
                    pe.matmul(b[0:TP, 8 * i:8 * i + 8], tri if j == i else ones_h[:, 0:TP], sel16[:, j, :],
                              start=j == 0, stop=j == i)
            for j in range(NT):
                last = pe.matmul(b[:, 64:72], ones_h[:, :], sel16[:, j, :], start=j == 0, stop=j == NT - 1)
            last.then_inc(work_full, 1)
            for t0, t1 in PARTS:
                b = work()
                for j in range(t0, t1):
                    last = pe.transpose(b[0:NX, TP * (j - t0):TP * (j - t0 + 1)], gat[:, j, 0, :],
                                        ident[0:TP, 0:TP])
                last.then_inc(work_full, 1)
            pe.wait_ge(bt_in[1], 16)
            pe.wait_ge(work_drained, WORK["FB"])
            for j in range(NT):
                pe.matmul(work()[0:TP, :], gT[:, TP * j:TP * j + TP], bT, start=True,
                          stop=True).then_inc(work_full, 1)
            for j in range(NT):
                pe.wait_ge(diag_ready, j + 1)
                pe.matmul(work()[:, 0:4 * TP], ones[:, :], dg[j % 2].rearrange("p a n -> p (a n)"),
                          start=True, stop=True).then_inc(work_full, 1)
            assert w[0] == WORK["END"] and a[0] == ACC["END"]
            pe.wait_ge(work_drained, WORK["END"])
            pe.wait_ge(acc_drained, ACC["END"])
            n_items = pe.value_load(items[0:1, NI:NI + 1], min_val=1, max_val=NI)

            def gather(i):
                pe.wait_ge(s_ready, i + 2)
                for dk in range(KD):
                    if dk >= 2:
                        pe.wait_ge(xc_lo, i * KD + (KD + dk - 1))
                    elif not isinstance(i, int):
                        pe.wait_ge(sc_added, i * NT + NT)
                    for j in range(NT):
                        for part in range(2):
                            last = pe.matmul(ps[6 + dk % 2][:, 0:SLOTS],
                                             XS[:, part, j, 128 * dk:128 * dk + 128], S[:, j, :],
                                             start=j == 0 and part == 0, stop=j == NT - 1 and part == 1)
                    last.then_inc(xc_full, 1)

            def scatter(i):
                pe.wait_ge(st_ready, i + 1)
                pe.wait_ge(ys_lo, i * 2 + 2)
                for j in range(NT):
                    if j >= 2:
                        pe.wait_ge(sc_added, i * NT + (j - 1))
                    for h in range(2):
                        for part in range(2):
                            last = pe.matmul(ps[6 + j % 2][0:TP, :], ST[:, h, TP * j:TP * j + TP],
                                             YS[:, part, h, :], start=h == 0 and part == 0,
                                             stop=h == 1 and part == 1)
                    last.then_inc(sc_full, 1)

            def item(i, tiles):
                pe.wait_ge(xc_lo, i * KD + KD)
                for m, (kind, q) in enumerate(ORDER):
                    pe.wait_ge(weight_lo, i * PER_ITEM + (STATIC + m + 1))
                    wh = wsp[:, m % RING, 0, :].rearrange("p (a n) -> p a n", a=KD if kind == "h" else 2)
                    wl = wsp[:, m % RING, 1, :].rearrange("p (a n) -> p a n", a=KD if kind == "h" else 2)
                    if kind == "h":
                        for f in range(2):
                            n = 2 * q + f
                            if n >= 4:
                                pe.wait_ge(hid_done, i * 16 + (n - 3))
                            three(ps[2 + n % 4][:, 0:SLOTS],
                                  [(wh[:, kc, 128 * f:128 * f + 128], wl[:, kc, 128 * f:128 * f + 128],
                                    XC[:, 0, kc, :], XC[:, 1, kc, :]) for kc in range(KD)],
                                  True, True).then_inc(h_full, 1)
                        if q == 1:
                            scatter(i)
                        if q == 7:
                            gather(i)
                    else:
                        pe.wait_ge(hd_lo, i * 16 + (2 * q + 2))
                        for h in range(tiles):
                            hs = slice(128 * h, 128 * h + 128)
                            last = three(ps[h][:, :],
                                         [(HD[:, q % 2, 0, f, hs], HD[:, q % 2, 1, f, hs],
                                           wh[:, f, :], wl[:, f, :]) for f in range(2)], q == 0, q == 7)
                            if q == 7:
                                last.then_inc(o_full, 2 // tiles)
                        if q < 7:
                            last.then_inc(w2_used, 1)

            gather(-1)
            with pe.Fori(0, n_items) as i:
                wide = pe.value_load(items[0:1, bass.ds(i + (NI + 1), 1)], min_val=0, max_val=1)
                with pe.If(wide > 0):
                    item(i, 2)
                with pe.Else():
                    item(i, 1)
            scatter(n_items)

        @block.vector
        def _(dve):
            steps = [0]

            def did(ins):
                ins.then_inc(step, 1)
                steps[0] += 1

            def settle():
                dve.wait_ge(step, steps[0])

            def minus(dst, src, hi, sem_=None):
                ins = dve.tensor_tensor(dst, src, hi.bitcast(F32), ALU.subtract)
                if sem_ is None:
                    did(ins)
                else:
                    ins.then_inc(sem_, 1)

            def moments(name, src):
                for j in range(NT):
                    did(dve.bn_stats(stats[:, j, :], src[0:TP, j, :]))
                settle()
                for j in range(NT):
                    ins = dve.bn_aggr(mv[:, j, :], stats[:, j, :])
                    if j < NT - 1:
                        did(ins)
                ins.then_inc(ln_mom, 1)
                dve.wait_ge(ln_std, LN[name] + 1)
                did(dve.reciprocal(rs[:, :], std[:, :]))
                settle()

            def norm(name, src, dst):
                moments(name, src)
                for j in range(NT):
                    dve.tensor_scalar(dst[0:TP, j, :], src[0:TP, j, :], mv[:, j, 0:1], rs[:, j:j + 1],
                                      ALU.subtract, ALU.mult).then_inc(ln_out, 1)
                dve.wait_ge(ln_out, NT * (LN_OUT[name] + 1))

            xt_n = [0]

            def transposed(name):
                k = WORK[name]
                for dk in range(KD):
                    for t0, t1 in PARTS:
                        xt_n[0] += 1
                        dve.wait_ge(work_full, k + 1)
                        dve.wait_ge(xt_hi, xt_n[0])
                        sl = slice(TP * t0, TP * t1)
                        minus(XT[:, 1, dk, sl], bank_w(k)[:, 0:TP * (t1 - t0)], XT[:, 0, dk, sl],
                              work_drained)
                        k += 1

            def gates(n, s):
                settle()
                for j in range(NT):
                    for p in range(n):
                        did(dve.max(v8[:, j, p, :], LGT[:, j, p, :]))
                settle()
                for j in range(NT):
                    for p in range(n):
                        did(dve.max_index(i8[:, j, p, :], v8[:, j, p, :], LGT[:, j, p, :]))
                if n < 5:
                    did(dve.memset(ex[:, :, :], 0.0))
                    settle()
                dve.tensor_tensor(ex[:, :, 0:n], v8[:, :, 0:n, 1], v8[:, :, 0:n, 0],
                                  ALU.subtract).then_inc(ex_in, 1)
                settle()
                did(dve.tensor_copy(idxf[:, :, 0:n, :], i8[:, :, 0:n, 0:2]))
                dve.wait_ge(ex_out, s + 1)
                did(dve.tensor_scalar(p12[:, :, 0:n, 1], ex[:, :, 0:n], 1.0, None, ALU.add))
                settle()
                did(dve.reciprocal(p12[:, :, 0:n, 0], p12[:, :, 0:n, 1]))
                settle()
                did(dve.tensor_tensor(p12[:, :, 0:n, 1], ex[:, :, 0:n], p12[:, :, 0:n, 0], ALU.mult))
                for c, (o_, last) in enumerate(((gat, False), (eqt, True))):
                    shape = [TP, NT, n, 8]
                    it = iota[:, 0:8].unsqueeze(1).unsqueeze(1).to_broadcast(shape)
                    settle()
                    did(dve.tensor_tensor(o_[:, :, 0:n, :], it,
                                          idxf[:, :, 0:n, c:c + 1].to_broadcast(shape), ALU.is_equal))
                    settle()
                    did(dve.tensor_tensor(o_[:, :, 0:n, :], o_[:, :, 0:n, :],
                                          p12[:, :, 0:n, c:c + 1].to_broadcast(shape), ALU.mult))
                settle()
                did(dve.tensor_tensor(gat[:, :, 0:n, :], gat[:, :, 0:n, :], eqt[:, :, 0:n, :], ALU.add))
                settle()

            dve.nop().then_inc(oh_ready, ET)
            dve.wait_ge(iotas, 8)
            did(dve.tensor_scalar(ident[:, :], mk[:, :], 0.0, None, ALU.is_equal))
            did(dve.memset(ones[:, :], 1.0))
            did(dve.memset(one8[:, :], 1.0))
            did(dve.memset(ones_h[:, :], 1.0))
            did(dve.memset(epst[:, :], EPS))
            did(dve.memset(tot[:, :, N:NP2], 0))
            did(dve.memset(LGT[:, :, 4, 4:8], NEG))
            dve.wait_ge(ids_in_s, 16)
            did(dve.tensor_copy(es, ids[:, 0, :]))
            did(dve.tensor_copy(ek, ids[:, 1, :]))
            did(dve.tensor_copy(etype, ids[:, 2, :]))
            dve.wait_ge(small_in, 80)
            did(dve.tensor_copy(ntf[:, :], nti[:, :]))
            settle()
            for t in range(NR):
                did(dve.tensor_scalar(mask[:, t, :], ntf[:, :], float(t), None, ALU.is_equal))
            settle()
            dve.nop().then_inc(consts_ready, 1)
            dve.wait_ge(x_in_s, 16)
            norm("x0", X, U)
            dve.wait_ge(rows_in_s[0], 96)
            for j in range(NT):
                did(dve.tensor_scalar(HB[0:TP, j, :], rows[:, 3, :], mask[:, 0, j:j + 1], None, ALU.mult))
            for t in range(1, NR):
                settle()
                for j in range(NT):
                    did(dve.scalar_tensor_tensor(HB[0:TP, j, :], rows[:, 3 + t, :], mask[:, t, j:j + 1],
                                                 HB[0:TP, j, :], ALU.mult, ALU.add))
            transposed("T0")

            def y_low(n):
                dve.wait_ge(y_hi, n + 1)
                minus(Y[:, 1, n, :], ytmp[n % 3], Y[:, 0, n, :], y_lo)

            for n in range(NR * NT):
                k = WORK["Y"] + n
                dve.wait_ge(work_full, k + 1)
                if n >= 3:
                    dve.wait_ge(y_lo, n - 2)
                dve.tensor_tensor(ytmp[n % 3], bank_w(k)[0:TP, :], rows[:, n // NT, :],
                                  ALU.add).then_inc(work_drained, 1)
                if n >= 1:
                    y_low(n - 1)
                if n < NS:
                    lo_ = TP * (n // 2) + SUB[n % 2][0]
                    settle()
                    did(dve.tensor_scalar(above[n % 2], ek, lo_ - 0.5, None, ALU.is_gt))
                    settle()
                    did(dve.scalar_tensor_tensor(in_half[:, n, :], ek, lo_ + SUB[n % 2][1] - 0.5,
                                                 above[n % 2], ALU.is_lt, ALU.mult))
            y_low(NR * NT - 1)
            settle()
            dve.nop().then_inc(flags_ready, 1)
            did(dve.scalar_tensor_tensor(ek, etype, float(N), ek, ALU.mult, ALU.add))
            for n, (c0, c1) in enumerate(FLAGS):
                dve.wait_ge(work_full, WORK["FLAG"] + n + 1)
                dve.tensor_reduce(present[:, c0:c1, :],
                                  bank_w(WORK["FLAG"] + n)[0:1, 0:(c1 - c0) * ET].rearrange("p (c n u) -> p c n u",
                                                                             c=c1 - c0, u=UNR),
                                  AX.X, ALU.add).then_inc(work_drained, 1)
            dve.wait_ge(work_drained, WORK["FLAG"] + len(FLAGS))
            steps_of = stepno[:, :].unsqueeze(1).to_broadcast([1, NS, EG])
            did(dve.tensor_scalar(marked[:, 1, :, :], steps_of, -1.0, EG + 1.0, ALU.mult, ALU.add))
            did(dve.scalar_tensor_tensor(marked[:, 0, :, :], present[:, :, :], 0.5, steps_of, ALU.is_gt, ALU.mult))
            settle()
            did(dve.scalar_tensor_tensor(marked[:, 1, :, :], present[:, :, :], 0.5, marked[:, 1, :, :],
                                         ALU.is_gt, ALU.mult))
            settle()
            did(dve.tensor_reduce(spanf[:, 0:2, :], marked, AX.X, ALU.max))
            settle()
            did(dve.tensor_scalar(spanf[:, 1, :], spanf[:, 1, :], 1.0, -1.0, ALU.max, ALU.mult))
            settle()
            did(dve.tensor_scalar(spanf[:, 1, :], spanf[:, 1, :], float(EG), None, ALU.add))
            settle()
            did(dve.scalar_tensor_tensor(spanf[:, 2, :], spanf[:, 1, :], 1.0, spanf[:, 0, :],
                                         ALU.add, ALU.max))
            settle()
            did(dve.tensor_tensor(spanf[:, 0, :], spanf[:, 2, :], spanf[:, 1, :], ALU.subtract))
            settle()
            did(dve.tensor_tensor_scan(spanf[:, 3, :], one8[0:1, 0:NS], spanf[:, 0, :], 0.0,
                                       ALU.mult, ALU.add))
            settle()
            did(dve.tensor_tensor(spanf[:, 3, :], spanf[:, 3, :], spanf[:, 2, :], ALU.subtract))
            settle()
            did(dve.tensor_scalar(spanf[:, 3, :], spanf[:, 3, :], float(UNR), float(ET),
                                  ALU.mult, ALU.add))
            settle()
            dve.tensor_copy(spans[:, :, :], spanf[:, 1:4, :]).then_inc(spans_ready, 1)
            for n in range(NR * NT):
                t, j = divmod(n, NT)
                k = WORK["SELF"] + n
                dve.wait_ge(work_full, k + 1)
                if t >= 1:
                    dve.wait_ge(work_drained, k - NT + 1)
                dve.scalar_tensor_tensor(HB[0:TP, j, :], bank_w(k)[0:TP, :], mask[:, t, j:j + 1],
                                         HB[0:TP, j, :], ALU.mult, ALU.add).then_inc(work_drained, 1)
            dve.memset(zero, 0.0).then_inc(zeros_ready, 1)
            dve.wait_ge(spans_ready, 1)
            iokr = iok[:, 0:NR * N].rearrange("p (r n) -> p r n", r=NR)

            def residual(c):
                k = WORK["AGG"] + c
                dve.wait_ge(work_full, k + 1)
                dve.tensor_tensor(HB[0:TP, c, :], bank_w(k)[0:TP, :], HB[0:TP, c, :],
                                  ALU.add).then_inc(work_drained, 1)
                dve.wait_ge(work_drained, k + 1)
                did(dve.scalar_tensor_tensor(X[:, c, :], HB[0:TP, c, :], 0.0, X[:, c, :],
                                             ALU.max, ALU.add))

            for c in range(NT):
                for n in (2 * c, 2 * c + 1):
                    first = dve.value_load(spans[0:1, 0, n:n + 1], min_val=0, max_val=EG - 1)
                    end = dve.value_load(spans[0:1, 1, n:n + 1], min_val=1, max_val=EG)
                    before = dve.value_load(spans[0:1, 2, n:n + 1], min_val=UNR, max_val=NS * ET)
                    d0, dw = SUB[n % 2]
                    d0 += TP * c
                    with dve.Fori(first, end) as it:
                        for u in range(UNR):
                            dve.wait_ge(oh_used, before + it * UNR + (u + 1))
                            dve.tensor_scalar(ohs[:, u, 0:NP2], iok[:, 0:NP2],
                                              es[:, bass.ds(it * UNR + u, 1)], None, ALU.is_equal)
                            dve.tensor_scalar(
                                ohk[:, u, 0:NR * dw].rearrange("p (r n) -> p r n", r=NR),
                                iokr[:, :, d0:d0 + dw], ek[:, bass.ds(it * UNR + u, 1)], None,
                                ALU.is_equal).then_inc(oh_ready, 1)
                if c >= 2:
                    residual(c - 2)
                for j in range(NT):
                    dve.wait_ge(acc_full, NT * c + j + 1)
                    dve.wait_ge(ac_hi, NT * c + j + 1)
                    minus(AC[c % 2][:, 1, j, :], ps[j][0:TP, 0:CW], AC[c % 2][:, 0, j, :])
                    with nc.allow_low_precision(reason="counts up to 20000 are exact in uint16"):
                        dve.tensor_reduce(tot[:, j, TP * c:TP * c + TP],
                                          ps[j][0:TP, 0:CW].rearrange("p (r n) -> p n r", r=NR), AX.X,
                                          ALU.add).then_inc(acc_drained, 1)
            residual(NT - 2)
            residual(NT - 1)
            did(dve.memset(XT[:, :, :, N:NP2].bitcast(F32), 0.0))
            settle()
            dve.nop().then_inc(rows_free, 1)
            norm("x1", X, U)
            for j in range(NT):
                did(dve.tensor_tensor(X[:, j, :], X[:, j, :], U[0:TP, j, :], ALU.add))
            transposed("T1")
            k = WORK["LG"]
            dve.wait_ge(work_full, k + 1)
            dve.tensor_copy(LGT[:, :, 4, 0:4],
                            bank_w(k)[0:TP, 0:40].rearrange("p (a b) -> p a b", a=NT)[:, :, 0:4]
                            ).then_inc(work_drained, 1)
            norm("z", U, Z)
            dve.wait_ge(rows_in_s[1], 96)
            for j in range(NT):
                did(dve.tensor_tensor(Z[0:TP, j, :], Z[0:TP, j, :], rows[:, 0, :], ALU.mult))
            settle()
            for j in range(NT):
                did(dve.tensor_tensor(Z[0:TP, j, :], Z[0:TP, j, :], rows[:, 1, :], ALU.add))
            settle()
            dve.nop().then_inc(z_done, 1)
            for c in range(16):
                did(dve.tensor_scalar(SEL[:, c, :], mk64[:, :], -2.0 * c, None, ALU.is_equal))
            did(dve.memset(IW[:, :, N:NP2].bitcast(F32), 0.0))
            did(dve.tensor_scalar(kg[:, 1, :], kg[:, 0, :], 7.5, None, ALU.is_lt))
            settle()
            did(dve.scalar_tensor_tensor(kg[:, 1, :], kg[:, 0, :], -0.5, kg[:, 1, :], ALU.is_gt, ALU.mult))
            dve.wait_ge(b2_in, 16)
            settle()
            for g in range(G0):
                settle()
                did(dve.tensor_scalar(b2m, b2f, kg[:, 1, g:g + 1], None, ALU.mult))
                settle()
                did(dve.tensor_copy(B2[:, 0, g, :], b2m))
                settle()
                minus(B2[:, 1, g, :], b2m, B2[:, 0, g, :])
            transposed("T2")
            k = WORK["LI"]
            dve.wait_ge(work_full, k + 1)
            dve.tensor_copy(LGT[:, :, 0:4, :],
                            bank_w(k)[0:TP, 0:160].rearrange("p (a b n) -> p a b n", a=NT, b=4)
                            ).then_inc(work_drained, 1)
            dve.wait_ge(work_drained, k + 1)
            gates(5, 0)
            dve.nop().then_inc(gates_ready, 1)
            for n in range(4):
                k = WORK["GT"] + n
                t0, t1 = PARTS[n % 2]
                sl = slice(TP * t0, TP * t1)
                dve.wait_ge(work_full, k + 1)
                if n < 2:
                    dve.wait_ge(gt_hi, n + 1)
                    minus(IW[:, 1, sl], bank_w(k)[0:32, 0:TP * (t1 - t0)], IW[:, 0, sl], work_drained)
                else:
                    dve.tensor_copy(gT[0:G0, sl], bank_w(k)[0:G0, 0:TP * (t1 - t0)]).then_inc(work_drained, 1)

            def hidden(g):
                for s in range(8):
                    cc, (c0, w) = s // 2, HALF[s % 2]
                    k = WORK["FF"] + 16 * g + 2 * s
                    q = 8 * g + s
                    dve.wait_ge(work_full, k + 2)
                    dve.wait_ge(relu_done, q + 1)
                    if q >= 2:
                        dve.wait_ge(ht_lo, q - 1)
                    dve.tensor_tensor(f2[q % 2][:, 0:w], f1[q % 2][:, 0:w], bank_w(k + 1)[:, 0:w],
                                      ALU.mult).then_inc(f2_done, 1)
                    dve.wait_ge(f2_done, q + 1)
                    dve.sem_inc(work_drained, 2)
                    dve.wait_ge(ht_hi, q + 1)
                    minus(HT[:, g % 2, 1, cc, c0:c0 + w], f2[q % 2][:, 0:w],
                          HT[:, g % 2, 0, cc, c0:c0 + w], ht_lo)

            def group(g):
                for j in range(NT):
                    n = ACC["MOE"] + NT * g + j
                    dve.wait_ge(acc_full, n + 1)
                    dve.tensor_tensor(HB[0:TP, j, :], ps[j][0:TP, :], Z[0:TP, j, :],
                                      ALU.add).then_inc(acc_drained, 1)
                dve.wait_ge(acc_drained, ACC["MOE"] + NT * (g + 1))
                moments(f"g{g}", HB)
                did(dve.tensor_tensor(ga[:, :], gat[:, :, 4, g], rs[:, :], ALU.mult))
                settle()
                did(dve.scalar_tensor_tensor(gc[:, :], mv[:, :, 0], -1.0, ga[:, :], ALU.mult, ALU.mult))
                for j in range(NT):
                    did(dve.scalar_tensor_tensor(HB[0:TP, j, :], HB[0:TP, j, :], ga[:, j:j + 1],
                                                 rows[:, 2 + g, :], ALU.mult, ALU.mult))
                settle()
                for j in range(NT):
                    did(dve.tensor_tensor(X[:, j, :], X[:, j, :], HB[0:TP, j, :], ALU.add))
                settle()
                for j in range(NT):
                    did(dve.scalar_tensor_tensor(X[:, j, :], rows[:, 2 + g, :], gc[:, j:j + 1],
                                                 X[:, j, :], ALU.mult, ALU.add))
                settle()

            hidden(0)
            hidden(1)
            group(0)
            hidden(2)
            group(1)
            hidden(3)
            group(2)
            group(3)
            dve.nop().then_inc(rows_free, 1)
            for j in range(NT):
                k = WORK["GB"] + j
                dve.wait_ge(work_full, k + 1)
                dve.tensor_tensor(X[:, j, :], bank_w(k)[0:TP, :], X[:, j, :], ALU.add).then_inc(work_drained, 1)
            dve.wait_ge(work_drained, WORK["GB"] + NT)
            norm("x2", X, U)
            for j in range(NT):
                dve.nop().then_inc(xs_src, 1)
            for j in range(NT):
                dve.wait_ge(xs_hi, j + 1)
                minus(XS[:, 1, j, :], U[0:TP, j, :], XS[:, 0, j, :], xs_lo)
                dve.wait_ge(at_hi, j + 1)
                minus(AT[:, 1, j, :], tot[:, j, :], AT[:, 0, j, :], at_lo)
            transposed("T3")
            k = WORK["DEG"]
            dve.wait_ge(work_full, k + 1)
            dve.tensor_scalar(rdeg[:, :], bank_w(k)[0:TP, 0:NT],
                              1.0, None, ALU.max).then_inc(work_drained, 1)
            dve.wait_ge(work_drained, k + 1)
            did(dve.reciprocal(rdeg[:, :], rdeg[:, :]))
            settle()
            ag_n = [0]

            def conv(s):
                k = WORK[("AG1", "AG2")[s]]
                for dk in range(KD):
                    for c0, w in HALF:
                        ag_n[0] += 1
                        dve.wait_ge(work_full, k + 1)
                        dve.wait_ge(ag_hi, ag_n[0])
                        minus(AG[:, 1, dk, c0:c0 + w], bank_w(k)[:, 0:w], AG[:, 0, dk, c0:c0 + w],
                              work_drained)
                        k += 1
                if s == 0:
                    dve.wait_ge(rows_in_s[2], 96)
                name = ("C1", "C2")[s]
                for j in range(NT):
                    n = ACC[name] + j
                    dve.wait_ge(acc_full, n + 1)
                    dve.scalar_tensor_tensor(Z[0:TP, j, :], ps[j][0:TP, :], rdeg[:, j:j + 1],
                                             rows[:, 3 * s, :], ALU.mult, ALU.add).then_inc(acc_drained, 1)
                dve.wait_ge(acc_drained, ACC[name] + NT)
                for j in range(NT):
                    k = WORK[name] + j
                    dve.wait_ge(work_full, k + 1)
                    dve.tensor_tensor(Z[0:TP, j, :], bank_w(k)[0:TP, :], Z[0:TP, j, :],
                                      ALU.add).then_inc(work_drained, 1)
                dve.wait_ge(work_drained, WORK[name] + NT)
                norm(("c1", "c2")[s], Z, Z)
                for j in range(NT):
                    did(dve.tensor_tensor(Z[0:TP, j, :], Z[0:TP, j, :], rows[:, 3 * s + 1, :], ALU.mult))
                settle()
                for j in range(NT):
                    did(dve.tensor_tensor(Z[0:TP, j, :], Z[0:TP, j, :], rows[:, 3 * s + 2, :], ALU.add))
                settle()

            conv(0)
            for j in range(NT):
                dve.scalar_tensor_tensor(U[0:TP, j, :], Z[0:TP, j, :], 0.0, U[0:TP, j, :],
                                         ALU.max, ALU.add).then_inc(xs_src, 1)
            dve.wait_ge(xs_src, 2 * NT)
            for j in range(NT):
                dve.wait_ge(xs_hi, NT + j + 1)
                minus(XS[:, 1, j, :], U[0:TP, j, :], XS[:, 0, j, :], xs_lo)
            transposed("T4")
            conv(1)
            dve.nop().then_inc(rows_free, 1)
            for src in (Z, U):
                for j in range(NT):
                    did(dve.tensor_tensor(X[:, j, :], X[:, j, :], src[0:TP, j, :], ALU.add))
                settle()
            norm("x3", X, U)
            norm("w0", U, Z)
            dve.wait_ge(rows_in_s[3], 32)
            for j in range(NT):
                did(dve.tensor_tensor(Z[0:TP, j, :], Z[0:TP, j, :], rows[:, 0, :], ALU.mult))
                did(dve.tensor_tensor(X[:, j, :], X[:, j, :], U[0:TP, j, :], ALU.add))
            settle()
            for j in range(NT):
                dve.tensor_tensor(Z[0:TP, j, :], Z[0:TP, j, :], rows[:, 1, :], ALU.add).then_inc(xs_src, 1)
            dve.wait_ge(xs_src, 3 * NT)
            dve.nop().then_inc(z_done, 1)
            dve.nop().then_inc(rows_free, 1)
            for j in range(NT):
                dve.wait_ge(xs_hi, 2 * NT + j + 1)
                minus(XS[:, 1, j, :], Z[0:TP, j, :], XS[:, 0, j, :], xs_lo)
            transposed("T5")
            k = WORK["LR"]
            dve.wait_ge(work_full, k + 1)
            dve.tensor_tensor(LGT[:, :, 0, :], bank_w(k)[0:TP, 0:40].rearrange("p (a b) -> p a b", a=NT),
                              rbt[:, :].unsqueeze(1).to_broadcast([TP, NT, NX]), ALU.add
                              ).then_inc(work_drained, 1)
            dve.wait_ge(work_drained, k + 1)
            gates(1, 1)
            shape = [TP, NT, NX]
            it = iota[:, 0:8].unsqueeze(1).to_broadcast(shape)
            did(dve.tensor_tensor(eq1, it, idxf[:, :, 0, 0:1].to_broadcast(shape), ALU.is_equal))
            did(dve.tensor_tensor(gsb, it, idxf[:, :, 0, 1:2].to_broadcast(shape), ALU.is_equal))
            did(dve.tensor_scalar(tri, mk[0:TP, 0:TP], 0.0, None, ALU.is_gt))
            settle()
            did(dve.tensor_tensor(sel16, eq1, gsb, ALU.add))
            settle()
            dve.nop().then_inc(sel_ready, 1)
            k = WORK["POS"]
            dve.wait_ge(work_full, k + 1)
            b = bank_w(k)
            did(dve.tensor_scalar(cum[:, 1, :], b[:, 64:72], 0.5, None, ALU.is_gt))
            for lim in (SLOTS + 0.5, 2 * SLOTS + 0.5):
                settle()
                did(dve.scalar_tensor_tensor(cum[:, 1, :], b[:, 64:72], lim, cum[:, 1, :],
                                             ALU.is_gt, ALU.add))
            settle()
            did(dve.tensor_tensor_scan(cum[:, 2, :], one8[:, 0:NX], cum[:, 1, :], 0.0, ALU.mult, ALU.add))
            settle()
            did(dve.tensor_tensor(cbase, cum[:, 2, :], cum[:, 1, :], ALU.subtract))
            si = [1, NI, NX]
            did(dve.tensor_tensor(ele[:, :, :], cum[0:1, 2, :].unsqueeze(1).to_broadcast(si),
                                  i12[:, :].unsqueeze(2).to_broadcast(si), ALU.is_le))
            settle()
            did(dve.tensor_reduce(itf[:, :], ele[:, :, :], AX.X, ALU.add))
            did(dve.scalar_tensor_tensor(ends, cbase[0:1, :], float(SLOTS), b[0:1, 64:72],
                                         ALU.mult, ALU.add))
            did(dve.tensor_scalar(lims, i12[:, :], float(SLOTS), 128.5, ALU.mult, ALU.add))
            did(dve.tensor_tensor(ele2, cbase[0:1, :].unsqueeze(1).to_broadcast(si),
                                  i12[:, :].unsqueeze(2).to_broadcast(si), ALU.is_le))
            settle()
            did(dve.tensor_tensor(ele2, ele2, ele, ALU.subtract))
            settle()
            did(dve.tensor_tensor(ele2, ele2, ends.unsqueeze(1).to_broadcast(si), ALU.mult))
            settle()
            did(dve.tensor_reduce(ends2, ele2, AX.X, ALU.add))
            settle()
            did(dve.tensor_tensor(ends2, ends2, lims, ALU.is_gt))
            settle()
            did(dve.tensor_copy(items[:, NI + 1:], ends2))
            settle()
            did(dve.tensor_scalar(itf[:, :], itf[:, :], float(NX - 1), None, ALU.min))
            settle()
            did(dve.tensor_copy(items[:, NI:NI + 1], cum[0:1, 2, NX - 1:NX]))
            settle()
            dve.tensor_copy(items[:, 0:NI], itf[:, :]).then_inc(items_ready, 1)
            did(dve.tensor_scalar(cbase, cbase, float(SLOTS), None, ALU.mult))
            settle()
            dve.tensor_tensor(gsv, b[0:TP, 0:40].rearrange("p (a b) -> p a b", a=NT),
                              cbase[0:TP, :].unsqueeze(1).to_broadcast(shape), ALU.add
                              ).then_inc(work_drained, 1)
            dve.wait_ge(work_drained, k + 1)
            did(dve.tensor_tensor(eq1, eq1, gsv, ALU.mult))
            did(dve.tensor_tensor(gsb, gsb, gsv, ALU.mult))
            settle()
            did(dve.tensor_reduce(gsl[:, :, 0], eq1, AX.X, ALU.add))
            did(dve.tensor_reduce(gsl[:, :, 1], gsb, AX.X, ALU.add))
            did(dve.tensor_copy(gsl[:, :, 2:4], p12[:, :, 0, :]))
            settle()
            did(dve.tensor_copy(gcur[:, :, :], gsl[:, :, 0:2]))
            for n in range(2):
                k = WORK["GX"] + n
                t0, t1 = PARTS[n]
                dve.wait_ge(work_full, k + 1)
                dve.tensor_copy(gT[:, TP * t0:TP * t1], bank_w(k)[0:NX, 0:TP * (t1 - t0)]
                                ).then_inc(work_drained, 1)
            for j in range(NT):
                k = WORK["FB"] + j
                dve.wait_ge(work_full, k + 1)
                dve.tensor_tensor(X[:, j, :], bank_w(k)[0:TP, :], X[:, j, :], ALU.add
                                  ).then_inc(work_drained, 1)
            for j in range(NT):
                k = WORK["DG"] + j
                if j >= 2:
                    dve.wait_ge(work_full, k - 1)
                for v in range(4):
                    ins = dve.tensor_scalar(dg[j % 2][:, v, :], ident[0:TP, 0:TP], gsl[:, j, v:v + 1],
                                            None, ALU.mult)
                ins.then_inc(diag_ready, 1)
                dve.wait_ge(work_full, k + 1)
                dve.tensor_copy(R4[:, :, TP * j:TP * j + TP],
                                bank_w(k)[:, 0:4 * TP].rearrange("p (a n) -> p a n", a=4)
                                ).then_inc(work_drained, 1)
            dve.wait_ge(work_drained, WORK["END"])
            settle()

            loop = sem("item_step")

            def s_first(j):
                return dve.tensor_scalar(s1[:, j, :], siota, gcur[:, j, 0:1], None, ALU.is_equal)

            def s_second(j):
                return dve.scalar_tensor_tensor(S[:, j, :], siota, gcur[:, j, 1:2], s1[:, j, :],
                                                ALU.is_equal, ALU.add)

            dve.wait_ge(iotas, 9)
            for j in range(NT):
                did(s_first(j))
            settle()
            for j in range(NT):
                ins = s_second(j)
            ins.then_inc(s_ready, 1)
            did(dve.memset(ps[1][:, :], 0.0))
            did(dve.memset(ST.bitcast(F32), 0.0))
            dve.memset(YS.bitcast(F32), 0.0).then_inc(ys_lo, 2)
            settle()
            dve.nop().then_inc(st_ready, 1)

            def gathered(done):
                for dk in range(KD):
                    dve.wait_ge(xc_full, done + (dk + 1))
                    dve.wait_ge(xc_hi, done + (dk + 1))
                    minus(XC[:, 1, dk, :], ps[6 + dk % 2][:, 0:SLOTS], XC[:, 0, dk, :], xc_lo)

            def scattered(i):
                for j in range(NT):
                    dve.wait_ge(sc_full, i * NT + (j + 1))
                    dve.tensor_tensor(X[:, j, :], ps[6 + j % 2][0:TP, :], X[:, j, :],
                                      ALU.add).then_inc(sc_added, 1)

            gathered(0)
            n_items = dve.value_load(items[0:1, NI:NI + 1], min_val=1, max_val=NI)
            with dve.Fori(0, n_items) as i:

                def loop_did(ins):
                    ins.then_inc(loop, 1)

                def hidden_low(q):
                    for f in range(2):
                        n = 2 * q + f
                        dve.wait_ge(hd_hi, i * 16 + (n + 1))
                        minus(HD[:, q % 2, 1, f, :], hid[:, q % 2, f, :], HD[:, q % 2, 0, f, :], hd_lo)

                def at(n):
                    dve.wait_ge(loop, i * CHAIN + n)

                hidden_low(0)
                hidden_low(1)
                scattered(i)
                hidden_low(2)
                n = 0
                for h in range(2):
                    loop_did(dve.tensor_scalar(stmp, R4[:, 0, :], sid[:, h:h + 1], None, ALU.is_equal))
                    n += 1
                    at(n)
                    loop_did(dve.scalar_tensor_tensor(ST[:, h, :], R4[:, 1, :], sid[:, h:h + 1], stmp,
                                                      ALU.is_equal, ALU.add))
                    n += 1
                    for c in range(2):
                        loop_did(dve.scalar_tensor_tensor(junk, R4[:, c, :], sid[:, h:h + 1],
                                                          R4[:, 2 + c, :], ALU.is_equal, ALU.mult,
                                                          accum_out=gs[:, h, c:c + 1]))
                        n += 1
                        at(n)
                    hidden_low(3 + h)
                dve.tensor_tensor(gsum[:, :], gs[:, :, 0], gs[:, :, 1], ALU.add).then_inc(st_ready, 1)
                loop_did(dve.tensor_scalar(sid[:, :], sid[:, :], float(SLOTS), None, ALU.add))
                n += 1
                loop_did(dve.tensor_scalar(gcur[:, :, :], gcur[:, :, :], -float(SLOTS), None, ALU.add))
                n += 1
                at(n)
                for j in range(NT):
                    loop_did(s_first(j))
                    n += 1
                hidden_low(5)
                at(n)
                for j in range(NT):
                    ins = s_second(j)
                ins.then_inc(s_ready, 1)
                hidden_low(6)
                hidden_low(7)
                gathered(i * KD + KD)
                dve.wait_ge(st_ready, i + 2)
                for h in range(2):
                    dve.wait_ge(o_full, i * 2 + (h + 1))
                    dve.tensor_scalar(ysf[:, h, :], ps[h][:, :], gsum[:, h:h + 1], None,
                                      ALU.mult).then_inc(ys_done, 1)
                for h in range(2):
                    dve.wait_ge(ys_hi, i * 2 + (h + 1))
                    minus(YS[:, 1, h, :], ysf[:, h, :], YS[:, 0, h, :], ys_lo)
                assert n == CHAIN
            scattered(n_items)


CHAIN = 15
ORDER = [("h", 0)] + [u for q in range(1, 8) for u in (("h", q), ("o", q - 1))] + [("o", 7)]


def kernel(**inputs):
    import numpy as _np
    import concourse.bacc as _bacc
    from concourse import mybir as _mybir
    from concourse.bass_utils import run_bass_kernel_spmd as _run

    a = {k: _np.asarray(v) for k, v in inputs.items()}

    def unit(m):
        return m.reshape(2, 2, 128, 512).transpose(0, 2, 1, 3).reshape(2, 128, HU)

    def w1_0(g):
        return unit(a["L0_ffn_W1"][g].transpose(1, 0, 2).reshape(D, D))

    def w2_0(g):
        return unit(a["L0_ffn_W2"][g].reshape(D, D))

    units = [unit(a["L0_gnn_W_rel"][r]) for r in range(3)] + [unit(a["L0_gnn_W_self"][t]) for t in range(3)]
    units += [w1_0(0), w1_0(1), w2_0(0), w1_0(2), w2_0(1), w1_0(3), w2_0(2), w2_0(3)]
    units += [unit(a[n].T) for n in ("L1_gnn_W1l", "L1_gnn_W1r", "L1_gnn_W2l", "L1_gnn_W2r")]
    w1 = a["L1_ffn_W1"].reshape(NX, KD, 128, 8, 256).transpose(0, 3, 2, 1, 4).reshape(NX, 8, 128, HU)
    w2 = a["L1_ffn_W2"].reshape(NX, 8, 2, 128, D).transpose(0, 1, 3, 2, 4).reshape(NX, 8, 128, HU)
    wmoe = _np.stack([(w1 if kind == "h" else w2)[:, q] for kind, q in ORDER], 1)
    gate = _np.concatenate([a["L0_ffn_wg_group"], a["L0_ffn_wg_inner"].transpose(1, 0, 2).reshape(D, 32),
                            a["L1_ffn_w_r"].T], 1).reshape(KD, 128, 44).transpose(1, 0, 2)
    rows = [a["L0_gnn_b_rel"], a["L0_gnn_b_self"], a["L0_ffn_ln_g"][None], a["L0_ffn_ln_b"][None],
            a["L0_ffn_gln_g"]]
    rows += [a[n][None] for n in ("L1_gnn_b1l", "L1_gnn_ln1_w", "L1_gnn_ln1_b", "L1_gnn_b2l",
                                  "L1_gnn_ln2_w", "L1_gnn_ln2_b", "L1_ffn_ln_g", "L1_ffn_ln_b")]
    ids = _np.stack([a["src"], a["dst"], a["edge_type_3"]]).reshape(3, ET, TP).transpose(2, 0, 1)
    arrays = {
        "x": a["x"].reshape(NT, TP, D).transpose(1, 0, 2), "ids": ids,
        "ntype": a["node_type_3"].reshape(NT, TP).T, "rows": _np.concatenate(rows),
        "wstat": _np.concatenate(units), "wmoe": wmoe, "gate": gate,
        "b1_0": a["L0_ffn_b1"].reshape(16, 128).T, "b2_0": a["L0_ffn_b2"].reshape(32, D),
        "glnb": a["L0_ffn_gln_b"], "rb": a["L1_ffn_b_r"][None],
        "b1_1": a["L1_ffn_b1"].reshape(NX * 16, 128).T, "b2_1": a["L1_ffn_b2"],
    }
    arrays = {f"in_{k}": _np.ascontiguousarray(v) for k, v in arrays.items()}
    nc = _bacc.Bacc("TRN2", target_bir_lowering=False, num_devices=1)
    args = [nc.dram_tensor(k, v.shape, _mybir.dt.from_np(v.dtype), kind="ExternalInput").ap()
            for k, v in arrays.items()]
    args.append(nc.dram_tensor("out_x", (TP, NT, D), _mybir.dt.float32, kind="ExternalOutput").ap())
    gnn_moe(nc, *args)
    r = _run(nc, [arrays], core_ids=[0])
    return _np.ascontiguousarray(r.results[0]["out_x"].transpose(1, 0, 2).reshape(N, D))
```

```python
from contextlib import ExitStack

import numpy as np

import concourse.bass as bass
from concourse import mybir

F32 = mybir.dt.float32
F32R = mybir.dt.float32r
F16 = mybir.dt.float16
I32 = mybir.dt.int32
U32 = mybir.dt.uint32
U16 = mybir.dt.uint16
ALU = mybir.AluOpType
ACT = mybir.ActivationFunctionType
AX = mybir.AxisListType

N = 625
D = 512
NT, TP = 5, 125
NP2 = N + 1
HALF = [(0, 314), (314, 312)]
KD = D // 128
E = 20000
ET = E // TP
UNR = 4
EG = ET // UNR
NR = 3
CW = NR * TP
SUB = [(0, 63), (63, 62)]
NS = NT * len(SUB)
FLAGS = [(0, 3), (3, 6), (6, 9), (9, 10)]
G0 = 4
NX = 8
SLOTS = 256
NI = 12
assert NI >= (2 * N + NX * (SLOTS - 1)) // SLOTS
EPS = 1e-5
NEG = -3.0e38
HU = 1024
STATIC = 36
PER_ITEM = 16
VLOWS = PER_ITEM // 4
PLOWS = PER_ITEM - VLOWS
RING = 4
LEAD = 6
DEEP = 8
PARTS = [(0, 3), (3, 5)]
SPAN = [(0, 313), (313, 312)]

WORK, ACC = {}, {}
_n = 0
for _name, _uses in [("T0", 5), ("Y", 15), ("FLAG", 4), ("SELF", 15), ("AGG", 5), ("T1", 5), ("LG", 2), ("T2", 5),
                     ("LGB", 1), ("LI", 2), ("LIB", 1), ("GT", 4), ("FF", 64), ("GB", 5), ("T3", 5),
                     ("DEG", 2), ("AG1", 8), ("T4", 5), ("AG2", 8), ("T5", 5), ("LR", 2), ("LRB", 1),
                     ("POS", 1), ("GX", 2), ("DGT", 2), ("END", 0)]:
    WORK[_name] = _n
    _n += _uses
_n = 0
for _name, _uses in [("CNT", 25), ("MOE", 20), ("C1", 5), ("C2", 5), ("FB", 5), ("DG", 8), ("END", 0)]:
    ACC[_name] = _n
    _n += _uses
LN = {n: i for i, n in enumerate(["x0", "x1", "z", "g0", "g1", "g2", "g3", "x2", "c1", "c2", "x3", "w0"])}

LN_OUT = {n: i for i, n in enumerate(["x0", "x1", "x2", "x3"])}


def on_vector(k):
    return k % 4 == 3


def pool_lows(k):
    return k + 1 - (k + 1) // 4


def vector_lows(k):
    return (k + 1) // 4


def unit_end(k):
    if k < 3:
        return "work", WORK["Y"] + 5 * (k + 1)
    if k < 6:
        return "work", WORK["SELF"] + 5 * (k - 2)
    if k < 14:
        kind, g = [("h", 0), ("h", 1), ("o", 0), ("h", 2), ("o", 1), ("h", 3), ("o", 2), ("o", 3)][k - 6]
        return ("work", WORK["FF"] + 16 * (g + 1)) if kind == "h" else ("acc", ACC["MOE"] + 5 * (g + 1))
    return [("work", WORK["DEG"] + 1), ("acc", ACC["C1"] + 5),
            ("work", WORK["AG2"] + 1), ("acc", ACC["C2"] + 5)][k - 14]


def gnn_moe(nc, x_in, ids_in, ntype_in, rows_in, wstat, wmoe, gate_in, b1_0, b2_0, glnb_in,
            rb_in, b1_1, b2_1, out):
    with ExitStack() as ctx:
        def sb(name, shape, dt=F32):
            return ctx.enter_context(nc.sbuf_tensor(name, shape, dt))

        sems = {}

        def sem(name):
            if name not in sems:
                sems[name] = ctx.enter_context(nc.semaphore(name))
            return sems[name]

        X = sb("X", [TP, NT, D])
        U = sb("U", [128, NT, D])
        Z = sb("Z", [128, NT, D])
        HB = sb("HB", [128, NT, D])
        rows = sb("rows", [TP, 6, D])
        raw = sb("raw", [128, RING, HU])
        wsp = sb("wsp", [128, RING, 2, HU], F32R)
        XT = sb("XT", [128, 2, KD, NP2], F32R)
        BIGW = 2 * NR * NT * D + 2 * NT * CW
        BIG = sb("BIG", [128, BIGW], F32R)
        tot = sb("tot", [TP, NT, NP2], U16)
        iota = sb("iota", [TP, 16])
        mk64 = sb("mk64", [32, 128])
        kg = sb("kg", [32, 2, G0])
        ident = sb("ident", [128, 128])
        tri = sb("tri", [TP, TP], F16)
        ones = sb("ones", [128, 128], F32R)
        ones_h = sb("ones_h", [TP, 128], F16)
        epst = sb("epst", [TP, 1])
        nti = sb("nti", [TP, NT], I32)
        ntf = sb("ntf", [TP, NT])
        mask = sb("mask", [TP, NR, NT])
        stats = sb("stats", [TP, NT, 6])
        mv = sb("mv", [TP, NT, 2])
        std = sb("std", [TP, NT])
        rs = sb("rs", [TP, NT])
        ga = sb("ga", [TP, NT])
        nmr = ga
        gw = sb("gw", [128, 2, KD, 44], F32R)
        LGT = sb("LGT", [TP, NT, 5, 8])
        v8 = sb("v8", [TP, NT, 5, 8])
        idxf = sb("idxf", [TP, NT, 5, 2])
        p12 = sb("p12", [TP, NT, 5, 2])
        ex = sb("ex", [TP, NT, 5])
        gat = v8
        eqt = LGT
        b1c = sb("b1c", [128, 16])
        b1e = sb("b1e", [128, NX * 16])
        rbt = sb("rbt", [TP, NX])
        cum = sb("cum", [128, 3, NX])
        i12 = sb("i12", [1, NI])
        itf = sb("itf", [1, NI])
        items = sb("items", [1, 2 * NI + 1], I32)
        spanf = sb("spanf", [1, 4, NS])
        spans = sb("spans", [1, 3, NS], I32)
        stepno = tot[0:1, 0, 0:2 * EG].bitcast(F32)
        gsl = sb("gsl", [TP, NT, 4])
        gcur = sb("gcur", [TP, NT, 2])
        sid = sb("sid", [128, 2])
        gs = sb("gs", [128, 2, 2])
        gsum = sb("gsum", [128, 2])

        def flat(t):
            return t[:, :, :].rearrange("p a b -> p (a b)")

        def big(p, off, *shape):
            n = int(np.prod(shape))
            names = list("abcde"[:len(shape)])
            pat = f"p ({' '.join(names)}) -> p {' '.join(names)}"
            return BIG[0:p, off:off + n].rearrange(pat, **dict(zip(names, shape)))

        Y = big(TP, 0, 2, NR * NT, D)
        AC = [big(TP, 2 * NR * NT * D, 2, NT, CW),
              XT[0:TP, :, :, :].rearrange("p a b n -> p (a b n)")[:, 0:2 * NT * CW]
              .rearrange("p (a b n) -> p a b n", a=2, b=NT)]
        HT = big(128, 0, 2, 2, KD, NP2)
        o = 4 * KD * NP2
        IW = big(32, o, 2, NP2)
        o += 2 * NP2
        SEL = big(32, o, 16, 128)
        o += 16 * 128
        B2 = big(32, o, 2, G0, D)
        assert o + 2 * G0 * D <= BIGW
        XS = big(TP, 0, 2, NT, D)
        AT = big(TP, 2 * NT * D, 2, NT, NP2)
        AG = big(128, 2 * NT * D + 2 * NT * NP2, 2, KD, NP2)
        o = 2 * NT * D
        XC = big(128, o, 2, KD, SLOTS)
        o += 2 * KD * SLOTS
        S = big(TP, o, NT, SLOTS)
        o += NT * SLOTS
        HD = big(128, o, 2, 2, 2, SLOTS)
        o += 8 * SLOTS
        ST = big(128, o, 2, N)
        o += 2 * N
        YS = big(128, o, 2, 2, D)
        o += 4 * D
        more = big(128, o, 2, 2, HU)
        assert o + 4 * HU <= BIGW
        more_xt = (XT[:, :, :, :].rearrange("p a b n -> p (a b n)")[:, 0:4 * HU]
                   .rearrange("p (s a n) -> p s a n", s=2, a=2))

        def split_slot(k, part):
            n = k % DEEP
            if n < RING:
                return wsp[:, n, part, :]
            return (more if n < RING + 2 else more_xt)[:, n % 2, part, :]

        zf, uf, hf = flat(Z), flat(U), flat(HB)
        es, ek = zf[0:TP, 0:ET], zf[0:TP, ET:2 * ET]
        iok = zf[0:TP, 320:1260].bitcast(F16)
        ohs = zf[0:TP, 1260:2516].bitcast(F16)[:, 0:UNR * 628].rearrange("p (u n) -> p u n", u=UNR)
        ohk = uf[0:TP, 0:752].bitcast(F16).rearrange("p (u n) -> p u n", u=UNR)
        zero = uf[0:TP, 752:752 + 188].bitcast(F16)
        nek = uf[0:TP, 1500:1500 + ET]
        dist = uf[0:TP, 1700:1890].bitcast(F16).rearrange("p (u n) -> p u n", u=2)
        iokr = iok[:, 0:NR * N].rearrange("p (r n) -> p r n", r=NR)
        etype = zf[0:TP, 1260:1260 + ET]
        in_half = zf[0:TP, 1420:1420 + NS * ET // 2].bitcast(F16).rearrange("p (c n) -> p c n", c=NS)
        above = [zf[0:TP, 2220 + ET * i:2220 + ET * i + ET] for i in range(2)]
        ytmp = [uf[0:TP, 1024 + D * i:1536 + D * i] for i in range(3)]
        ids = hf[0:TP, 0:3 * ET].bitcast(I32).rearrange("p (a n) -> p a n", a=3)
        f1 = [uf[:, 314 * i:314 * i + 314] for i in range(2)]
        f2 = [uf[:, 314 * (i + 2):314 * (i + 2) + 314] for i in range(2)]
        gT = uf[0:8, 1256:1256 + NP2]
        bT = uf[0:8, 1882:1882 + D]
        i8 = hf[0:TP, 2000:2200].bitcast(U32).rearrange("p (a b n) -> p a b n", a=NT, b=5)
        b2f = hf[0:32, 0:D]
        R4 = uf[:, 0:4 * N].rearrange("p (a n) -> p a n", a=4)
        g4T = hf[0:4, 0:N]
        pick = zf[0:4, 0:512].rearrange("p (v n) -> p v n", v=4)
        gsb = hf[0:TP, 1040:1080].rearrange("p (a n) -> p a n", a=NT)
        eq1 = hf[0:TP, 1080:1120].rearrange("p (a n) -> p a n", a=NT)
        cbase, cslot = hf[0:128, 1120:1128], hf[0:128, 1264:1272]
        ntok = hf[0:1, 1272:1280]
        marked = uf[0:1, 0:800].rearrange("p (a c n) -> p a c n", a=2, c=NS)
        present = uf[0:1, 1024:1424].rearrange("p (c n) -> p c n", c=NS)
        ele, ele2 = [hf[0:1, 1400 + NI * NX * i:1400 + NI * NX * (i + 1)].rearrange("p (a n) -> p a n", a=NI)
                     for i in range(2)]
        ends2 = hf[0:1, 1630:1630 + NI]
        ends, lims = hf[0:1, 1600:1600 + NX], hf[0:1, 1610:1610 + NI]
        gsv = hf[0:TP, 1130:1170].rearrange("p (a n) -> p a n", a=NT)
        gw_raw = hf[:, 600:776].rearrange("p (a n) -> p a n", a=KD)
        mk = hf[:, 800:928]
        logT = [hf[0:32, 1254:1254 + NP2], hf[0:G0, 624:624 + NP2]]
        rdeg = hf[:, 0:NP2]
        agt = [hf[:, 640 + 314 * i:954 + 314 * i] for i in range(2)]
        sel16 = hf[0:TP, 1270:1290].bitcast(F16).rearrange("p (a n) -> p a n", a=NT)
        stmp, junk = hf[:, 0:N], hf[:, N:2 * N]
        s1 = hf[0:TP, 1250:1250 + NT * SLOTS].rearrange("p (a n) -> p a n", a=NT)
        hid = zf[:, 0:1024].rearrange("p (b c s) -> p b c s", b=2, c=2)
        ysf = zf[:, 1024:2048].rearrange("p (a n) -> p a n", a=2)
        siota = rows[:, 5, 0:SLOTS]

        ps = [ctx.enter_context(nc.psum_tensor(f"bank{i}", [128, 512], F32)) for i in range(8)]

        x_in_s, ids_in_s, small_in = [sem(f"x_landed{j}") for j in range(NT)], sem("ids_landed"), sem("small_landed")
        rows_in_s = [sem(f"rows_landed{i}") for i in range(4)]
        bt_in = [sem(f"bias_rows_landed{i}") for i in range(2)]
        b2_in, b2_hi = sem("b2_landed"), sem("b2_hi")
        raw_in = [sem(f"raw_landed{i}") for i in range(RING)]
        weight_hi, weight_lo, weight_lo_v = sem("weight_hi"), sem("weight_lo"), sem("weight_lo_by_vector")
        work_full, work_drained = sem("work_full"), sem("work_drained")
        acc_full, acc_drained = sem("acc_full"), sem("acc_drained")
        iotas, step = sem("iotas_made"), sem("vector_step")
        ln_std, ln_mom, ln_out, ln_coef = sem("ln_std"), sem("ln_moments"), sem("ln_out"), sem("ln_coefficients")
        xt_hi, y_hi, y_lo = sem("xt_hi"), sem("y_hi"), sem("y_lo")
        oh_ready, oh_used, ohk_act, dist_act = (sem("onehot_ready"), sem("onehot_used"),
                                                 sem("destination_by_scalar"), sem("distance_by_scalar"))
        ac_hi, ag_hi, ag_lo = sem("ac_hi"), sem("ag_hi"), sem("ag_lo")
        ex_in, ex_out = sem("exp_in"), sem("exp_out")
        gates_ready, gt_hi = sem("gates_ready"), sem("gates_t_hi")
        normed, weighed = sem("group_normed"), sem("group_weighed")
        relu_done, f2_done, ht_hi, ht_lo = sem("relu_done"), sem("gated"), sem("ht_hi"), sem("ht_lo")
        xs_src, xs_hi, xs_lo = sem("xs_source"), sem("xs_hi"), sem("xs_lo")
        at_hi, at_lo = sem("at_hi"), sem("at_lo")
        flags_ready, spans_ready = sem("chunk_flags_ready"), sem("spans_ready")
        zeros_ready = sem("zeros_ready")
        consts_ready, u_free, z_done, c1_done = (sem("constants_ready"), sem("u_free"), sem("z_done"),
                                                 sem("conv1_normed"))
        rows_free = sem("rows_free")
        sel_ready, gsl_ready, items_ready = sem("sel_ready"), sem("slots_ready"), sem("items_ready")
        s_ready, st_ready, st_zero = sem("s_ready"), sem("st_ready"), sem("st_zero")
        xc_full, xc_hi, xc_lo = sem("xc_full"), sem("xc_hi"), sem("xc_lo")
        h_full, hid_done, hd_hi, hd_lo = sem("h_full"), sem("hid_done"), sem("hd_hi"), sem("hd_lo")
        w2_used, o_full, ys_done, ys_hi, ys_lo = (sem("w2_used"), sem("o_full"), sem("ys_done"),
                                                  sem("ys_hi"), sem("ys_lo"))
        sc_full, sc_added = sem("scattered"), sem("scatter_added")
        out_done = sem("out_landed")

        block = ctx.enter_context(nc.Block())

        def bank_w(k):
            return ps[5 + k % 3]

        def blocks(k):
            return bank_w(k)[:, 0:KD * TP].rearrange("p (a n) -> p a n", a=KD)

        @block.sync
        def _(sp):
            for j in range(NT):
                sp.dma_start(X[:, j, :], x_in[:, j, :]).then_inc(x_in_s[j], 16)
            sp.dma_start(ids, ids_in).then_inc(ids_in_s, 16)
            for n in range(STATIC):
                if n >= RING:
                    sp.wait_ge(weight_lo, n - RING + 1)
                sp.dma_start(raw[:, n % RING, :], wstat[n]).then_inc(raw_in[n % RING], 16)

            def slot_free(i, k):
                if on_vector(k):
                    sp.wait_ge(weight_lo_v, i * VLOWS + (1 + vector_lows(k - RING)))
                else:
                    sp.wait_ge(weight_lo, i * PLOWS + (STATIC + pool_lows(k - RING)))

            sp.wait_ge(items_ready, 1)
            n_items = sp.value_load(items[0:1, NI:NI + 1], min_val=1, max_val=NI)
            with sp.Fori(0, n_items) as i:
                e = sp.value_load(items[0:1, bass.ds(i, 1)], min_val=0, max_val=NX - 1)
                for k in range(PER_ITEM):
                    slot_free(i, k)
                    sp.dma_start(raw[:, k % RING, :],
                                 wmoe[bass.ds(e, 1), k].rearrange("a p n -> (a p) n")
                                 ).then_inc(raw_in[k % RING], 16)
            for k in range(LEAD):
                slot_free(n_items, k)
                sp.dma_start(raw[:, k % RING, :], wmoe[0, k]).then_inc(raw_in[k % RING], 16)
            sp.wait_ge(sc_added, n_items * NT + NT)
            sp.dma_start(out, X[:, :, :]).then_inc(out_done, 16)
            sp.wait_ge(out_done, 16)

        @block.gpsimd
        def _(pool):
            def io(o_, pattern, mul):
                pool.iota(o_, pattern, base=0, channel_multiplier=mul,
                          allow_small_or_imprecise_dtypes=True).then_inc(iotas, 1)

            io(mk[:, :], [[1, 128]], -1)
            io(iota[:, :], [[1, 16]], 0)
            io(mk64[:, :], [[1, 2], [0, 64]], -1)
            io(kg[:, 0, :], [[-8, G0]], 1)
            io(iok, [[1, 1880]], 0)
            io(i12[:, :], [[1, NI]], 0)
            io(sid[:, :], [[128, 2]], 1)
            pool.iota(stepno, [[1, EG]], base=1, channel_multiplier=0,
                      allow_small_or_imprecise_dtypes=True).then_inc(iotas, 1)

            def lo(slot, hi, low):
                pool.tensor_tensor(low, raw[:, slot, :], hi.bitcast(F32), ALU.subtract).then_inc(weight_lo, 1)

            def item_lo(i, k):
                pool.wait_ge(weight_hi, i * PER_ITEM + (STATIC + k + 1))
                lo(k % RING, split_slot(k, 0), split_slot(k, 1))

            for n in range(STATIC):
                if n in (21, 25):
                    g = (21, 25).index(n)
                    for j in range(NT):
                        pool.wait_ge(normed, NT * g + j + 1)
                        pool.tensor_tensor(HB[0:TP, j, :], HB[0:TP, j, :], rows[:, 2 + g, :],
                                           ALU.mult).then_inc(weighed, 1)
                pool.wait_ge(weight_hi, n + 1)
                lo(n % RING, wsp[:, n % RING, 0, :], wsp[:, n % RING, 1, :])
            pool.wait_ge(acc_full, ACC["C2"] + NT)
            pool.memset(ST.bitcast(F32), 0.0).then_inc(st_zero, 1)
            pool.memset(YS.bitcast(F32), 0.0).then_inc(ys_lo, 2)
            pool.wait_ge(rows_free, 4)
            io(siota, [[1, SLOTS]], 0)
            pool.wait_ge(items_ready, 1)
            n_items = pool.value_load(items[0:1, NI:NI + 1], min_val=1, max_val=NI)
            with pool.Fori(0, n_items) as i:
                for k in range(PER_ITEM):
                    if not on_vector(k):
                        item_lo(i, k)
            for k in range(LEAD - RING):
                item_lo(n_items, k)

        @block.scalar
        def _(act):
            def rows_load(dst0, src0, n, sem_):
                for r in range(n):
                    act.dma_start(rows[:, dst0 + r, :],
                                  rows_in[src0 + r:src0 + r + 1, :].partition_broadcast(TP)
                                  .rearrange("p a n -> p (a n)")).then_inc(sem_, 16)

            act.dma_start(gw_raw, gate_in).then_inc(small_in, 16)
            act.dma_start(nti[:, :], ntype_in).then_inc(small_in, 16)
            act.dma_start(b1c[:, :], b1_0).then_inc(small_in, 16)
            act.dma_start(b1e[:, :], b1_1).then_inc(small_in, 16)
            act.dma_start(rbt[:, :], rb_in.partition_broadcast(TP).rearrange("p a n -> p (a n)")
                          ).then_inc(small_in, 16)

            def copy(dst, src, sem_):
                act.activation(dst, src, ACT.Copy).then_inc(sem_, 1)

            def hi_unit(k):
                if k >= STATIC // 2:
                    return
                for n in (2 * k, 2 * k + 1):
                    act.wait_ge(raw_in[n % RING], 16 * (n // RING + 1))
                    if k >= 2:
                        kind, v = unit_end(k - 2)
                        act.wait_ge(work_full if kind == "work" else acc_full, v)
                    copy(wsp[:, n % RING, 0, :], raw[:, n % RING, :], weight_hi)

            def norm(name):
                act.wait_ge(ln_mom, LN[name] + 1)
                act.activation(std[:, :], mv[:, :, 1], ACT.Sqrt, bias=epst[:, 0:1]).then_inc(ln_std, 1)

            def norm_apply(n, src, dst):
                act.wait_ge(ln_coef, n)
                for j in range(NT):
                    act.activation(dst[0:TP, j, :], src[:, j, :], ACT.Identity, bias=nmr[:, j:j + 1],
                                   scale=rs[:, j:j + 1]).then_inc(ln_out, 1)

            def transposed(name):
                k = WORK[name]
                for j in range(NT):
                    act.wait_ge(work_full, k + j + 1)
                    copy(XT[:, 0, :, TP * j:TP * j + TP], blocks(k + j), xt_hi)

            def split_rows(s):
                for j in range(NT):
                    act.wait_ge(xs_src, NT * s + j + 1)
                    copy(XS[:, 0, j, :], (U, U, Z)[s][0:TP, j, :], xs_hi)

            def aggregated(name):
                k = WORK[name]
                for dk in range(KD):
                    for c0, w in HALF:
                        act.wait_ge(work_drained, k + 1)
                        copy(AG[:, 0, dk, c0:c0 + w], agt[(k - WORK[name]) % 2][:, 0:w], ag_hi)
                        k += 1

            def gate_exp(s):
                act.wait_ge(ex_in, s + 1)
                act.activation(ex[:, :, :], ex[:, :, :], ACT.Exp).then_inc(ex_out, 1)

            act.wait_ge(consts_ready, 1)
            norm("x0")
            rows_load(0, 0, 6, rows_in_s[0])
            hi_unit(0)
            transposed("T0")
            hi_unit(1)
            for r in range(NR):
                for j in range(NT):
                    act.wait_ge(work_drained, WORK["Y"] + NT * r + j + 1)
                    copy(Y[:, 0, NT * r + j, :], ytmp[(NT * r + j) % 3], y_hi)
                hi_unit(r + 2)
            for t in range(NR):
                hi_unit(t + 5)
            act.nop().then_inc(ohk_act, ET + UNR)
            act.nop().then_inc(dist_act, ET)
            act.wait_ge(spans_ready, 1)
            for c in range(NT):
                for n in (2 * c, 2 * c + 1):
                    first = act.value_load(spans[0:1, 0, n:n + 1], min_val=0, max_val=EG - 1)
                    end = act.value_load(spans[0:1, 1, n:n + 1], min_val=1, max_val=EG)
                    before = act.value_load(spans[0:1, 2, n:n + 1], min_val=UNR, max_val=NS * ET)
                    d0, dw = SUB[n % 2]
                    d0 += TP * c
                    with act.Fori(first, end) as it:
                        for u in range(1, UNR, 2):
                            d3 = dist[:, u // 2, 0:NR * dw].rearrange("p (r n) -> p r n", r=NR)
                            act.wait_ge(ohk_act, before + it * UNR + (u + 1))
                            act.activation(d3, iokr[:, :, d0:d0 + dw], ACT.Abs,
                                           bias=nek[:, bass.ds(it * UNR + u, 1)]).then_inc(dist_act, 2)
                        for u in range(1, UNR, 2):
                            d3 = dist[:, u // 2, 0:NR * dw].rearrange("p (r n) -> p r n", r=NR)
                            act.wait_ge(oh_used, before + it * UNR + (u + 1))
                            act.wait_ge(dist_act, before + it * UNR + (u + 1))
                            act.activation(ohk[:, u, 0:NR * dw].rearrange("p (r n) -> p r n", r=NR), d3,
                                           ACT.Relu, bias=ones[0:TP, 0:1].bitcast(F32),
                                           scale=-1.0).then_inc(ohk_act, 2)
                for j in range(NT):
                    act.wait_ge(acc_full, NT * c + j + 1)
                    copy(AC[c % 2][:, 0, j, :], ps[j][0:TP, 0:CW], ac_hi)
            act.wait_ge(rows_free, 1)
            rows_load(0, 6, 6, rows_in_s[1])
            act.dma_start(b2f, b2_0).then_inc(b2_in, 16)
            norm("x1")
            norm_apply(1, X, U)
            transposed("T1")
            norm("z")
            transposed("T2")
            act.wait_ge(u_free, 1)
            act.dma_start(bT[0:G0, :], glnb_in).then_inc(bt_in[0], 16)
            gate_exp(0)
            for k in range(2):
                act.wait_ge(work_full, WORK["GT"] + k + 1)
                a, b = PARTS[k]
                copy(IW[:, 0, TP * a:TP * b], bank_w(WORK["GT"] + k)[0:32, 0:TP * (b - a)], gt_hi)

            def hidden(g):
                for s in range(8):
                    cc, (c0, w) = s // 2, HALF[s % 2]
                    k = WORK["FF"] + 16 * g + 2 * s
                    q = 8 * g + s
                    act.wait_ge(work_full, k + 1)
                    if q >= 2:
                        act.wait_ge(f2_done, q - 1)
                    act.activation(f1[q % 2][:, 0:w], bank_w(k)[:, 0:w], ACT.Relu,
                                   bias=b1c[:, 4 * g + cc:4 * g + cc + 1]).then_inc(relu_done, 1)
                    if g >= 2 and s < NT:
                        act.wait_ge(ln_coef, g)
                        act.activation(HB[0:TP, s, :], HB[0:TP, s, :], ACT.Identity, bias=nmr[:, s:s + 1],
                                       scale=rs[:, s:s + 1]).then_inc(normed, 1)
                    act.wait_ge(f2_done, q + 1)
                    copy(HT[:, g % 2, 0, cc, c0:c0 + w], f2[q % 2][:, 0:w], ht_hi)

            act.wait_ge(gates_ready, 1)
            act.wait_ge(b2_in, 16)
            for g in range(G0):
                act.activation(B2[:, 0, g, :], b2f, ACT.Copy, scale=kg[:, 1, g:g + 1]).then_inc(b2_hi, 1)
            hidden(0)
            hi_unit(8)
            hidden(1)
            hi_unit(9)
            norm("g0")
            hi_unit(10)
            hidden(2)
            hi_unit(11)
            norm("g1")
            hi_unit(12)
            hidden(3)
            hi_unit(13)
            norm("g2")
            hi_unit(14)
            norm("g3")
            hi_unit(15)
            act.wait_ge(rows_free, 2)
            rows_load(0, 12, 6, rows_in_s[2])
            norm("x2")
            transposed("T3")
            act.wait_ge(acc_full, ACC["C1"])
            for j in range(NT):
                act.wait_ge(xs_src, j + 1)
                copy(XS[:, 0, j, :], U[0:TP, j, :], xs_hi)
                copy(AT[:, 0, j, :], tot[:, j, :], at_hi)
            aggregated("AG1")
            hi_unit(16)
            hi_unit(17)
            norm("c1")
            act.wait_ge(rows_free, 3)
            rows_load(0, 18, 2, rows_in_s[3])
            transposed("T4")
            split_rows(1)
            aggregated("AG2")
            norm("c2")
            norm("x3")
            norm_apply(4, X, U)
            norm("w0")
            transposed("T5")
            split_rows(2)
            act.wait_ge(u_free, 2)
            act.dma_start(bT, b2_1).then_inc(bt_in[1], 16)
            gate_exp(1)
            act.wait_ge(items_ready, 1)
            act.wait_ge(work_drained, WORK["END"])
            def hi_item(i, k):
                act.wait_ge(raw_in[k % RING], i * (16 * PER_ITEM // RING)
                            + 16 * ((STATIC + k) // RING + 1))
                if k >= DEEP:
                    used(i, k - DEEP)
                copy(split_slot(k, 0), raw[:, k % RING, :], weight_hi)

            def used(i, k):
                kind, q = ORDER[k % PER_ITEM]
                d = k // PER_ITEM
                if kind == "h":
                    act.wait_ge(h_full, i * 16 + (16 * d + 2 * q + 2))
                elif q < 7:
                    act.wait_ge(w2_used, i * 7 + (7 * d + q + 1))
                else:
                    act.wait_ge(o_full, i * 2 + (2 * d + 2))

            def gathered(done):
                for dk in range(KD):
                    act.wait_ge(xc_full, done + (dk + 1))
                    copy(XC[:, 0, dk, :], ps[6 + dk % 2][:, 0:SLOTS], xc_hi)

            gathered(0)
            for k in range(LEAD):
                hi_item(0, k)
            n_items = act.value_load(items[0:1, NI:NI + 1], min_val=1, max_val=NI)
            with act.Fori(0, n_items) as i:
                e = act.value_load(items[0:1, bass.ds(i, 1)], min_val=0, max_val=NX - 1)
                for m, (kind, q) in enumerate(ORDER):
                    if kind == "h":
                        for f in range(2):
                            n = 2 * q + f
                            act.wait_ge(h_full, i * 16 + (n + 1))
                            if n >= 4:
                                act.wait_ge(hd_lo, i * 16 + (n - 3))
                            act.activation(hid[:, q % 2, f, :], ps[2 + n % 4][:, 0:SLOTS], ACT.Gelu,
                                           bias=b1e[:, bass.ds(e * 16 + n, 1)]).then_inc(hid_done, 1)
                            act.wait_ge(hid_done, i * 16 + (n + 1))
                            copy(HD[:, q % 2, 0, f, :], hid[:, q % 2, f, :], hd_hi)
                    if (kind, q) == ("h", 7):
                        gathered(i * KD + KD)
                    if m >= 1:
                        hi_item(i, m - 1 + LEAD)
                for h in range(2):
                    act.wait_ge(ys_done, i * 2 + (h + 1))
                    copy(YS[:, 0, h, :], ysf[:, h, :], ys_hi)
                hi_item(i, PER_ITEM + LEAD - 1)

        @block.tensor
        def _(pe):
            w = [0]
            a = [0]

            def work():
                k = w[0]
                if k >= 3:
                    pe.wait_ge(work_drained, k - 2)
                w[0] += 1
                return bank_w(k)

            def acc(j):
                if a[0] >= NT:
                    pe.wait_ge(acc_drained, a[0] - NT + 1)
                a[0] += 1
                return ps[j]

            def three(o_, terms, start, stop):
                last = None
                for n, (lh, ll, rh, rl) in enumerate(terms):
                    for m, (l, r) in enumerate([(lh, rh), (lh, rl), (ll, rh)]):
                        last = pe.matmul(o_, l, r, start=start and n == 0 and m == 0,
                                         stop=stop and n == len(terms) - 1 and m == 2)
                return last

            def weights(k):
                pe.wait_ge(weight_lo, 2 * k + 2)

            def wpart(k, kc, part, c0=0, cw=D):
                return wsp[:, (2 * k) % RING + kc // 2, part, (kc % 2) * D + c0:(kc % 2) * D + c0 + cw]

            def transpose(name, src, ready, before):
                assert w[0] == WORK[name]
                for j in range(NT):
                    pe.wait_ge(ready, before + j + 1)
                    b = work()
                    for dk in range(KD):
                        last = pe.transpose(b[:, TP * dk:TP * dk + TP],
                                            src[0:TP, j, 128 * dk:128 * dk + 128], ident[0:TP, 0:TP])
                    last.then_inc(work_full, 1)

            def rows_by(o_, src, j, k):
                return three(o_, [(src[:, 0, kc, TP * j:TP * j + TP], src[:, 1, kc, TP * j:TP * j + TP],
                                   wpart(k, kc, 0), wpart(k, kc, 1)) for kc in range(KD)], True, True)

            def logits(name, c0, n):
                assert w[0] == WORK[name]
                for t0, tw in HALF:
                    three(work()[0:n, 0:tw],
                          [(gw[:, 0, kc, c0:c0 + n], gw[:, 1, kc, c0:c0 + n],
                            XT[:, 0, kc, t0:t0 + tw], XT[:, 1, kc, t0:t0 + tw])
                           for kc in range(KD)], True, True).then_inc(work_full, 1)

            def logits_back(name, src, n):
                assert w[0] == WORK[name]
                b = work()
                for j in range(NT):
                    last = pe.transpose(b[0:TP, n * j:n * j + n], src[0:n, TP * j:TP * j + TP],
                                        ident[0:n, 0:n])
                last.then_inc(work_full, 1)

            pe.nop().then_inc(oh_used, UNR + ET)
            pe.wait_ge(consts_ready, 1)
            transpose("T0", U, ln_out, 0)
            pe.wait_ge(work_drained, WORK["Y"])
            for r in range(NR):
                weights(r)
                for j in range(NT):
                    rows_by(work()[0:TP, :], XT, j, r).then_inc(work_full, 1)
            pe.wait_ge(flags_ready, 1)
            for c0, c1 in FLAGS:
                pe.matmul(work()[:, 0:(c1 - c0) * ET], ones_h[:, :],
                          in_half[:, c0:c1, :].rearrange("p c n -> p (c n)"),
                          start=True, stop=True).then_inc(work_full, 1)
            for t in range(NR):
                weights(NR + t)
                for j in range(NT):
                    rows_by(work()[0:TP, :], XT, j, NR + t).then_inc(work_full, 1)
            pe.wait_ge(spans_ready, 1)
            pe.wait_ge(zeros_ready, 1)

            def messages(c):
                if c == 0:
                    pe.wait_ge(y_lo, NR * NT)
                pe.wait_ge(acc_drained, NT * (c + 1))
                three(work()[0:TP, :],
                      [(AC[c % 2][:, 0, j, TP * r:TP * r + TP], AC[c % 2][:, 1, j, TP * r:TP * r + TP],
                        Y[:, 0, NT * r + j, :], Y[:, 1, NT * r + j, :])
                       for r in range(NR) for j in range(NT)], True, True).then_inc(work_full, 1)

            for c in range(NT):
                for j in range(NT):
                    acc(j)
                    pe.matmul(ps[j][0:TP, 0:CW], zero[:, 0:TP], zero[:, 0:CW], start=True, stop=False)
                for h, (d0, dw) in enumerate(SUB):
                    n = 2 * c + h
                    first = pe.value_load(spans[0:1, 0, n:n + 1], min_val=0, max_val=EG - 1)
                    end = pe.value_load(spans[0:1, 1, n:n + 1], min_val=1, max_val=EG)
                    before = pe.value_load(spans[0:1, 2, n:n + 1], min_val=UNR, max_val=NS * ET)
                    with pe.Fori(first, end) as it:
                        for u in range(UNR):
                            pe.wait_ge(oh_ready, before + it * UNR + (u + 1))
                            if u % 2:
                                pe.wait_ge(ohk_act, before + it * UNR + (u + 1 + UNR))
                            for j in range(NT):
                                last = pe.matmul(
                                    ps[j][0:TP, 0:CW].rearrange("p (r n) -> p r n", r=NR)[:, :, d0:d0 + dw],
                                    ohs[:, u, TP * j:TP * j + TP],
                                    ohk[:, u, 0:NR * dw].rearrange("p (r n) -> p r n", r=NR),
                                    start=False, stop=False)
                            last.then_inc(oh_used, 1)
                for j in range(NT):
                    pe.matmul(ps[j][0:TP, 0:CW], zero[:, 0:TP], zero[:, 0:CW],
                              start=False, stop=True).then_inc(acc_full, 1)
                if c >= 1:
                    messages(c - 1)
            messages(NT - 1)
            transpose("T1", U, ln_out, NT * LN_OUT["x1"])
            pe.wait_ge(work_drained, WORK["LG"])
            logits("LG", 0, G0)
            transpose("T2", Z, z_done, 0)
            pe.wait_ge(work_drained, WORK["LG"] + 2)
            logits_back("LGB", logT[1], G0)
            pe.wait_ge(work_drained, WORK["LGB"])
            logits("LI", 4, 32)
            pe.wait_ge(work_drained, WORK["LIB"])
            logits_back("LIB", logT[0], 32)
            pe.wait_ge(gates_ready, 1)
            for width, sl in ((32, None), (G0, 4)):
                for t0, t1 in PARTS:
                    b = work()
                    for j in range(t0, t1):
                        src = (gat[:, j, 0:4, :].rearrange("p a b -> p (a b)") if sl is None
                               else gat[:, j, 4, 0:G0])
                        last = pe.transpose(b[0:width, TP * (j - t0):TP * (j - t0 + 1)], src,
                                            ident[0:TP, 0:TP])
                    last.then_inc(work_full, 1)
            pe.wait_ge(work_drained, WORK["FF"])

            def hidden(g, k):
                weights(k)
                for cc in range(KD):
                    for c0, cw in HALF:
                        b = work()
                        three(b[:, 0:cw], [(wpart(k, kc, 0, 128 * cc, 128), wpart(k, kc, 1, 128 * cc, 128),
                                            XT[:, 0, kc, c0:c0 + cw], XT[:, 1, kc, c0:c0 + cw])
                                           for kc in range(KD)], True, True).then_inc(work_full, 1)
                        b = work()
                        pe.matmul(b[:, 0:cw], SEL[:, 4 * g + cc, :], IW[:, 0, c0:c0 + cw],
                                  start=True, stop=False)
                        pe.matmul(b[:, 0:cw], SEL[:, 4 * g + cc, :], IW[:, 1, c0:c0 + cw],
                                  start=False, stop=True).then_inc(work_full, 1)

            def second(g, k):
                weights(k)
                pe.wait_ge(ht_lo, 8 * (g + 1))
                for j in range(NT):
                    sl = slice(TP * j, TP * j + TP)
                    b = acc(j)[0:TP, :]
                    three(b, [(HT[:, g % 2, 0, cc, sl], HT[:, g % 2, 1, cc, sl], wpart(k, cc, 0),
                               wpart(k, cc, 1)) for cc in range(KD)], True, False)
                    three(b, [(IW[:, 0, sl], IW[:, 1, sl], B2[:, 0, g, :], B2[:, 1, g, :])],
                          False, True).then_inc(acc_full, 1)

            hidden(0, 6)
            hidden(1, 7)
            second(0, 8)
            hidden(2, 9)
            second(1, 10)
            hidden(3, 11)
            pe.wait_ge(bt_in[0], 16)
            for j in range(NT):
                pe.matmul(work()[0:TP, :], gT[0:G0, TP * j:TP * j + TP], bT[0:G0, :], start=True,
                          stop=True).then_inc(work_full, 1)
            second(2, 12)
            second(3, 13)
            transpose("T3", U, ln_out, NT * LN_OUT["x2"])

            def conv(s, k):
                weights(k)
                pe.wait_ge(work_drained, w[0])
                banks = [acc(j)[0:TP, :] for j in range(NT)]
                for j in range(NT):
                    three(banks[j], [(XT[:, 0, kc, TP * j:TP * j + TP], XT[:, 1, kc, TP * j:TP * j + TP],
                                      wpart(k, kc, 0), wpart(k, kc, 1)) for kc in range(KD)], True, False)
                if s == 0:
                    pe.wait_ge(at_lo, NT)
                    for c0, cw in HALF:
                        b = work()
                        for part in range(2):
                            for j in range(NT):
                                last = pe.matmul(b[:, 0:cw], ones[0:TP, :], AT[:, part, j, c0:c0 + cw],
                                                 start=part + j == 0, stop=part == 1 and j == NT - 1)
                        last.then_inc(work_full, 1)
                pe.wait_ge(xs_lo, NT * (s + 1))
                for dk in range(KD):
                    for c0, cw in HALF:
                        three(work()[:, 0:cw],
                              [(XS[:, 0, j, 128 * dk:128 * dk + 128], XS[:, 1, j, 128 * dk:128 * dk + 128],
                                AT[:, 0, j, c0:c0 + cw], AT[:, 1, j, c0:c0 + cw])
                               for j in range(NT)], True, True).then_inc(work_full, 1)
                weights(k + 1)
                pe.wait_ge(ag_lo, 2 * KD * (s + 1))
                for j in range(NT):
                    three(banks[j], [(AG[:, 0, kc, TP * j:TP * j + TP], AG[:, 1, kc, TP * j:TP * j + TP],
                                      wpart(k + 1, kc, 0), wpart(k + 1, kc, 1))
                                     for kc in range(KD)], False, True).then_inc(acc_full, 1)

            conv(0, 14)
            transpose("T4", U, xs_src, NT)
            conv(1, 16)
            transpose("T5", Z, xs_src, 2 * NT)
            pe.wait_ge(work_drained, WORK["LR"])
            logits("LR", 36, NX)
            pe.wait_ge(work_drained, WORK["LRB"])
            logits_back("LRB", logT[0], NX)
            pe.wait_ge(sel_ready, 1)
            b = work()
            for i in range(NT):
                for j in range(i + 1):
                    pe.matmul(b[0:TP, 8 * i:8 * i + 8], tri[:, :] if j == i else ones_h[:, 0:TP], sel16[:, j, :],
                              start=j == 0, stop=j == i)
            for j in range(NT):
                last = pe.matmul(b[:, 64:72], ones_h[:, :], sel16[:, j, :], start=j == 0, stop=j == NT - 1)
            last.then_inc(work_full, 1)
            for t0, t1 in PARTS:
                b = work()
                for j in range(t0, t1):
                    last = pe.transpose(b[0:NX, TP * (j - t0):TP * (j - t0 + 1)], gat[:, j, 0, :],
                                        ident[0:TP, 0:TP])
                last.then_inc(work_full, 1)
            pe.wait_ge(bt_in[1], 16)
            pe.wait_ge(work_drained, WORK["DGT"])
            for j in range(NT):
                pe.matmul(acc(j)[0:TP, :], gT[:, TP * j:TP * j + TP], bT, start=True,
                          stop=True).then_inc(acc_full, 1)
            pe.wait_ge(gsl_ready, 1)
            for t0, t1 in PARTS:
                b = work()
                for j in range(t0, t1):
                    last = pe.transpose(b[0:4, TP * (j - t0):TP * (j - t0 + 1)], gsl[:, j, :],
                                        ident[0:TP, 0:TP])
                last.then_inc(work_full, 1)
            assert w[0] == WORK["END"]
            pe.wait_ge(work_drained, WORK["END"])
            n_items = pe.value_load(items[0:1, NI:NI + 1], min_val=1, max_val=NI)

            def gather(i):
                pe.wait_ge(s_ready, i + 2)
                for dk in range(KD):
                    if dk >= 2:
                        pe.wait_ge(xc_lo, i * KD + (KD + dk - 1))
                    elif not isinstance(i, int):
                        pe.wait_ge(sc_added, i * NT + NT)
                    for j in range(NT):
                        for part in range(2):
                            last = pe.matmul(ps[6 + dk % 2][:, 0:SLOTS],
                                             XS[:, part, j, 128 * dk:128 * dk + 128], S[:, j, :],
                                             start=j == 0 and part == 0, stop=j == NT - 1 and part == 1)
                    last.then_inc(xc_full, 1)

            def scatter(i):
                pe.wait_ge(st_ready, i + 1)
                pe.wait_ge(ys_lo, i * 2 + 2)
                for j in range(NT):
                    if j >= 2:
                        pe.wait_ge(sc_added, i * NT + (j - 1))
                    for h in range(2):
                        for part in range(2):
                            last = pe.matmul(ps[6 + j % 2][0:TP, :], ST[:, h, TP * j:TP * j + TP],
                                             YS[:, part, h, :], start=h == 0 and part == 0,
                                             stop=h == 1 and part == 1)
                    last.then_inc(sc_full, 1)

            def item(i, tiles):
                pe.wait_ge(xc_lo, i * KD + KD)
                for m, (kind, q) in enumerate(ORDER):
                    if on_vector(m):
                        pe.wait_ge(weight_lo_v, i * VLOWS + (1 + vector_lows(m)))
                    else:
                        pe.wait_ge(weight_lo, i * PLOWS + (STATIC + pool_lows(m)))
                    wh, wl = [split_slot(m, part).rearrange("p (a n) -> p a n", a=KD if kind == "h" else 2)
                              for part in range(2)]
                    if kind == "h":
                        for f in range(2):
                            n = 2 * q + f
                            if n >= 4:
                                pe.wait_ge(hid_done, i * 16 + (n - 3))
                            three(ps[2 + n % 4][:, 0:SLOTS],
                                  [(wh[:, kc, 128 * f:128 * f + 128], wl[:, kc, 128 * f:128 * f + 128],
                                    XC[:, 0, kc, :], XC[:, 1, kc, :]) for kc in range(KD)],
                                  True, True).then_inc(h_full, 1)
                        if q == 1:
                            scatter(i)
                        if q == 7:
                            gather(i)
                    else:
                        pe.wait_ge(hd_lo, i * 16 + (2 * q + 2))
                        for h in range(tiles):
                            hs = slice(128 * h, 128 * h + 128)
                            last = three(ps[h][:, :],
                                         [(HD[:, q % 2, 0, f, hs], HD[:, q % 2, 1, f, hs],
                                           wh[:, f, :], wl[:, f, :]) for f in range(2)], q == 0, q == 7)
                            if q == 7:
                                last.then_inc(o_full, 2 // tiles)
                        if q < 7:
                            last.then_inc(w2_used, 1)

            gather(-1)
            for q, (c0, cw) in enumerate(2 * SPAN):
                for v in (2 * (q // 2), 2 * (q // 2) + 1):
                    b = acc(a[0] % NT)
                    pe.matmul(b[:, 0:cw], pick[:, v, :], g4T[:, c0:c0 + cw], start=True,
                              stop=True).then_inc(acc_full, 1)
            assert a[0] == ACC["END"]
            pe.wait_ge(acc_drained, ACC["END"])
            with pe.Fori(0, n_items) as i:
                wide = pe.value_load(items[0:1, bass.ds(i + (NI + 1), 1)], min_val=0, max_val=1)
                with pe.If(wide > 0):
                    item(i, 2)
                with pe.Else():
                    item(i, 1)
            scatter(n_items)

        @block.vector
        def _(dve):
            steps = [0]

            def did(ins):
                ins.then_inc(step, 1)
                steps[0] += 1

            def settle():
                dve.wait_ge(step, steps[0])

            def minus(dst, src, hi, sem_=None):
                ins = dve.tensor_tensor(dst, src, hi.bitcast(F32), ALU.subtract)
                if sem_ is None:
                    did(ins)
                else:
                    ins.then_inc(sem_, 1)

            def stat(j, src):
                did(dve.bn_stats(stats[:, j, :], src[0:TP, j, :]))

            def moments(name):
                settle()
                for j in range(NT):
                    ins = dve.bn_aggr(mv[:, j, :], stats[:, j, :])
                    if j < NT - 1:
                        did(ins)
                ins.then_inc(ln_mom, 1)
                dve.wait_ge(ln_std, LN[name] + 1)
                did(dve.reciprocal(rs[:, :], std[:, :]))
                settle()

            def norm(name, src, dst, ready=0):
                for j in range(ready, NT):
                    stat(j, src)
                moments(name)
                for j in range(NT):
                    dve.tensor_scalar(dst[0:TP, j, :], src[0:TP, j, :], mv[:, j, 0:1], rs[:, j:j + 1],
                                      ALU.subtract, ALU.mult).then_inc(ln_out, 1)
                dve.wait_ge(ln_out, NT * (LN_OUT[name] + 1))

            def coefficients():
                dve.scalar_tensor_tensor(nmr[:, :], mv[:, :, 0], -1.0, rs[:, :], ALU.mult,
                                         ALU.mult).then_inc(ln_coef, 1)

            def norm_and_stat(name, src, dst, ready=0):
                for j in range(ready, NT):
                    stat(j, src)
                moments(name)
                coefficients()
                for j in range(NT):
                    dve.wait_ge(ln_out, NT * LN_OUT[name] + j + 1)
                    stat(j, dst)

            def norm_rows(name, src, dst, weight, bias, ready, done):
                for j in range(ready, NT):
                    stat(j, src)
                moments(name)
                for j in range(NT):
                    did(dve.scalar_tensor_tensor(dst[0:TP, j, :], src[0:TP, j, :], mv[:, j, 0:1],
                                                 weight, ALU.subtract, ALU.mult))
                settle()
                for j in range(NT):
                    dve.scalar_tensor_tensor(dst[0:TP, j, :], dst[0:TP, j, :], rs[:, j:j + 1],
                                             bias, ALU.mult, ALU.add).then_inc(done, 1)

            def logits(name, to):
                n = to.shape[0]
                for q, (c0, cw) in enumerate(HALF):
                    dve.wait_ge(work_full, WORK[name] + q + 1)
                    dve.tensor_copy(to[:, c0:c0 + cw], bank_w(WORK[name] + q)[0:n, 0:cw]
                                    ).then_inc(work_drained, 1)

            xt_n = [0]

            def transposed(name):
                k = WORK[name]
                for j in range(NT):
                    xt_n[0] += 1
                    dve.wait_ge(work_full, k + j + 1)
                    dve.wait_ge(xt_hi, xt_n[0])
                    sl = slice(TP * j, TP * j + TP)
                    minus(XT[:, 1, :, sl], blocks(k + j), XT[:, 0, :, sl], work_drained)

            def gates(n, s):
                settle()
                for j in range(NT):
                    for p in range(n):
                        did(dve.max(v8[:, j, p, :], LGT[:, j, p, :]))
                settle()
                for j in range(NT):
                    for p in range(n):
                        did(dve.max_index(i8[:, j, p, :], v8[:, j, p, :], LGT[:, j, p, :]))
                if n < 5:
                    did(dve.memset(ex[:, :, :], 0.0))
                    settle()
                dve.tensor_tensor(ex[:, :, 0:n], v8[:, :, 0:n, 1], v8[:, :, 0:n, 0],
                                  ALU.subtract).then_inc(ex_in, 1)
                settle()
                did(dve.tensor_copy(idxf[:, :, 0:n, :], i8[:, :, 0:n, 0:2]))
                dve.wait_ge(ex_out, s + 1)
                did(dve.tensor_scalar(p12[:, :, 0:n, 1], ex[:, :, 0:n], 1.0, None, ALU.add))
                settle()
                did(dve.reciprocal(p12[:, :, 0:n, 0], p12[:, :, 0:n, 1]))
                settle()
                did(dve.tensor_tensor(p12[:, :, 0:n, 1], ex[:, :, 0:n], p12[:, :, 0:n, 0], ALU.mult))
                for c, (o_, last) in enumerate(((gat, False), (eqt, True))):
                    shape = [TP, NT, n, 8]
                    it = iota[:, 0:8].unsqueeze(1).unsqueeze(1).to_broadcast(shape)
                    settle()
                    did(dve.tensor_tensor(o_[:, :, 0:n, :], it,
                                          idxf[:, :, 0:n, c:c + 1].to_broadcast(shape), ALU.is_equal))
                    settle()
                    did(dve.tensor_tensor(o_[:, :, 0:n, :], o_[:, :, 0:n, :],
                                          p12[:, :, 0:n, c:c + 1].to_broadcast(shape), ALU.mult))
                settle()
                did(dve.tensor_tensor(gat[:, :, 0:n, :], gat[:, :, 0:n, :], eqt[:, :, 0:n, :], ALU.add))
                settle()

            dve.nop().then_inc(oh_ready, ET)
            did(dve.memset(ones[:, :].bitcast(F32), 1.0))
            did(dve.memset(ones_h[:, :], 1.0))
            did(dve.memset(epst[:, :], EPS))
            did(dve.memset(tot[:, :, N:NP2], 0))
            did(dve.memset(LGT[:, :, 4, 4:8], NEG))
            dve.wait_ge(iotas, 1)
            did(dve.tensor_scalar(ident[:, :], mk, 0.0, None, ALU.is_equal))
            did(dve.tensor_scalar(tri[:, :], mk[0:TP, 0:TP], 0.0, None, ALU.is_gt))
            settle()
            dve.nop().then_inc(consts_ready, 1)
            for j in range(NT):
                dve.wait_ge(x_in_s[j], 16)
                stat(j, X)
            norm("x0", X, U, NT)
            transposed("T0")
            dve.wait_ge(iotas, 8)
            dve.wait_ge(ids_in_s, 16)
            did(dve.tensor_copy(es, ids[:, 0, :]))
            did(dve.tensor_copy(ek, ids[:, 1, :]))
            did(dve.tensor_copy(etype, ids[:, 2, :]))
            dve.wait_ge(small_in, 80)
            did(dve.tensor_copy(ntf[:, :], nti[:, :]))
            did(dve.tensor_copy(gw[:, 0, :, :], gw_raw))
            settle()
            minus(gw[:, 1, :, :], gw_raw, gw[:, 0, :, :])
            for t in range(NR):
                did(dve.tensor_scalar(mask[:, t, :], ntf[:, :], float(t), None, ALU.is_equal))
            settle()
            dve.wait_ge(rows_in_s[0], 96)
            for j in range(NT):
                did(dve.tensor_scalar(HB[0:TP, j, :], rows[:, 3, :], mask[:, 0, j:j + 1], None, ALU.mult))
            for t in range(1, NR):
                settle()
                for j in range(NT):
                    did(dve.scalar_tensor_tensor(HB[0:TP, j, :], rows[:, 3 + t, :], mask[:, t, j:j + 1],
                                                 HB[0:TP, j, :], ALU.mult, ALU.add))

            def y_low(n):
                dve.wait_ge(y_hi, n + 1)
                minus(Y[:, 1, n, :], ytmp[n % 3], Y[:, 0, n, :], y_lo)

            for n in range(NR * NT):
                k = WORK["Y"] + n
                dve.wait_ge(work_full, k + 1)
                if n >= 3:
                    dve.wait_ge(y_lo, n - 2)
                dve.tensor_tensor(ytmp[n % 3], bank_w(k)[0:TP, :], rows[:, n // NT, :],
                                  ALU.add).then_inc(work_drained, 1)
                if n >= 1:
                    y_low(n - 1)
                if n < NS:
                    lo_ = TP * (n // 2) + SUB[n % 2][0]
                    settle()
                    did(dve.tensor_scalar(above[n % 2], ek, lo_ - 0.5, None, ALU.is_gt))
                    settle()
                    did(dve.scalar_tensor_tensor(in_half[:, n, :], ek, lo_ + SUB[n % 2][1] - 0.5,
                                                 above[n % 2], ALU.is_lt, ALU.mult))
            y_low(NR * NT - 1)
            settle()
            dve.nop().then_inc(flags_ready, 1)
            did(dve.scalar_tensor_tensor(ek, etype, float(N), ek, ALU.mult, ALU.add))
            settle()
            did(dve.tensor_scalar(nek, ek, -1.0, None, ALU.mult))
            for n, (c0, c1) in enumerate(FLAGS):
                dve.wait_ge(work_full, WORK["FLAG"] + n + 1)
                dve.tensor_reduce(present[:, c0:c1, :],
                                  bank_w(WORK["FLAG"] + n)[0:1, 0:(c1 - c0) * ET].rearrange("p (c n u) -> p c n u",
                                                                             c=c1 - c0, u=UNR),
                                  AX.X, ALU.add).then_inc(work_drained, 1)
            dve.wait_ge(work_drained, WORK["FLAG"] + len(FLAGS))
            steps_of = stepno.unsqueeze(1).to_broadcast([1, NS, EG])
            did(dve.tensor_scalar(marked[:, 1, :, :], steps_of, -1.0, EG + 1.0, ALU.mult, ALU.add))
            did(dve.scalar_tensor_tensor(marked[:, 0, :, :], present[:, :, :], 0.5, steps_of, ALU.is_gt, ALU.mult))
            settle()
            did(dve.scalar_tensor_tensor(marked[:, 1, :, :], present[:, :, :], 0.5, marked[:, 1, :, :],
                                         ALU.is_gt, ALU.mult))
            settle()
            did(dve.tensor_reduce(spanf[:, 0:2, :], marked, AX.X, ALU.max))
            settle()
            did(dve.tensor_scalar(spanf[:, 1, :], spanf[:, 1, :], 1.0, -1.0, ALU.max, ALU.mult))
            settle()
            did(dve.tensor_scalar(spanf[:, 1, :], spanf[:, 1, :], float(EG), None, ALU.add))
            settle()
            did(dve.scalar_tensor_tensor(spanf[:, 2, :], spanf[:, 1, :], 1.0, spanf[:, 0, :],
                                         ALU.add, ALU.max))
            settle()
            did(dve.tensor_tensor(spanf[:, 0, :], spanf[:, 2, :], spanf[:, 1, :], ALU.subtract))
            settle()
            did(dve.tensor_tensor_scan(spanf[:, 3, :], ones[0:1, 0:NS].bitcast(F32), spanf[:, 0, :], 0.0,
                                       ALU.mult, ALU.add))
            settle()
            did(dve.tensor_tensor(spanf[:, 3, :], spanf[:, 3, :], spanf[:, 2, :], ALU.subtract))
            settle()
            did(dve.tensor_scalar(spanf[:, 3, :], spanf[:, 3, :], float(UNR), float(ET),
                                  ALU.mult, ALU.add))
            settle()
            dve.tensor_copy(spans[:, :, :], spanf[:, 1:4, :]).then_inc(spans_ready, 1)
            for n in range(NR * NT):
                t, j = divmod(n, NT)
                k = WORK["SELF"] + n
                dve.wait_ge(work_full, k + 1)
                if t >= 1:
                    dve.wait_ge(work_drained, k - NT + 1)
                dve.scalar_tensor_tensor(HB[0:TP, j, :], bank_w(k)[0:TP, :], mask[:, t, j:j + 1],
                                         HB[0:TP, j, :], ALU.mult, ALU.add).then_inc(work_drained, 1)
            dve.memset(zero, 0.0).then_inc(zeros_ready, 1)
            dve.wait_ge(spans_ready, 1)

            def residual(c):
                k = WORK["AGG"] + c
                dve.wait_ge(work_full, k + 1)
                dve.tensor_tensor(HB[0:TP, c, :], bank_w(k)[0:TP, :], HB[0:TP, c, :],
                                  ALU.add).then_inc(work_drained, 1)
                dve.wait_ge(work_drained, k + 1)
                did(dve.scalar_tensor_tensor(X[:, c, :], HB[0:TP, c, :], 0.0, X[:, c, :],
                                             ALU.max, ALU.add))

            for c in range(NT):
                for n in (2 * c, 2 * c + 1):
                    first = dve.value_load(spans[0:1, 0, n:n + 1], min_val=0, max_val=EG - 1)
                    end = dve.value_load(spans[0:1, 1, n:n + 1], min_val=1, max_val=EG)
                    before = dve.value_load(spans[0:1, 2, n:n + 1], min_val=UNR, max_val=NS * ET)
                    d0, dw = SUB[n % 2]
                    d0 += TP * c
                    with dve.Fori(first, end) as it:
                        for u in range(UNR):
                            dve.wait_ge(oh_used, before + it * UNR + (u + 1))
                            source = dve.tensor_scalar(ohs[:, u, 0:NP2], iok[:, 0:NP2],
                                                       es[:, bass.ds(it * UNR + u, 1)], None, ALU.is_equal)
                            if u % 2:
                                source.then_inc(oh_ready, 1)
                                continue
                            dve.tensor_scalar(
                                ohk[:, u, 0:NR * dw].rearrange("p (r n) -> p r n", r=NR),
                                iokr[:, :, d0:d0 + dw], ek[:, bass.ds(it * UNR + u, 1)], None,
                                ALU.is_equal).then_inc(oh_ready, 1)
                if c >= 2:
                    residual(c - 2)
                for j in range(NT):
                    dve.wait_ge(acc_full, NT * c + j + 1)
                    dve.wait_ge(ac_hi, NT * c + j + 1)
                    minus(AC[c % 2][:, 1, j, :], ps[j][0:TP, 0:CW], AC[c % 2][:, 0, j, :])
                    with nc.allow_low_precision(reason="counts up to 20000 are exact in uint16"):
                        dve.tensor_reduce(tot[:, j, TP * c:TP * c + TP],
                                          ps[j][0:TP, 0:CW].rearrange("p (r n) -> p n r", r=NR), AX.X,
                                          ALU.add).then_inc(acc_drained, 1)
            residual(NT - 2)
            settle()
            for j in range(NT - 1):
                stat(j, X)
            residual(NT - 1)
            did(dve.memset(XT[:, :, :, N:NP2].bitcast(F32), 0.0))
            settle()
            dve.nop().then_inc(rows_free, 1)
            norm_and_stat("x1", X, U, NT - 1)
            transposed("T1")
            dve.wait_ge(rows_in_s[1], 96)
            norm_rows("z", U, Z, rows[:, 0, :], rows[:, 1, :], NT, z_done)
            logits("LG", logT[1])
            transposed("T2")
            k = WORK["LGB"]
            dve.wait_ge(work_full, k + 1)
            dve.tensor_copy(LGT[:, :, 4, 0:G0],
                            bank_w(k)[0:TP, 0:NT * G0].rearrange("p (a b) -> p a b", a=NT)
                            ).then_inc(work_drained, 1)
            dve.wait_ge(work_drained, k + 1)
            for c in range(16):
                did(dve.tensor_scalar(SEL[:, c, :], mk64[:, :], -2.0 * c, None, ALU.is_equal))
            did(dve.memset(IW[:, :, N:NP2].bitcast(F32), 0.0))
            did(dve.tensor_scalar(kg[:, 1, :], kg[:, 0, :], 7.5, None, ALU.is_lt))
            settle()
            did(dve.scalar_tensor_tensor(kg[:, 1, :], kg[:, 0, :], -0.5, kg[:, 1, :],
                                         ALU.is_gt, ALU.mult))
            for j in range(NT):
                did(dve.tensor_tensor(X[:, j, :], X[:, j, :], U[0:TP, j, :], ALU.add))
            settle()
            dve.nop().then_inc(u_free, 1)
            logits("LI", logT[0])
            k = WORK["LIB"]
            dve.wait_ge(work_full, k + 1)
            dve.tensor_copy(LGT[:, :, 0:4, :],
                            bank_w(k)[0:TP, 0:160].rearrange("p (a b n) -> p a b n", a=NT, b=4)
                            ).then_inc(work_drained, 1)
            dve.wait_ge(work_drained, k + 1)
            gates(5, 0)
            dve.nop().then_inc(gates_ready, 1)
            for n in range(4):
                k = WORK["GT"] + n
                t0, t1 = PARTS[n % 2]
                sl = slice(TP * t0, TP * t1)
                dve.wait_ge(work_full, k + 1)
                if n < 2:
                    dve.wait_ge(gt_hi, n + 1)
                    minus(IW[:, 1, sl], bank_w(k)[0:32, 0:TP * (t1 - t0)], IW[:, 0, sl], work_drained)
                else:
                    dve.tensor_copy(gT[0:G0, sl], bank_w(k)[0:G0, 0:TP * (t1 - t0)]).then_inc(work_drained, 1)

            def second_bias(g):
                dve.wait_ge(b2_hi, g + 1)
                did(dve.scalar_tensor_tensor(B2[:, 1, g, :], b2f, kg[:, 1, g:g + 1],
                                             B2[:, 0, g, :].bitcast(F32), ALU.mult, ALU.subtract))

            def hidden(g):
                for s in range(8):
                    cc, (c0, w) = s // 2, HALF[s % 2]
                    k = WORK["FF"] + 16 * g + 2 * s
                    q = 8 * g + s
                    dve.wait_ge(work_full, k + 2)
                    dve.wait_ge(relu_done, q + 1)
                    if q >= 2:
                        dve.wait_ge(ht_lo, q - 1)
                    dve.tensor_tensor(f2[q % 2][:, 0:w], f1[q % 2][:, 0:w], bank_w(k + 1)[:, 0:w],
                                      ALU.mult).then_inc(f2_done, 1)
                    dve.wait_ge(f2_done, q + 1)
                    dve.sem_inc(work_drained, 2)
                    if g == 1 and s < G0:
                        second_bias(s)
                    if g >= 2:
                        if 2 <= s < 2 + NT:
                            collect(g - 2, s - 2)
                    dve.wait_ge(ht_hi, q + 1)
                    minus(HT[:, g % 2, 1, cc, c0:c0 + w], f2[q % 2][:, 0:w],
                          HT[:, g % 2, 0, cc, c0:c0 + w], ht_lo)

            def group(g):
                for j in range(NT):
                    n = ACC["MOE"] + NT * g + j
                    dve.wait_ge(acc_full, n + 1)
                    dve.tensor_tensor(HB[0:TP, j, :], ps[j][0:TP, :], Z[0:TP, j, :],
                                      ALU.add).then_inc(acc_drained, 1)
                    dve.wait_ge(acc_drained, n + 1)
                    stat(j, HB)
                moments(f"g{g}")
                if g < 2:
                    coefficients()

            def collect(g, j):
                dve.wait_ge(weighed, NT * g + j + 1)
                did(dve.scalar_tensor_tensor(X[:, j, :], HB[0:TP, j, :], gat[:, j, 4, g:g + 1], X[:, j, :],
                                             ALU.mult, ALU.add))

            hidden(0)
            hidden(1)
            settle()
            group(0)
            hidden(2)
            settle()
            group(1)
            hidden(3)
            settle()
            for j in range(NT):
                k = WORK["GB"] + j
                dve.wait_ge(work_full, k + 1)
                dve.tensor_tensor(X[:, j, :], bank_w(k)[0:TP, :], X[:, j, :], ALU.add).then_inc(work_drained, 1)
            dve.wait_ge(work_drained, WORK["GB"] + NT)
            for g in (2, 3):
                group(g)
                did(dve.tensor_tensor(ga[:, :], gat[:, :, 4, g], rs[:, :], ALU.mult))
                for j in range(NT):
                    did(dve.scalar_tensor_tensor(HB[0:TP, j, :], HB[0:TP, j, :], mv[:, j, 0:1],
                                                 rows[:, 2 + g, :], ALU.subtract, ALU.mult))
                settle()
                for j in range(NT):
                    did(dve.scalar_tensor_tensor(X[:, j, :], HB[0:TP, j, :], ga[:, j:j + 1],
                                                 X[:, j, :], ALU.mult, ALU.add))
                settle()
            dve.nop().then_inc(rows_free, 1)
            norm("x2", X, U)
            dve.nop().then_inc(xs_src, NT)
            transposed("T3")
            for j in range(NT):
                dve.wait_ge(xs_hi, j + 1)
                minus(XS[:, 1, j, :], U[0:TP, j, :], XS[:, 0, j, :], xs_lo)
                dve.wait_ge(at_hi, j + 1)
                minus(AT[:, 1, j, :], tot[:, j, :], AT[:, 0, j, :], at_lo)
            for q, (c0, cw) in enumerate(HALF):
                k = WORK["DEG"] + q
                dve.wait_ge(work_full, k + 1)
                dve.tensor_scalar(rdeg[:, c0:c0 + cw], bank_w(k)[:, 0:cw],
                                  1.0, None, ALU.max).then_inc(work_drained, 1)
            dve.wait_ge(work_drained, WORK["DEG"] + 2)
            did(dve.reciprocal(rdeg, rdeg))
            settle()

            def mean_low(s, q):
                dk, (c0, w) = q // 2, HALF[q % 2]
                dve.wait_ge(ag_hi, 2 * KD * s + q + 1)
                minus(AG[:, 1, dk, c0:c0 + w], agt[q % 2][:, 0:w], AG[:, 0, dk, c0:c0 + w], ag_lo)

            def conv(s):
                for q in range(2 * KD):
                    k = WORK[("AG1", "AG2")[s]] + q
                    c0, w = HALF[q % 2]
                    dve.wait_ge(work_full, k + 1)
                    if q >= 2:
                        dve.wait_ge(ag_lo, 2 * KD * s + q - 1)
                    dve.tensor_tensor(agt[q % 2][:, 0:w], bank_w(k)[:, 0:w], rdeg[:, c0:c0 + w],
                                      ALU.mult).then_inc(work_drained, 1)
                    if q >= 1:
                        mean_low(s, q - 1)
                mean_low(s, 2 * KD - 1)
                if s == 0:
                    dve.wait_ge(rows_in_s[2], 96)
                for j in range(NT):
                    n = ACC[("C1", "C2")[s]] + j
                    dve.wait_ge(acc_full, n + 1)
                    dve.tensor_tensor(Z[0:TP, j, :], ps[j][0:TP, :], rows[:, 3 * s, :],
                                      ALU.add).then_inc(acc_drained, 1)
                    dve.wait_ge(acc_drained, n + 1)
                    stat(j, Z)

            conv(0)
            norm_rows("c1", Z, Z, rows[:, 1, :], rows[:, 2, :], NT, c1_done)
            dve.nop().then_inc(rows_free, 1)
            for j in range(NT):
                dve.wait_ge(c1_done, j + 1)
                dve.scalar_tensor_tensor(U[0:TP, j, :], Z[0:TP, j, :], 0.0, U[0:TP, j, :],
                                         ALU.max, ALU.add).then_inc(xs_src, 1)
            dve.wait_ge(xs_src, 2 * NT)
            transposed("T4")
            for j in range(NT):
                dve.wait_ge(xs_hi, NT + j + 1)
                minus(XS[:, 1, j, :], U[0:TP, j, :], XS[:, 0, j, :], xs_lo)
            for add in (U[0:TP], None):
                for j in range(NT):
                    did(dve.tensor_tensor(X[:, j, :], X[:, j, :],
                                          rows[:, 5, :] if add is None else add[:, j, :], ALU.add))
                settle()
            conv(1)
            moments("c2")
            for j in range(NT):
                did(dve.scalar_tensor_tensor(Z[0:TP, j, :], Z[0:TP, j, :], mv[:, j, 0:1],
                                             rows[:, 4, :], ALU.subtract, ALU.mult))
            settle()
            for j in range(NT):
                did(dve.scalar_tensor_tensor(X[:, j, :], Z[0:TP, j, :], rs[:, j:j + 1],
                                             X[:, j, :], ALU.mult, ALU.add))
            settle()
            norm_and_stat("x3", X, U)
            dve.wait_ge(rows_in_s[3], 32)
            norm_rows("w0", U, Z, rows[:, 0, :], rows[:, 1, :], NT, xs_src)
            dve.nop().then_inc(rows_free, 1)
            transposed("T5")
            for j in range(NT):
                did(dve.tensor_tensor(X[:, j, :], X[:, j, :], U[0:TP, j, :], ALU.add))
            logits("LR", logT[0][0:NX])
            settle()
            dve.nop().then_inc(u_free, 1)
            k = WORK["LRB"]
            dve.wait_ge(work_full, k + 1)
            dve.tensor_tensor(LGT[:, :, 0, :], bank_w(k)[0:TP, 0:40].rearrange("p (a b) -> p a b", a=NT),
                              rbt[:, :].unsqueeze(1).to_broadcast([TP, NT, NX]), ALU.add
                              ).then_inc(work_drained, 1)
            dve.wait_ge(work_drained, k + 1)
            gates(1, 1)
            shape = [TP, NT, NX]
            it = iota[:, 0:8].unsqueeze(1).to_broadcast(shape)
            did(dve.tensor_tensor(eq1, it, idxf[:, :, 0, 0:1].to_broadcast(shape), ALU.is_equal))
            did(dve.tensor_tensor(gsb, it, idxf[:, :, 0, 1:2].to_broadcast(shape), ALU.is_equal))
            settle()
            did(dve.tensor_tensor(sel16, eq1, gsb, ALU.add))
            settle()
            dve.nop().then_inc(sel_ready, 1)
            for j in range(2):
                dve.wait_ge(xs_hi, 2 * NT + j + 1)
                minus(XS[:, 1, j, :], Z[0:TP, j, :], XS[:, 0, j, :], xs_lo)
            k = WORK["POS"]
            dve.wait_ge(work_full, k + 1)
            b = bank_w(k)
            did(dve.tensor_scalar(cum[:, 1, :], b[:, 64:72], 0.5, None, ALU.is_gt))
            for lim in (SLOTS + 0.5, 2 * SLOTS + 0.5):
                settle()
                did(dve.scalar_tensor_tensor(cum[:, 1, :], b[:, 64:72], lim, cum[:, 1, :],
                                             ALU.is_gt, ALU.add))
            settle()
            did(dve.tensor_tensor_scan(cum[:, 2, :], ones[:, 0:NX].bitcast(F32), cum[:, 1, :], 0.0, ALU.mult, ALU.add))
            settle()
            did(dve.tensor_tensor(cbase, cum[:, 2, :], cum[:, 1, :], ALU.subtract))
            settle()
            did(dve.tensor_scalar(cslot, cbase, float(SLOTS), None, ALU.mult))
            settle()
            did(dve.tensor_copy(ntok, b[0:1, 64:72]))
            dve.tensor_tensor(gsv, b[0:TP, 0:40].rearrange("p (a b) -> p a b", a=NT),
                              cslot[0:TP, :].unsqueeze(1).to_broadcast(shape), ALU.add
                              ).then_inc(work_drained, 1)
            dve.wait_ge(work_drained, k + 1)
            for n in range(2):
                k = WORK["GX"] + n
                t0, t1 = PARTS[n]
                dve.wait_ge(work_full, k + 1)
                dve.tensor_copy(gT[:, TP * t0:TP * t1], bank_w(k)[0:NX, 0:TP * (t1 - t0)]
                                ).then_inc(work_drained, 1)
            did(dve.tensor_tensor(eq1, eq1, gsv, ALU.mult))
            did(dve.tensor_tensor(gsb, gsb, gsv, ALU.mult))
            settle()
            did(dve.tensor_reduce(gsl[:, :, 0], eq1, AX.X, ALU.add))
            did(dve.tensor_reduce(gsl[:, :, 1], gsb, AX.X, ALU.add))
            did(dve.tensor_copy(gsl[:, :, 2:4], p12[:, :, 0, :]))
            settle()
            did(dve.tensor_copy(gcur[:, :, :], gsl[:, :, 0:2]))
            settle()
            dve.nop().then_inc(gsl_ready, 1)
            for j in range(2, NT):
                dve.wait_ge(xs_hi, 2 * NT + j + 1)
                minus(XS[:, 1, j, :], Z[0:TP, j, :], XS[:, 0, j, :], xs_lo)
            si = [1, NI, NX]
            did(dve.tensor_tensor(ele[:, :, :], cum[0:1, 2, :].unsqueeze(1).to_broadcast(si),
                                  i12[:, :].unsqueeze(2).to_broadcast(si), ALU.is_le))
            settle()
            did(dve.tensor_reduce(itf[:, :], ele[:, :, :], AX.X, ALU.add))
            did(dve.scalar_tensor_tensor(ends, cbase[0:1, :], float(SLOTS), ntok,
                                         ALU.mult, ALU.add))
            did(dve.tensor_scalar(lims, i12[:, :], float(SLOTS), 128.5, ALU.mult, ALU.add))
            did(dve.tensor_tensor(ele2, cbase[0:1, :].unsqueeze(1).to_broadcast(si),
                                  i12[:, :].unsqueeze(2).to_broadcast(si), ALU.is_le))
            settle()
            did(dve.tensor_tensor(ele2, ele2, ele, ALU.subtract))
            settle()
            did(dve.tensor_tensor(ele2, ele2, ends.unsqueeze(1).to_broadcast(si), ALU.mult))
            settle()
            did(dve.tensor_reduce(ends2, ele2, AX.X, ALU.add))
            settle()
            did(dve.tensor_tensor(ends2, ends2, lims, ALU.is_gt))
            settle()
            did(dve.tensor_copy(items[:, NI + 1:], ends2))
            settle()
            did(dve.tensor_scalar(itf[:, :], itf[:, :], float(NX - 1), None, ALU.min))
            settle()
            did(dve.tensor_copy(items[:, NI:NI + 1], cum[0:1, 2, NX - 1:NX]))
            settle()
            dve.tensor_copy(items[:, 0:NI], itf[:, :]).then_inc(items_ready, 1)
            dve.wait_ge(xs_lo, 3 * NT)
            did(dve.tensor_copy(pick, ident[0:4, 0:4].unsqueeze(2).to_broadcast([4, 4, 128])))
            settle()
            for n in range(2):
                k = WORK["DGT"] + n
                t0, t1 = PARTS[n]
                dve.wait_ge(work_full, k + 1)
                dve.tensor_copy(g4T[:, TP * t0:TP * t1], bank_w(k)[0:4, 0:TP * (t1 - t0)]
                                ).then_inc(work_drained, 1)

            loop = sem("item_step")

            def s_first(j):
                return dve.tensor_scalar(s1[:, j, :], siota, gcur[:, j, 0:1], None, ALU.is_equal)

            def s_second(j):
                return dve.scalar_tensor_tensor(S[:, j, :], siota, gcur[:, j, 1:2], s1[:, j, :],
                                                ALU.is_equal, ALU.add)

            dve.wait_ge(iotas, 9)
            for j in range(NT):
                did(s_first(j))
            settle()
            for j in range(NT):
                ins = s_second(j)
            ins.then_inc(s_ready, 1)
            for j in range(NT):
                n = ACC["FB"] + j
                dve.wait_ge(acc_full, n + 1)
                dve.tensor_tensor(X[:, j, :], ps[j][0:TP, :], X[:, j, :], ALU.add).then_inc(acc_drained, 1)
            dve.wait_ge(acc_drained, ACC["FB"] + NT)

            def gathered(done):
                for dk in range(KD):
                    dve.wait_ge(xc_full, done + (dk + 1))
                    dve.wait_ge(xc_hi, done + (dk + 1))
                    minus(XC[:, 1, dk, :], ps[6 + dk % 2][:, 0:SLOTS], XC[:, 0, dk, :], xc_lo)

            def scattered(i):
                for j in range(NT):
                    dve.wait_ge(sc_full, i * NT + (j + 1))
                    dve.tensor_tensor(X[:, j, :], ps[6 + j % 2][0:TP, :], X[:, j, :],
                                      ALU.add).then_inc(sc_added, 1)

            gathered(0)
            n = ACC["DG"]
            for q, (c0, cw) in enumerate(2 * SPAN):
                for v in (2 * (q // 2), 2 * (q // 2) + 1):
                    dve.wait_ge(acc_full, n + 1)
                    dve.tensor_copy(R4[:, v, c0:c0 + cw], ps[n % NT][:, 0:cw]).then_inc(acc_drained, 1)
                    n += 1
            dve.wait_ge(acc_drained, ACC["END"])
            did(dve.memset(ps[1][:, :], 0.0))
            settle()
            dve.wait_ge(st_zero, 1)
            dve.nop().then_inc(st_ready, 1)
            dve.wait_ge(weight_lo, STATIC)
            dve.nop().then_inc(weight_lo_v, 1)

            def weight_low(i, k):
                dve.wait_ge(weight_hi, i * PER_ITEM + (STATIC + k + 1))
                minus(split_slot(k, 1), raw[:, k % RING, :], split_slot(k, 0), weight_lo_v)

            n_items = dve.value_load(items[0:1, NI:NI + 1], min_val=1, max_val=NI)
            with dve.Fori(0, n_items) as i:

                def loop_did(ins):
                    ins.then_inc(loop, 1)

                def hidden_low(q):
                    for f in range(2):
                        n = 2 * q + f
                        dve.wait_ge(hd_hi, i * 16 + (n + 1))
                        minus(HD[:, q % 2, 1, f, :], hid[:, q % 2, f, :], HD[:, q % 2, 0, f, :], hd_lo)

                def at(n):
                    dve.wait_ge(loop, i * CHAIN + n)

                weight_low(i, 3)
                hidden_low(0)
                scattered(i)
                hidden_low(1)
                hidden_low(2)
                weight_low(i, 7)
                n = 0
                for h in range(2):
                    loop_did(dve.tensor_scalar(stmp, R4[:, 0, :], sid[:, h:h + 1], None, ALU.is_equal))
                    n += 1
                    at(n)
                    loop_did(dve.scalar_tensor_tensor(ST[:, h, :], R4[:, 1, :], sid[:, h:h + 1], stmp,
                                                      ALU.is_equal, ALU.add))
                    n += 1
                    for c in range(2):
                        loop_did(dve.scalar_tensor_tensor(junk, R4[:, c, :], sid[:, h:h + 1],
                                                          R4[:, 2 + c, :], ALU.is_equal, ALU.mult,
                                                          accum_out=gs[:, h, c:c + 1]))
                        n += 1
                        at(n)
                    hidden_low(3 + h)
                    if h == 1:
                        weight_low(i, 11)
                dve.tensor_tensor(gsum[:, :], gs[:, :, 0], gs[:, :, 1], ALU.add).then_inc(st_ready, 1)
                loop_did(dve.tensor_scalar(sid[:, :], sid[:, :], float(SLOTS), None, ALU.add))
                n += 1
                loop_did(dve.tensor_scalar(gcur[:, :, :], gcur[:, :, :], -float(SLOTS), None, ALU.add))
                n += 1
                at(n)
                for j in range(NT):
                    loop_did(s_first(j))
                    n += 1
                hidden_low(5)
                at(n)
                for j in range(NT):
                    ins = s_second(j)
                ins.then_inc(s_ready, 1)
                hidden_low(6)
                weight_low(i, 15)
                hidden_low(7)
                gathered(i * KD + KD)
                dve.wait_ge(st_ready, i + 2)
                for h in range(2):
                    dve.wait_ge(o_full, i * 2 + (h + 1))
                    dve.tensor_scalar(ysf[:, h, :], ps[h][:, :], gsum[:, h:h + 1], None,
                                      ALU.mult).then_inc(ys_done, 1)
                for h in range(2):
                    dve.wait_ge(ys_hi, i * 2 + (h + 1))
                    minus(YS[:, 1, h, :], ysf[:, h, :], YS[:, 0, h, :], ys_lo)
                assert n == CHAIN
            scattered(n_items)


CHAIN = 15
ORDER = [("h", 0)] + [u for q in range(1, 8) for u in (("h", q), ("o", q - 1))] + [("o", 7)]


def kernel(**inputs):
    import numpy as _np
    import concourse.bacc as _bacc
    from concourse import mybir as _mybir
    from concourse.bass_utils import run_bass_kernel_spmd as _run

    a = {k: _np.asarray(v) for k, v in inputs.items()}

    def unit(m):
        return m.reshape(2, 2, 128, 512).transpose(0, 2, 1, 3).reshape(2, 128, HU)

    def w1_0(g):
        return unit(a["L0_ffn_W1"][g].transpose(1, 0, 2).reshape(D, D))

    def w2_0(g):
        return unit(a["L0_ffn_W2"][g].reshape(D, D))

    units = [unit(a["L0_gnn_W_rel"][r]) for r in range(3)] + [unit(a["L0_gnn_W_self"][t]) for t in range(3)]
    units += [w1_0(0), w1_0(1), w2_0(0), w1_0(2), w2_0(1), w1_0(3), w2_0(2), w2_0(3)]
    units += [unit(a[n].T) for n in ("L1_gnn_W1r", "L1_gnn_W1l", "L1_gnn_W2r", "L1_gnn_W2l")]
    w1 = a["L1_ffn_W1"].reshape(NX, KD, 128, 8, 256).transpose(0, 3, 2, 1, 4).reshape(NX, 8, 128, HU)
    w2 = a["L1_ffn_W2"].reshape(NX, 8, 2, 128, D).transpose(0, 1, 3, 2, 4).reshape(NX, 8, 128, HU)
    wmoe = _np.stack([(w1 if kind == "h" else w2)[:, q] for kind, q in ORDER], 1)
    gate = _np.concatenate([a["L0_ffn_wg_group"], a["L0_ffn_wg_inner"].transpose(1, 0, 2).reshape(D, 32),
                            a["L1_ffn_w_r"].T], 1).reshape(KD, 128, 44).transpose(1, 0, 2)
    rows = [a["L0_gnn_b_rel"], a["L0_gnn_b_self"], a["L0_ffn_ln_g"][None], a["L0_ffn_ln_b"][None],
            a["L0_ffn_gln_g"]]
    rows += [a[n][None] for n in ("L1_gnn_b1l", "L1_gnn_ln1_w", "L1_gnn_ln1_b", "L1_gnn_b2l",
                                  "L1_gnn_ln2_w", "L1_gnn_ln2_b", "L1_ffn_ln_g", "L1_ffn_ln_b")]
    ids = _np.stack([a["src"], a["dst"], a["edge_type_3"]]).reshape(3, ET, TP).transpose(2, 0, 1)
    arrays = {
        "x": a["x"].reshape(NT, TP, D).transpose(1, 0, 2), "ids": ids,
        "ntype": a["node_type_3"].reshape(NT, TP).T, "rows": _np.concatenate(rows),
        "wstat": _np.concatenate(units), "wmoe": wmoe, "gate": gate,
        "b1_0": a["L0_ffn_b1"].reshape(16, 128).T, "b2_0": a["L0_ffn_b2"].reshape(32, D),
        "glnb": a["L0_ffn_gln_b"], "rb": a["L1_ffn_b_r"][None],
        "b1_1": a["L1_ffn_b1"].reshape(NX * 16, 128).T, "b2_1": a["L1_ffn_b2"],
    }
    arrays = {f"in_{k}": _np.ascontiguousarray(v) for k, v in arrays.items()}
    nc = _bacc.Bacc("TRN2", target_bir_lowering=False, num_devices=1)
    args = [nc.dram_tensor(k, v.shape, _mybir.dt.from_np(v.dtype), kind="ExternalInput").ap()
            for k, v in arrays.items()]
    args.append(nc.dram_tensor("out_x", (TP, NT, D), _mybir.dt.float32, kind="ExternalOutput").ap())
    gnn_moe(nc, *args)
    r = _run(nc, [arrays], core_ids=[0])
    return _np.ascontiguousarray(r.results[0]["out_x"].transpose(1, 0, 2).reshape(N, D))
```
